# Optimizing a Trainium2 kernel written in Bass

```python
import numpy as np
import jax
import jax.numpy as jnp

def _softmax(x, axis=-1):
    return jax.nn.softmax(x, axis=axis)

def _gelu(x):
    return jax.nn.gelu(x, approximate=True)

def _silu(x):
    return jax.nn.silu(x)

def _sigmoid(x):
    return jax.nn.sigmoid(x)

def _layernorm(x, axis=-1, eps=1e-05):
    m = jnp.mean(x, axis=axis, keepdims=True)
    v = jnp.var(x, axis=axis, keepdims=True)
    return (x - m) / jnp.sqrt(v + eps)

def _scatter_add(tgt, idx, src, axis=0):
    return tgt.at[idx].add(src)

def _segment_sum(src, seg, n):
    return jax.ops.segment_sum(src, seg, n)
kernel_name = 'mk_gnn_ffn_d2_gnn_r32_d346e9'

def setup_inputs(seed: int=0):
    np.random.seed(seed)
    _w = jnp.asarray

    def _rec_inputs():
        import jax
        import jax.numpy as jnp
        _gk = jax.random.key(seed)
        x = -0.0002117 + 1 * jax.random.normal(jax.random.fold_in(_gk, 1), (3125, 256), jnp.float32)
        src = jax.random.randint(jax.random.fold_in(_gk, 2), (50000,), 0, 3125, jnp.int32)
        dst = jax.random.randint(jax.random.fold_in(_gk, 3), (50000,), 0, 3125, jnp.int32)
        _o = jnp.argsort(dst, stable=True)
        src = src[_o]
        dst = dst[_o]
        edge_weight = 0.000714719 + 1.00021 * jax.random.normal(jax.random.fold_in(_gk, 12), (50000,), jnp.float32)
        return (x, src, dst, edge_weight)
    x, src, dst, edge_weight = _rec_inputs()

    def _L0_gnn_setup():
        import jax, jax.numpy as jnp
        import numpy as np
        N = 3125
        E = 100000
        D = 256
        LN_EPS = 1e-05

        def _safe(x):
            return jnp.nan_to_num(x, nan=0.0, posinf=0.0, neginf=0.0)

        def _layernorm(h, g, b):
            mu = jnp.mean(h, axis=-1, keepdims=True)
            var = jnp.mean(jnp.square(h - mu), axis=-1, keepdims=True)
            return (h - mu) * jax.lax.rsqrt(var + LN_EPS) * g + b

        def _gcn_conv(h, row, col, ew, dis, W, b):
            xw = h @ W
            norm = dis[row] * ew * dis[col]
            msg = norm[:, None] * xw[row]
            agg = jax.ops.segment_sum(msg, col, num_segments=N)
            agg = agg + (dis * dis)[:, None] * xw
            return agg + b
        key = jax.random.key(seed)
        ks = jax.random.split(key, 8)
        x = jax.random.normal(ks[0], (N, D), dtype=jnp.float32)
        edge_index = jax.random.randint(ks[1], (2, E), 0, N, dtype=jnp.int64)
        edge_weight = jax.random.normal(ks[2], (E,), dtype=jnp.float32)
        s = 1.0 / np.sqrt(D)
        W1 = jax.random.uniform(ks[3], (D, D), jnp.float32, -s, s)
        W2 = jax.random.uniform(ks[4], (D, D), jnp.float32, -s, s)
        b1 = jax.random.uniform(ks[5], (D,), jnp.float32, -s, s)
        b2 = jax.random.uniform(ks[6], (D,), jnp.float32, -s, s)
        ln_g1 = jnp.ones((D,), jnp.float32)
        ln_b1 = jnp.zeros((D,), jnp.float32)
        ln_g2 = jnp.ones((D,), jnp.float32)
        ln_b2 = jnp.zeros((D,), jnp.float32)
        return dict(x=x, edge_index=edge_index, edge_weight=edge_weight, W1=W1, b1=b1, ln_g1=ln_g1, ln_b1=ln_b1, W2=W2, b2=b2, ln_g2=ln_g2, ln_b2=ln_b2)
    _L0_gnn_all = _L0_gnn_setup()
    _L0_gnn_in = {k: v for k, v in _L0_gnn_all.items() if k in ('W1', 'b1', 'ln_g1', 'ln_b1', 'W2', 'b2', 'ln_g2', 'ln_b2')}
    del _L0_gnn_all

    def _L0_ffn_setup():
        import jax, jax.numpy as jnp
        import numpy as np
        TOP_K = 2
        LN_EPS = 1e-05
        key = jax.random.key(seed)
        ks = jax.random.split(key, 8)
        B, S, D, E, H = (16, 1024, 256, 8, 1024)
        x = jax.random.normal(ks[0], (B, S, D), dtype=jnp.float32)
        Wr = jax.random.normal(ks[1], (D, E), dtype=jnp.float32) * 0.1
        br = jnp.zeros((E,), dtype=jnp.float32)
        ln_g = jnp.ones((E, D), dtype=jnp.float32)
        ln_b = jnp.zeros((E, D), dtype=jnp.float32)
        W1 = jax.random.normal(ks[2], (E, D, H), dtype=jnp.float32) * (1.0 / np.sqrt(D))
        b1 = jnp.zeros((E, H), dtype=jnp.float32)
        W2 = jax.random.normal(ks[3], (E, H, D), dtype=jnp.float32) * (1.0 / np.sqrt(H))
        b2 = jnp.zeros((E, D), dtype=jnp.float32)
        return {'x': x, 'Wr': Wr, 'br': br, 'ln_g': ln_g, 'ln_b': ln_b, 'W1': W1, 'b1': b1, 'W2': W2, 'b2': b2}
    _L0_ffn_all = _L0_ffn_setup()
    _L0_ffn_in = {k: v for k, v in _L0_ffn_all.items() if k in ('Wr', 'br', 'ln_g', 'ln_b', 'W1', 'b1', 'W2', 'b2')}
    del _L0_ffn_all

    def _L1_gnn_setup():
        import jax, jax.numpy as jnp
        import numpy as np
        N_NODES = 625
        N_EDGES = 10000
        D = 256
        NUM_LAYERS = 5

        def gru_cell(m, h, w_ih, w_hh, b_ih, b_hh):
            gi = m @ w_ih.T + b_ih
            gh = h @ w_hh.T + b_hh
            i_r, i_z, i_n = jnp.split(gi, 3, axis=1)
            h_r, h_z, h_n = jnp.split(gh, 3, axis=1)
            r = jax.nn.sigmoid(i_r + h_r)
            z = jax.nn.sigmoid(i_z + h_z)
            n = jnp.tanh(i_n + r * h_n)
            return (1.0 - z) * n + z * h
        key = jax.random.key(seed)
        ks = jax.random.split(key, 8)
        x = jax.random.normal(ks[0], (N_NODES, D), dtype=jnp.float32)
        src = jax.random.randint(ks[1], (N_EDGES,), 0, N_NODES)
        dst = jax.random.randint(ks[2], (N_EDGES,), 0, N_NODES)
        edge_index = jnp.stack([src, dst]).astype(jnp.int64)
        edge_attr = jax.random.uniform(ks[3], (N_EDGES,), dtype=jnp.float32)
        s = 1.0 / np.sqrt(D)
        weight = jax.random.uniform(ks[4], (NUM_LAYERS, D, D), minval=-s, maxval=s, dtype=jnp.float32)
        w_ih = jax.random.uniform(ks[5], (3 * D, D), minval=-s, maxval=s, dtype=jnp.float32)
        w_hh = jax.random.uniform(ks[6], (3 * D, D), minval=-s, maxval=s, dtype=jnp.float32)
        b = jax.random.uniform(ks[7], (2, 3 * D), minval=-s, maxval=s, dtype=jnp.float32)
        return {'x': x, 'edge_index': edge_index, 'edge_attr': edge_attr, 'weight': weight, 'w_ih': w_ih, 'w_hh': w_hh, 'b_ih': b[0], 'b_hh': b[1]}
    _L1_gnn_all = _L1_gnn_setup()
    _L1_gnn_in = {k: v for k, v in _L1_gnn_all.items() if k in ('weight', 'w_ih', 'w_hh', 'b_ih', 'b_hh')}
    del _L1_gnn_all

    def _L1_ffn_setup():
        import math
        import jax, jax.numpy as jnp
        import numpy as np
        CAPACITY_FACTOR = 1.25
        TOP_K = 2
        LN_EPS = 1e-05

        def _layer_norm(x, gamma, beta):
            mu = jnp.mean(x, axis=-1, keepdims=True)
            var = jnp.var(x, axis=-1, keepdims=True)
            return (x - mu) * jax.lax.rsqrt(var + LN_EPS) * gamma + beta
        key = jax.random.key(seed)
        ks = jax.random.split(key, 4)
        B, S, D, F, E = (8, 128, 256, 512, 8)
        x = jax.random.normal(ks[0], (B, S, D), dtype=jnp.float32)
        Wr = jax.random.normal(ks[1], (D, E), dtype=jnp.float32) / np.sqrt(D)
        br = jnp.zeros((E,), jnp.float32)
        W1 = jax.random.normal(ks[2], (E, D, F), dtype=jnp.float32) / np.sqrt(D)
        b1 = jnp.zeros((E, F), jnp.float32)
        W2 = jax.random.normal(ks[3], (E, F, D), dtype=jnp.float32) / np.sqrt(F)
        b2 = jnp.zeros((E, D), jnp.float32)
        gamma = jnp.ones((D,), jnp.float32)
        beta = jnp.zeros((D,), jnp.float32)
        return {'x': x, 'Wr': Wr, 'br': br, 'W1': W1, 'b1': b1, 'W2': W2, 'b2': b2, 'gamma': gamma, 'beta': beta}
    _L1_ffn_all = _L1_ffn_setup()
    _L1_ffn_in = {k: v for k, v in _L1_ffn_all.items() if k in ('Wr', 'br', 'W1', 'b1', 'W2', 'b2', 'gamma', 'beta')}
    del _L1_ffn_all
    return {'x': x, 'src': src, 'dst': dst, 'edge_weight': edge_weight, 'L0_gnn_W1': _L0_gnn_in['W1'], 'L0_gnn_b1': _L0_gnn_in['b1'], 'L0_gnn_ln_g1': _L0_gnn_in['ln_g1'], 'L0_gnn_ln_b1': _L0_gnn_in['ln_b1'], 'L0_gnn_W2': _L0_gnn_in['W2'], 'L0_gnn_b2': _L0_gnn_in['b2'], 'L0_gnn_ln_g2': _L0_gnn_in['ln_g2'], 'L0_gnn_ln_b2': _L0_gnn_in['ln_b2'], 'L0_ffn_Wr': _L0_ffn_in['Wr'], 'L0_ffn_br': _L0_ffn_in['br'], 'L0_ffn_ln_g': _L0_ffn_in['ln_g'], 'L0_ffn_ln_b': _L0_ffn_in['ln_b'], 'L0_ffn_W1': _L0_ffn_in['W1'], 'L0_ffn_b1': _L0_ffn_in['b1'], 'L0_ffn_W2': _L0_ffn_in['W2'], 'L0_ffn_b2': _L0_ffn_in['b2'], 'L1_gnn_weight': _L1_gnn_in['weight'], 'L1_gnn_w_ih': _L1_gnn_in['w_ih'], 'L1_gnn_w_hh': _L1_gnn_in['w_hh'], 'L1_gnn_b_ih': _L1_gnn_in['b_ih'], 'L1_gnn_b_hh': _L1_gnn_in['b_hh'], 'L1_ffn_Wr': _L1_ffn_in['Wr'], 'L1_ffn_br': _L1_ffn_in['br'], 'L1_ffn_W1': _L1_ffn_in['W1'], 'L1_ffn_b1': _L1_ffn_in['b1'], 'L1_ffn_W2': _L1_ffn_in['W2'], 'L1_ffn_b2': _L1_ffn_in['b2'], 'L1_ffn_gamma': _L1_ffn_in['gamma'], 'L1_ffn_beta': _L1_ffn_in['beta']}

def reference(x, src, dst, edge_weight, L0_gnn_W1, L0_gnn_b1, L0_gnn_ln_g1, L0_gnn_ln_b1, L0_gnn_W2, L0_gnn_b2, L0_gnn_ln_g2, L0_gnn_ln_b2, L0_ffn_Wr, L0_ffn_br, L0_ffn_ln_g, L0_ffn_ln_b, L0_ffn_W1, L0_ffn_b1, L0_ffn_W2, L0_ffn_b2, L1_gnn_weight, L1_gnn_w_ih, L1_gnn_w_hh, L1_gnn_b_ih, L1_gnn_b_hh, L1_ffn_Wr, L1_ffn_br, L1_ffn_W1, L1_ffn_b1, L1_ffn_W2, L1_ffn_b2, L1_ffn_gamma, L1_ffn_beta):
    import jax
    import jax.numpy as jnp

    def _L0_gnn_ref(x, edge_index, edge_weight, W1, b1, ln_g1, ln_b1, W2, b2, ln_g2, ln_b2):
        import jax, jax.numpy as jnp
        import numpy as np
        N = 3125
        E = 100000
        D = 256
        LN_EPS = 1e-05

        def _safe(x):
            return jnp.nan_to_num(x, nan=0.0, posinf=0.0, neginf=0.0)

        def _layernorm(h, g, b):
            mu = jnp.mean(h, axis=-1, keepdims=True)
            var = jnp.mean(jnp.square(h - mu), axis=-1, keepdims=True)
            return (h - mu) * jax.lax.rsqrt(var + LN_EPS) * g + b

        def _gcn_conv(h, row, col, ew, dis, W, b):
            xw = h @ W
            norm = dis[row] * ew * dis[col]
            msg = norm[:, None] * xw[row]
            agg = jax.ops.segment_sum(msg, col, num_segments=N)
            agg = agg + (dis * dis)[:, None] * xw
            return agg + b
        row, col = (edge_index[0], edge_index[1])
        h = _safe(x)
        ew = jnp.clip(jnp.abs(_safe(edge_weight.reshape(-1))), 1e-06, None)
        deg = jax.ops.segment_sum(ew, col, num_segments=N) + 1.0
        dis = jax.lax.rsqrt(deg)
        for W, b, g, be in ((W1, b1, ln_g1, ln_b1), (W2, b2, ln_g2, ln_b2)):
            h_res = h
            h = _gcn_conv(h, row, col, ew, dis, W, b)
            h = _safe(h)
            h = _safe(_layernorm(h, g, be))
            h = jax.nn.relu(h)
            h = _safe(h)
            h = _safe(h + h_res)
        return h

    def _L0_ffn_ref(x, Wr, br, ln_g, ln_b, W1, b1, W2, b2):
        import jax, jax.numpy as jnp
        import numpy as np
        TOP_K = 2
        LN_EPS = 1e-05
        B, S, D = x.shape
        N = B * S
        xt = x.reshape(N, D)
        logits = xt @ Wr + br
        probs = jax.nn.softmax(logits, axis=-1)
        top_p, top_idx = jax.lax.top_k(probs, TOP_K)
        weights = top_p / top_p.sum(axis=-1, keepdims=True)
        mu = xt.mean(axis=-1, keepdims=True)
        var = ((xt - mu) ** 2).mean(axis=-1, keepdims=True)
        xn = (xt - mu) * jax.lax.rsqrt(var + LN_EPS)
        xe = xn[None, :, :] * ln_g[:, None, :] + ln_b[:, None, :]
        h = jax.nn.gelu(jnp.einsum('end,edh->enh', xe, W1) + b1[:, None, :], approximate=False)
        y = jnp.einsum('enh,ehd->end', h, W2) + b2[:, None, :]
        y_tok = jnp.transpose(y, (1, 0, 2))
        sel = jnp.take_along_axis(y_tok, top_idx[:, :, None], axis=1)
        out = (weights[:, :, None] * sel).sum(axis=1)
        return out.reshape(B, S, D)

    def _L1_gnn_ref(x, edge_index, edge_attr, weight, w_ih, w_hh, b_ih, b_hh):
        import jax, jax.numpy as jnp
        import numpy as np
        N_NODES = 625
        N_EDGES = 10000
        D = 256
        NUM_LAYERS = 5

        def gru_cell(m, h, w_ih, w_hh, b_ih, b_hh):
            gi = m @ w_ih.T + b_ih
            gh = h @ w_hh.T + b_hh
            i_r, i_z, i_n = jnp.split(gi, 3, axis=1)
            h_r, h_z, h_n = jnp.split(gh, 3, axis=1)
            r = jax.nn.sigmoid(i_r + h_r)
            z = jax.nn.sigmoid(i_z + h_z)
            n = jnp.tanh(i_n + r * h_n)
            return (1.0 - z) * n + z * h
        src = edge_index[0]
        dst = edge_index[1]
        n_nodes = x.shape[0]
        h = x
        for i in range(weight.shape[0]):
            m = h @ weight[i]
            msgs = m[src] * edge_attr[:, None]
            agg = jax.ops.segment_sum(msgs, dst, num_segments=n_nodes)
            h = gru_cell(agg, h, w_ih, w_hh, b_ih, b_hh)
        return h

    def _L1_ffn_ref(x, Wr, br, W1, b1, W2, b2, gamma, beta):
        import math
        import jax, jax.numpy as jnp
        import numpy as np
        CAPACITY_FACTOR = 1.25
        TOP_K = 2
        LN_EPS = 1e-05

        def _layer_norm(x, gamma, beta):
            mu = jnp.mean(x, axis=-1, keepdims=True)
            var = jnp.var(x, axis=-1, keepdims=True)
            return (x - mu) * jax.lax.rsqrt(var + LN_EPS) * gamma + beta
        B, S, D = x.shape
        E = Wr.shape[1]
        N = B * S
        K = TOP_K
        logits = jnp.mean(x, axis=1) @ Wr + br
        routing_weights = jax.nn.softmax(logits, axis=-1)
        capacity = float(math.ceil(N * CAPACITY_FACTOR / E))
        expected_loads = routing_weights.sum(axis=0) * (N / B)
        scale = jnp.where(expected_loads > capacity, capacity / expected_loads, 1.0)
        routing_weights = jax.nn.softmax(routing_weights * scale, axis=-1)
        rw_tok = jnp.broadcast_to(routing_weights[:, None, :], (B, S, E)).reshape(N, E)
        top_w, top_i = jax.lax.top_k(rw_tok, K)
        top_w = jax.nn.softmax(top_w, axis=-1)
        xf = x.reshape(N, D)
        h = jax.nn.gelu(jnp.einsum('nd,edf->enf', xf, W1) + b1[:, None, :], approximate=False)
        y = jnp.einsum('enf,efd->end', h, W2) + b2[:, None, :]
        w_dense = jnp.zeros((N, E), x.dtype).at[jnp.arange(N)[:, None], top_i].add(top_w)
        out = jnp.einsum('ne,end->nd', w_dense, y).reshape(B, S, D)
        out = _layer_norm(out + x, gamma, beta)
        return out
    edge_index = jnp.stack([src, dst])
    x = x + _L0_gnn_ref(_layernorm(x, axis=-1), edge_index, edge_weight, L0_gnn_W1, L0_gnn_b1, L0_gnn_ln_g1, L0_gnn_ln_b1, L0_gnn_W2, L0_gnn_b2, L0_gnn_ln_g2, L0_gnn_ln_b2)
    x = x + _L0_ffn_ref(_layernorm(x, axis=-1)[None], L0_ffn_Wr, L0_ffn_br, L0_ffn_ln_g, L0_ffn_ln_b, L0_ffn_W1, L0_ffn_b1, L0_ffn_W2, L0_ffn_b2)[0]
    x = x + _L1_gnn_ref(_layernorm(x, axis=-1), edge_index, edge_weight, L1_gnn_weight, L1_gnn_w_ih, L1_gnn_w_hh, L1_gnn_b_ih, L1_gnn_b_hh)
    x = x + _L1_ffn_ref(_layernorm(x, axis=-1)[None], L1_ffn_Wr, L1_ffn_br, L1_ffn_W1, L1_ffn_b1, L1_ffn_W2, L1_ffn_b2, L1_ffn_gamma, L1_ffn_beta)[0]
    return x

_drawn_inputs = setup_inputs


def setup_inputs(seed=0):
    import zlib

    import numpy as np

    out = dict(_drawn_inputs(seed))
    spreads = {'L0_gnn_ln_g1': (1.0, 0.2),
     'L0_gnn_ln_b1': (0.0, 0.1),
     'L0_gnn_ln_g2': (1.0, 0.2),
     'L0_gnn_ln_b2': (0.0, 0.1),
     'L0_ffn_br': (0.0, 0.1),
     'L0_ffn_ln_g': (1.0, 0.2),
     'L0_ffn_ln_b': (0.0, 0.339),
     'L0_ffn_b1': (0.0, 0.338),
     'L0_ffn_b2': (0.0, 0.1),
     'L1_ffn_br': (0.0, 0.8),
     'L1_ffn_b1': (0.0, 0.594),
     'L1_ffn_b2': (0.0, 0.398),
     'L1_ffn_gamma': (1.0, 0.2),
     'L1_ffn_beta': (0.0, 0.281)}
    factors = {'L1_gnn_b_ih': 4.107, 'L1_gnn_b_hh': 6.248}
    for name, (base, spread) in spreads.items():
        noise = np.random.default_rng([zlib.crc32(name.encode()), seed]).standard_normal(out[name].shape)
        drawn = base * np.exp(spread * noise) if base else spread * noise
        out[name] = jnp.asarray(drawn.astype(out[name].dtype))
    for name, factor in factors.items():
        out[name] = (out[name] * factor).astype(out[name].dtype)
    return out
```

```python
import math

import concourse.bass as bass
from concourse import mybir
from contextlib import ExitStack, contextmanager

FP32 = mybir.dt.float32
BF16 = mybir.dt.bfloat16
I32 = mybir.dt.int32
U32 = mybir.dt.uint32
ALU = mybir.AluOpType
ACT = mybir.ActivationFunctionType
AX = mybir.AxisListType.X

N = 3125
D = 256
KD = D // 128
E = 50000
NT = -(-N // 128)
NP = NT * 128
EP = 125
ET = E // EP
G = 4
KB = 4
CW = 512
CT = CW // 128
NC = NP // CW
TW = NP - NC * CW
CH = NC + 1
RB = 5
RR = NT // RB
X0, H0 = 8, 1024
F1 = 512
LAYERS = 5
EPS = 1e-5
FLT_MAX = 3.4028234663852886e38
CAPACITY = float(math.ceil(N * 1.25 / X0))


class Count:

    def __init__(self, eng, sem):
        self.eng, self.sem, self.base, self.k = eng, sem, 0, 0

    def go(self, ins):
        self.k += 1
        ins.then_inc(self.sem, 1)

    def link(self, ins):
        self.go(ins)
        self.eng.wait_ge(self.sem, self.base + self.k)

    @contextmanager
    def loop(self, start, end, steps):
        base, k = self.base, self.k
        with self.eng.Fori(start, end) as i:
            self.base, self.k = base + i * steps + k - start * steps, 0
            yield i
            assert self.k == steps, (self.k, steps)
        self.base, self.k = base, k + steps * (end - start)


def build(nc, a, out):
    adj = nc.dram_tensor("adj", [NP * NP + NP, 2], FP32).ap()
    adj_sd = adj[0:NP * NP, :].rearrange("(s d) k -> s d k", d=NP)
    adj_w = nc.dram_tensor("adj_w", [NP, NP], FP32).ap()
    key_rows = nc.dram_tensor("key_rows", [ET, EP], FP32).ap()

    ctx = ExitStack()
    with ctx:
        scope = [ctx]

        def sb(n, s, d=FP32):
            return scope[-1].enter_context(nc.sbuf_tensor(n, s, d))

        def sem(n):
            return ctx.enter_context(nc.semaphore(n))

        bank = [ctx.enter_context(nc.psum_tensor(f"bank{n}", [128, 512], FP32)) for n in range(8)]
        agg_ps, gate_ps, tr_ps = bank[0:2], bank[2:6], bank[6:8]

        ident = sb("ident", [128, 128])
        row = sb("row", [128, 128])
        ones = sb("ones", [128, 128])
        dis = sb("dis", [128, NT])
        stats = sb("stats", [128, NT, 6])
        st_sum = sb("st_sum", [128, NT]); st_dif = sb("st_dif", [128, NT]); st_m2 = sb("st_m2", [128, NT]); st_sq = sb("st_sq", [128, NT])
        mean = sb("mean", [128, NT]); var = sb("var", [128, NT]); std = sb("std", [128, NT]); rstd = sb("rstd", [128, NT])
        res = sb("res", [128, NT, D])
        nat = sb("nat", [128, NT, D])
        nat2 = sb("nat2", [128, NT, D])
        scope.append(ExitStack())
        zeros = sb("zeros", [128, 2 * NP])
        srci = sb("srci", [EP, ET], I32); dsti = sb("dsti", [EP, ET], I32); w = sb("w", [EP, ET])
        wabs = sb("wabs", [EP, ET]); wbits = sb("wbits", [EP, ET]); finite = sb("finite", [EP, ET], U32)
        srcf = sb("srcf", [EP, ET]); dstf = sb("dstf", [EP, ET]); key = sb("key", [EP, ET])
        lo_i = sb("lo_i", [EP, ET], I32); hi_i = sb("hi_i", [EP, ET], I32)
        dlo = sb("dlo", [EP, ET]); dhi = sb("dhi", [EP, ET])
        spare_i = sb("spare_i", [EP, ET], I32); to_spare = sb("to_spare", [EP, ET]); rest = sb("rest", [EP, ET])
        parts0 = sb("parts0", [EP, ET, 8], BF16); parts1 = sb("parts1", [EP, ET, 8], BF16)
        before = sb("before", [EP, EP])
        keyT = sb("keyT", [100, 4, EP])
        keyrow = sb("keyrow", [EP, KB, G * EP])
        eq = sb("eq", [EP, 2, G, G * EP], BF16)
        hit_lo = sb("hit_lo", [EP, 2, G, 128]); hit_hi = sb("hit_hi", [EP, 2, G, NT])
        own = sb("own", [EP, 2, G, EP], BF16); own_n = sb("own_n", [EP, 2, G])
        sums = sb("sums", [EP, 2, G, 8]); half = sb("half", [EP, 2, G, 2]); pair = sb("pair", [EP, 2, G, 2])
        earlier = sb("earlier", [EP, 2, G]); shift = sb("shift", [EP, 2, G]); slot = sb("slot", [EP, 2, G], U32)
        scope.pop().close()
        xT = sb("xT", [128, KD, NP])
        scope.append(ExitStack())
        ring2 = sb("ring2", [128, RB, CW, 2])
        stage = sb("stage", [128, RB, CW])
        aggT = sb("aggT", [128, KD, CW])
        gw = sb("gw", [128, 2, KD, D])
        grow = sb("grow", [128, 2, 3, D])
        conv = sb("conv", [128, CT, D]); conv_d = sb("conv_d", [128, CT, D]); fin_mask = sb("fin_mask", [128, CT, D], U32)
        safe = sb("safe", [128, CT, D]); normed = sb("normed", [128, CT, D])
        scope.pop().close()
        scope.append(ExitStack())
        w1 = sb("w1", [128, 2, KD, H0]); w2 = sb("w2", [128, 2, H0 // 128, D])
        xe = sb("xe", [128, KD, CW]); hid = sb("hid", [128, H0 // 128, CW])
        ewr = sb("ewr", [128, KD, X0]); ebr = sb("ebr", [128, X0])
        eg = sb("eg", [128, KD, X0 + 1]); eb = sb("eb", [128, KD, X0 + 1]); eb1 = sb("eb1", [128, X0, H0 // 128]); eb2 = sb("eb2", [X0, D])
        lg = sb("lg", [128, NT, X0]); pr = sb("pr", [128, NT, X0]); t8 = sb("t8", [128, NT, X0]); u8 = sb("u8", [128, NT, X0])
        oh1 = sb("oh1", [128, NT, X0]); oh2 = sb("oh2", [128, NT, X0]); wd = sb("wd", [128, NT, X0])
        m1 = sb("m1", [128, NT]); m2 = sb("m2", [128, NT]); ix = sb("ix", [128, NT]); q1 = sb("q1", [128, NT]); q2 = sb("q2", [128, NT])
        wdT = sb("wdT", [X0, NP])
        scope.pop().close()
        scope.append(ExitStack())
        ringw = sb("ringw", [128, RB, RB, CW])
        gT = sb("gT", [128, KD, CW])
        spare = nat2[:, :, :].rearrange("p t f -> p (t f)")
        wt_sb = spare[:, 0:LAYERS * KD * D].rearrange("p (i k f) -> p i k f", i=LAYERS, k=KD)
        wih = sb("wih", [128, KD, 3 * D]); whh = sb("whh", [128, KD, 3 * D])
        v_all = sb("v_all", [128, LAYERS, KD, 3 * D]); v_now = sb("v_now", [128, KD, 3 * D])
        bih = sb("bih", [128, 6]); bhh = sb("bhh", [128, 6]); brz = sb("brz", [128, 4])
        gr, gz, gn, ga, gb = (spare[:, n * KD * CW:(n + 1) * KD * CW].rearrange("p (k c) -> p k c", k=KD) for n in range(5))
        scope.pop().close()
        scope.append(ExitStack())
        fw1 = sb("fw1", [128, 2, KD, F1]); fw2 = sb("fw2", [128, 2, F1 // 128, D]); fw2s = sb("fw2s", [128, 2, F1 // 128, D])
        fb1 = sb("fb1", [128, 2, F1 // 128]); fb2 = sb("fb2", [128, 2, D]); fmix = sb("fmix", [128, D])
        fwr = sb("fwr", [128, KD, X0]); fbr = sb("fbr", [1, X0]); fgb = sb("fgb", [128, 2, D])
        fhid = sb("fhid", [128, 2, F1 // 128, CW])
        fmean = sb("fmean", [128, KD]); r8 = [sb(f"r8_{n}", [1, X0]) for n in range(8)]; r1 = [sb(f"r1_{n}", [1, 1]) for n in range(6)]
        top = sb("top", [1, 8]); topi = sb("topi", [1, 8], U32); tw = sb("tw", [1, 2]); te = sb("te", [1, 2]); twb = sb("twb", [128, 2])
        fo = sb("fo", [128, CT, D]); fn = sb("fn", [128, CT, D])
        scope.pop().close()

        consts = sem("consts"); edges_in = sem("edges_in"); x_in = sem("x_in")
        zeroed = sem("zeroed"); diag_in = sem("diag_in"); dve_n = sem("dve_n")
        key_done = sem("key_done"); keyT_ps = sem("keyT_ps"); keyT_sb = sem("keyT_sb"); keyT_out = sem("keyT_out")
        keyrow_in = [sem(f"keyrow_in{b}") for b in range(KB)]
        compared = sem("compared"); summed = sem("summed"); sums_out = sem("sums_out"); placed = sem("placed")
        turn = sem("turn"); scattered = sem("scattered"); deg_done = sem("deg_done")
        var_ready = sem("var_ready"); std_ready = sem("std_ready")
        gcn_in = sem("gcn_in")
        hs_ready = sem("hs_ready"); chunk_done = [sem(f"chunk_done{l}") for l in range(2)]
        ring_in = [[sem(f"ring_in{l}_{b}") for b in range(RB)] for l in range(2)]
        used = [sem(f"used{l}") for l in range(2)]
        planes = sem("planes"); staged = sem("staged")
        aggT_rdy = [sem(f"aggT_rdy{l}") for l in range(2)]
        projd = [sem(f"projd{l}") for l in range(2)]; conv_taken = [sem(f"conv_taken{l}") for l in range(2)]
        cvar = [sem(f"cvar{l}") for l in range(2)]; cstd = [sem(f"cstd{l}") for l in range(2)]
        nat_ready = sem("nat_ready"); tr_done = sem("tr_done"); tr_out = sem("tr_out"); logits_done = sem("logits_done")
        moe_in = sem("moe_in"); lmax = sem("lmax"); lexp = sem("lexp"); wd_ready = sem("wd_ready"); wdT_done = sem("wdT_done"); wdT_out = sem("wdT_out")
        b2_done = sem("b2_done"); b2_taken = sem("b2_taken")
        w_in = [sem(f"w_in{b}") for b in range(2)]; w_used = sem("w_used")
        xe_ready = sem("xe_ready"); xe_used = sem("xe_used"); hid_ps = sem("hid_ps"); hid_rdy = sem("hid_rdy"); y_done = sem("y_done"); y_taken = sem("y_taken")
        gru_in = sem("gru_in"); v_ps = sem("v_ps"); v_out = sem("v_out"); v_set = sem("v_set")
        rw_in = [sem(f"rw_in{b}") for b in range(RB)]; rw_used = sem("rw_used")
        gT_rdy = sem("gT_rdy"); gates = sem("gates"); g_act = sem("g_act"); g_dve = sem("g_dve"); g_tanh = sem("g_tanh"); g_new = sem("g_new"); back_ps = sem("back_ps"); back_out = sem("back_out")
        f_in = sem("f_in"); f_mean = sem("f_mean"); f_meanT = sem("f_meanT"); f_lg = sem("f_lg"); f_e = sem("f_e"); f_a = sem("f_a"); f_top = sem("f_top"); f_twb = sem("f_twb"); fw_in = sem("fw_in"); fw_rdy = sem("fw_rdy")
        fh_ps = sem("fh_ps"); fh_rdy = sem("fh_rdy"); fy = sem("fy"); fy_taken = sem("fy_taken"); fvar = sem("fvar"); fstd = sem("fstd"); o_ready = sem("o_ready"); stored = sem("stored")

        held = sem("held")

        def hold(eng):
            eng.sem_inc(held, 1)

        block = ctx.enter_context(nc.Block())
        x_tiles = a["x"][0:(NT - 1) * 128, :].rearrange("(t p) f -> p t f", p=128)
        LAST = N - (NT - 1) * 128

        def bcast(v, rows=128):
            return v.rearrange("(a n) -> a n", a=1).to_broadcast([rows, v.shape[0]])

        @block.sync
        def _(sp):
            e = lambda v: v.rearrange("(p t) -> p t", p=EP)
            sp.dma_start(srci[:, :], e(a["src"])).then_inc(edges_in, 16)
            sp.dma_start(dsti[:, :], e(a["dst"])).then_inc(edges_in, 16)
            sp.dma_start(w[:, :], e(a["edge_weight"])).then_inc(edges_in, 16)
            sp.wait_ge(consts, 1)
            sp.dma_start(res[:, 0:NT - 1, :], x_tiles).then_inc(x_in, 16)
            sp.dma_start(res[0:LAST, NT - 1, :], a["x"][(NT - 1) * 128:N, :]).then_inc(x_in, 16)
            sp.wait_ge(consts, 2)
            for t in range(NT):
                sp.dma_start(adj[t * 128 * NP:(t + 1) * 128 * NP, :].rearrange("(p c) k -> p (c k)", p=128), zeros[:, :]).then_inc(zeroed, 16)
            sp.dma_start(adj[NP * NP:NP * NP + NP, :].rearrange("(p c) k -> p (c k)", p=128), zeros[:, 0:2 * NT]).then_inc(zeroed, 16)
            sp.wait_ge(zeroed, 16 * (NT + 1))
            sp.wait_ge(consts, 3)
            with nc.allow_non_contiguous_dma(reason="the diagonal"):
                sp.dma_start(bass.AP(tensor=adj.tensor, offset=1, ap=[[2 * (NP + 1) * NT, 128], [2 * (NP + 1), NT], [1, 1]]),
                             ones[:, 0:NT].rearrange("p (a b) -> p a b", b=1)).then_inc(diag_in, 16)
            sp.wait_ge(keyT_sb, 1)
            sp.dma_start(key_rows.rearrange("(c t) p -> t c p", c=4), keyT[:, :, :]).then_inc(keyT_out, 16)
            sp.wait_ge(keyT_out, 16)
            flat = key_rows.rearrange("t p -> (t p)").rearrange("(a n) -> a n", a=1)
            with sp.Fori(0, ET // G // KB) as i:
                for b in range(KB):
                    sp.wait_ge(compared, KB * i + b + 1)
                    hold(sp)
                    sp.dma_start(keyrow[:, b, :], flat[:, bass.ds((KB * i + b) * G * EP, G * EP)].to_broadcast([EP, G * EP])).then_inc(keyrow_in[b], 16)
            sp.wait_ge(scattered, 16 * ET)
            sp.wait_ge(hs_ready, 1)
            for l in range(2):
                k = l + 1
                sp.dma_start(gw[:, l, :, :], a[f"L0_gnn_W{k}"].rearrange("(k p) f -> p k f", p=128)).then_inc(gcn_in, 16)
                for m, n in enumerate((f"L0_gnn_b{k}", f"L0_gnn_ln_g{k}", f"L0_gnn_ln_b{k}")):
                    sp.dma_start(grow[:, l, m, :], bcast(a[n])).then_inc(gcn_in, 16)

            def load2(l, c, width, r, b):
                n = NT * c + RB * r + b
                sp.wait_ge(used[l], n + 1)
                if l == 0:
                    sp.wait_ge(planes, n + 1)
                hold(sp)
                t = RB * r + b
                sp.dma_start(ring2[:, b, 0:width, :], adj_sd[t * 128:(t + 1) * 128, bass.ds(c * CW, width), :]).then_inc(ring_in[l][b], 16)

            def store_plane(c, width, r):
                sp.wait_ge(planes, NT * c + RB * r + 2 * RB)
                hold(sp)
                sp.dma_start(adj_w[RB * r * 128:RB * (r + 1) * 128, bass.ds(c * CW, width)].rearrange("(b p) d -> p b d", p=128),
                             stage[:, :, 0:width]).then_inc(staged, 16)

            def loads2(l, c, width):
                for r in range(RR):
                    for b in range(RB):
                        load2(l, c, width, r, b)
                    if l == 0 and r:
                        store_plane(c, width, r - 1)
                if l == 0:
                    store_plane(c, width, RR - 1)

            sp.sem_inc(staged, 16)
            for l in range(2):
                with sp.Fori(0, NC) as c:
                    loads2(l, c, CW)
                loads2(l, NC, TW)
            sp.wait_ge(used[0], NT * CH + RB)
            sp.dma_start(nat[:, 0:NT - 1, :], x_tiles).then_inc(x_in, 16)
            sp.dma_start(nat[0:LAST, NT - 1, :], a["x"][(NT - 1) * 128:N, :]).then_inc(x_in, 16)
            sp.wait_ge(chunk_done[1], CH)
            sp.dma_start(ewr[:, :, :], a["L0_ffn_Wr"].rearrange("(k p) e -> p k e", p=128)).then_inc(moe_in, 16)
            sp.dma_start(ebr[:, :], bcast(a["L0_ffn_br"])).then_inc(moe_in, 16)
            sp.dma_start(eb2[:, :], a["L0_ffn_b2"]).then_inc(moe_in, 16)
            sp.dma_start(eg[:, :, 0:X0], a["L0_ffn_ln_gT"].rearrange("(k p) e -> p k e", p=128)).then_inc(moe_in, 16)
            sp.dma_start(eb[:, :, 0:X0], a["L0_ffn_ln_bT"].rearrange("(k p) e -> p k e", p=128)).then_inc(moe_in, 16)
            sp.dma_start(eb1[:, :, :].rearrange("p e h -> p (e h)"), a["L0_ffn_b1T"]).then_inc(moe_in, 16)
            w1_all = a["L0_ffn_W1"].rearrange("e d h -> (e d) h")
            w2_all = a["L0_ffn_W2"].rearrange("e h d -> (e h) d")
            with sp.Fori(0, X0 // 2) as i:
                for b in range(2):
                    sp.wait_ge(w_used, 2 * i + b + 1)
                    hold(sp)
                    sp.dma_start(w1[:, b, :, :], w1_all[bass.ds((2 * i + b) * D, D), :].rearrange("(k p) h -> p k h", p=128)).then_inc(w_in[b], 16)
                    sp.dma_start(w2[:, b, :, :], w2_all[bass.ds((2 * i + b) * H0, H0), :].rearrange("(k p) d -> p k d", p=128)).then_inc(w_in[b], 16)
            sp.wait_ge(y_taken, X0 * CH + 1)
            sp.dma_start(wih[:, :, :], a["L1_gnn_w_ihT"].rearrange("(k p) g -> p k g", p=128)).then_inc(gru_in, 16)
            sp.dma_start(whh[:, :, :], a["L1_gnn_w_hhT"].rearrange("(k p) g -> p k g", p=128)).then_inc(gru_in, 16)
            for i in range(LAYERS):
                sp.dma_start(wt_sb[:, i, :, :], a["L1_gnn_weightT"][i, :, :].rearrange("(k p) f -> p k f", p=128)).then_inc(gru_in, 16)
            sp.dma_start(bih[:, :], a["L1_gnn_b_ihT"]).then_inc(gru_in, 16)
            sp.dma_start(bhh[:, :], a["L1_gnn_b_hhT"]).then_inc(gru_in, 16)
            sp.wait_ge(staged, 16 * (RR * CH + 1))

            def loadw(i, c, width, r):
                n = RR * (CH * i + c) + r
                sp.wait_ge(rw_used, n + 1)
                hold(sp)
                sp.dma_start(ringw[:, r, :, 0:width], adj_w[RB * r * 128:RB * (r + 1) * 128, bass.ds(c * CW, width)].rearrange("(b p) d -> p b d", p=128)).then_inc(rw_in[r], 16)

            with sp.Fori(0, LAYERS) as i:
                with sp.Fori(0, NC) as c:
                    for r in range(RR):
                        loadw(i, c, CW, r)
                for r in range(RR):
                    loadw(i, NC, TW, r)
            sp.wait_ge(g_new, CH * LAYERS + 1)
            sp.wait_ge(back_out, NT * (LAYERS + 1) + 2)
            sp.dma_start(fwr[:, :, :], a["L1_ffn_Wr"].rearrange("(k p) e -> p k e", p=128)).then_inc(f_in, 16)
            sp.dma_start(fbr[:, :], bcast(a["L1_ffn_br"], 1)).then_inc(f_in, 16)
            sp.dma_start(fgb[:, 0, :], bcast(a["L1_ffn_gamma"])).then_inc(f_in, 16)
            sp.dma_start(fgb[:, 1, :], bcast(a["L1_ffn_beta"])).then_inc(f_in, 16)
            sp.wait_ge(f_top, 1)
            fw1_all = a["L1_ffn_W1"].rearrange("e d f -> (e d) f")
            fw2_all = a["L1_ffn_W2"].rearrange("e f d -> (e f) d")
            for k in range(2):
                x = sp.value_load(topi[0:1, k:k + 1], min_val=0, max_val=X0 - 1)
                sp.dma_start(fw1[:, k, :, :], fw1_all[bass.ds(x * D, D), :].rearrange("(k p) h -> p k h", p=128)).then_inc(fw_in, 16)
                sp.dma_start(fw2[:, k, :, :], fw2_all[bass.ds(x * F1, F1), :].rearrange("(k p) d -> p k d", p=128)).then_inc(fw_in, 16)
                sp.dma_start(fb2[:, k, :], a["L1_ffn_b2"][bass.ds(x, 1), :].to_broadcast([128, D])).then_inc(fw_in, 16)
                sp.dma_start(fb1[:, k, :], a["L1_ffn_b1T"][bass.ds(x * 128, 128), :]).then_inc(fw_in, 16)
            with sp.Fori(0, NC) as c:
                sp.wait_ge(o_ready, c + 1)
                hold(sp)
                sp.dma_start(out[bass.ds(c * CW, CW), :].rearrange("(t p) f -> p t f", p=128), res[:, bass.ds(c * CT, CT), :]).then_inc(stored, 16)
            sp.wait_ge(o_ready, CH)
            sp.dma_start(out[NC * CW:N, :], res[0:LAST, NT - 1, :]).then_inc(stored, 16)
            sp.wait_ge(stored, 16 * CH)

        @block.gpsimd
        def _(pool):
            g_ = nc.gpsimd
            g_.memset(res[:, :, :], 0.0).then_inc(consts, 1)
            g_.memset(zeros[:, :], 0.0).then_inc(consts, 1)
            g_.memset(ones[:, :], 1.0).then_inc(consts, 1)
            g_.memset(ident[:, :], 0.0).then_inc(consts, 1)
            g_.memset(before[:, :], 1.0).then_inc(consts, 1)
            g_.iota(row[:, :], [[1, 128]], base=0, channel_multiplier=0, allow_small_or_imprecise_dtypes=True).then_inc(consts, 1)
            g_.iota(spare_i[:, :], [[0, ET // G], [EP, G]], base=NP * NP, channel_multiplier=1).then_inc(consts, 1)
            pool.wait_ge(consts, 7)
            g_.affine_select(out=ident[:, :], in_=ident[:, :], compare_op=ALU.not_equal, fill=1.0, base=0, pattern=[[-1, 128]], channel_multiplier=1).then_inc(consts, 1)
            g_.affine_select(out=before[:, :], in_=before[:, :], compare_op=ALU.is_gt, fill=0.0, base=0, pattern=[[-1, EP]], channel_multiplier=1).then_inc(consts, 1)
            pool.wait_ge(diag_in, 16)
            pool.sem_inc(turn, 1)
            with pool.Fori(0, ET // G // KB) as i:
                for b in range(KB):
                    pool.wait_ge(placed, KB * i + b + 3)
                    pool.sem_inc(turn, 1)
                    for g in range(G):
                        g_.indirect_dma_start(out=adj, out_offset=bass.IndirectOffsetOnAxis(slot[:, b % 2, g:g + 1], 0),
                                              in_=pair[:, b % 2, g, :], in_offset=None, compute_op=ALU.add).then_inc(scattered, 16)
                    pool.wait_ge(scattered, 16 * G * (KB * i + b + 1))

        @block.tensor
        def _(pe):
            mm, tr = nc.tensor.matmul, nc.tensor.transpose
            ps_sum = [bank[b][0:EP, 0:8 * G].rearrange("p (g k) -> p g k", k=8) for b in range(2)]
            ps_deg = bank[2][:, 0:NT]
            ps_key = bank[3][0:100, 0:4 * EP].rearrange("p (c k) -> p c k", c=4)
            pe.sem_inc(summed, 2)
            pe.wait_ge(consts, 9)
            mm(ps_deg, zeros[0:EP, 0:128], zeros[0:EP, 0:NT], start=True, stop=False)
            pe.wait_ge(key_done, 1)
            for c in range(4):
                last = tr(ps_key[:, c, :], key[:, c * 100:(c + 1) * 100], ident[0:EP, 0:EP])
            last.then_inc(keyT_ps, 1)
            with pe.Fori(0, ET // G // KB) as i:
                for b in range(KB):
                    pe.wait_ge(compared, KB * i + b + 1 + KB)
                    pe.wait_ge(sums_out, KB * i + b + 1)
                    for g in range(G):
                        for q in range(G):
                            parts = (parts1 if q < g else parts0)[:, bass.ds(KB * G * i + G * b + q, 1), :].rearrange("p a k -> p (a k)")
                            mm(ps_sum[b % 2][:, g, :], eq[:, b % 2, q, g * EP:(g + 1) * EP], parts, start=(q == 0), stop=(q == G - 1))
                    for g in range(G):
                        last = mm(ps_deg, hit_lo[:, b % 2, g, :], hit_hi[:, b % 2, g, :], start=False, stop=False)
                    last.then_inc(summed, 1)
            mm(ps_deg, zeros[0:EP, 0:128], zeros[0:EP, 0:NT], start=False, stop=True).then_inc(deg_done, 1)

            for l in range(2):
                hs = (nat, nat2)[l]
                pe.sem_inc(used[l], RB)

                def project(c, tiles):
                    pe.wait_ge(aggT_rdy[l], c + 2)
                    pe.wait_ge(conv_taken[l], c + 1)
                    for j in range(tiles):
                        for k in range(KD):
                            last = mm(gate_ps[j][:, 0:D], aggT[:, k, j * 128:(j + 1) * 128], gw[:, l, k, :], start=(k == 0), stop=(k == KD - 1))
                    last.then_inc(projd[l], 1)

                def aggregate(c, width, first=False, mid=None):
                    for t in range(NT):
                        if t == 0:
                            pe.wait_ge(aggT_rdy[l], c + 1)
                        if first and l == 0 and t == 0:
                            pe.wait_ge(hs_ready, 1)
                        if first and l == 1 and t % CT == 0:
                            pe.wait_ge(chunk_done[0], t // CT + 1)
                        pe.wait_ge(ring_in[l][t % RB], (RR * c + t // RB) * 16 + 16)
                        for f in range(KD):
                            last = mm(agg_ps[f][:, 0:width], hs[:, t, f * 128:(f + 1) * 128], ring2[:, t % RB, 0:width, 1], start=(t == 0), stop=(t == NT - 1))
                        last.then_inc(used[l], 1)
                        if mid and t == NT // 3:
                            mid()

                aggregate(0, CW, first=True)
                if l == 0:
                    pe.wait_ge(gcn_in, 16 * 8)
                with pe.Fori(0, NC - 1) as c:
                    aggregate(c + 1, CW, mid=lambda: project(c, CT))
                aggregate(NC, TW, mid=lambda: project(NC - 1, CT))
                project(NC, TW // 128)

            turned = [0]

            def transpose_in(src):
                for t in range(NT):
                    n = turned[0]
                    if n >= 2:
                        pe.wait_ge(tr_out, n - 1)
                    for k in range(KD):
                        last = tr(tr_ps[n % 2][:, k * 128:(k + 1) * 128], src[:, t, k * 128:(k + 1) * 128], ident[:, :])
                    last.then_inc(tr_done, 1)
                    turned[0] += 1

            pe.wait_ge(nat_ready, 1)
            transpose_in(nat)
            pe.wait_ge(tr_out, NT)
            pe.wait_ge(moe_in, 16 * 6)
            for t in range(NT):
                for k in range(KD):
                    last = mm(bank[0][:, t * X0:(t + 1) * X0], xT[:, k, t * 128:(t + 1) * 128], ewr[:, k, :], start=(k == 0), stop=(k == KD - 1))
            last.then_inc(logits_done, 1)
            pe.wait_ge(nat_ready, 2)
            transpose_in(nat2)
            pe.wait_ge(wd_ready, 1)
            for t in range(NT):
                if t % 4 == 0 and t >= 8:
                    pe.wait_ge(wdT_out, t // 4 - 1)
                last = tr(bank[t // 4 % 2][0:X0, t % 4 * 128:(t % 4 + 1) * 128], wd[:, t, :], ident[:, :])
                if t % 4 == 3 or t == NT - 1:
                    last.then_inc(wdT_done, 1)
            pe.wait_ge(wdT_out, -(-NT // 4))
            for t in range(NT):
                if t >= 4:
                    pe.wait_ge(b2_taken, t - 3)
                mm(gate_ps[t % 4][:, 0:D], wdT[:, t * 128:(t + 1) * 128], eb2[:, :], start=True, stop=True).then_inc(b2_done, 1)
            pe.wait_ge(b2_taken, NT)
            pe.wait_ge(tr_out, 2 * NT)

            y_ps = [bank[0], bank[1], bank[6], bank[7]]

            def experts(n, b, width):
                pe.wait_ge(xe_ready, n + 1)
                for h in range(H0 // 128):
                    pe.wait_ge(hid_rdy, 8 * n + h + 1)
                    for k in range(KD):
                        last = mm(gate_ps[h % 4][:, 0:width], w1[:, b, k, h * 128:(h + 1) * 128], xe[:, k, 0:width], start=(k == 0), stop=(k == KD - 1))
                    last.then_inc(hid_ps, 1)
                pe.wait_ge(y_taken, n + 1)
                for h in range(H0 // 128):
                    pe.wait_ge(hid_rdy, 8 * n + h + 5)
                    for j in range(width // 128):
                        last = mm(y_ps[j][:, 0:D], hid[:, h, j * 128:(j + 1) * 128], w2[:, b, h, :], start=(h == 0), stop=(h == H0 // 128 - 1))
                last.then_inc(y_done, 1)

            pe.sem_inc(w_used, 2)
            with pe.Fori(0, X0 // 2) as i:
                for b in range(2):
                    pe.wait_ge(w_in[b], 32 * i + 32)
                    hold(pe)
                    with pe.Fori(0, NC) as c:
                        experts(CH * (2 * i + b) + c, b, CW)
                    experts(CH * (2 * i + b) + NC, b, TW)
                    pe.wait_ge(y_done, CH * (2 * i + b) + CH + 1)
                    pe.sem_inc(w_used, 1)

            pe.wait_ge(gru_in, 16 * (4 + LAYERS))
            pe.wait_ge(y_taken, X0 * CH + 1)
            n = 0
            for i in range(LAYERS):
                for m in range(KD):
                    for lo, hi in ((0, 512), (512, 768)):
                        if n >= 4:
                            pe.wait_ge(v_out, n - 3)
                        for k in range(KD):
                            last = mm(gate_ps[n % 4][:, 0:hi - lo], wt_sb[:, i, k, m * 128:(m + 1) * 128], wih[:, k, lo:hi], start=(k == 0), stop=(k == KD - 1))
                        last.then_inc(v_ps, 1)
                        n += 1
            pe.wait_ge(nat_ready, 3)
            transpose_in(nat)
            pe.wait_ge(tr_out, 3 * NT)
            pe.wait_ge(v_out, n)
            pe.sem_inc(rw_used, RR)

            def turn_back(i, t):
                pe.wait_ge(back_out, NT * i + t + (2 if t == 0 else 1))
                for k in range(KD):
                    last = tr(tr_ps[t % 2][:, k * 128:(k + 1) * 128], xT[:, k, t * 128:(t + 1) * 128], ident[:, :])
                last.then_inc(back_ps, 1)

            def aggregate_w(i, c, width, back=False, mid=None):
                q = CH * i + c
                for t in range(NT):
                    if t == 0:
                        pe.wait_ge(gT_rdy, q + 1)
                    if back and t + 2 < NT:
                        turn_back(i, t + 2)
                    if back:
                        pe.wait_ge(back_out, NT * i + t + 3)
                    if t % RB == 0:
                        pe.wait_ge(rw_in[t // RB], q * 16 + 16)
                    for f in range(KD):
                        last = mm(agg_ps[f][:, 0:width], nat[:, t, f * 128:(f + 1) * 128], ringw[:, t // RB, t % RB, 0:width], start=(t == 0), stop=(t == NT - 1))
                    if t % RB == RB - 1:
                        last.then_inc(rw_used, 1)
                    if mid and t == NT // 3:
                        mid()

            def gate_products(i, c, width):
                q = CH * i + c
                pe.wait_ge(gT_rdy, q + 2)
                at = bass.ds(c * CW, width)
                for j in range(KD):
                    pe.wait_ge(g_act, 2 * q + j + 1)
                    pe.wait_ge(g_dve, 2 * q + j + 1)
                    for b, blk, parts in ((0, j, "ih"), (1, KD + j, "ih"), (2, 2 * KD + j, "i"), (3, 2 * KD + j, "h")):
                        cols = slice(blk * 128, (blk + 1) * 128)
                        ops = [(v_now[:, k, cols], gT[:, k, 0:width]) for k in range(KD)] * ("i" in parts)
                        ops += [(whh[:, k, cols], xT[:, k, at]) for k in range(KD)] * ("h" in parts)
                        for m, (lhs, rhs) in enumerate(ops):
                            last = mm(gate_ps[b][:, 0:width], lhs, rhs, start=(m == 0), stop=(m == len(ops) - 1))
                    last.then_inc(gates, 1)

            with pe.Fori(0, LAYERS) as i:
                pe.wait_ge(g_new, CH * i + 1)
                turn_back(i, 0)
                turn_back(i, 1)
                aggregate_w(i, 0, CW, back=True)
                pe.wait_ge(v_set, i + 1)
                hold(pe)
                with pe.Fori(0, NC - 1) as c:
                    aggregate_w(i, c + 1, CW, mid=lambda: gate_products(i, c, CW))
                aggregate_w(i, NC, TW, mid=lambda: gate_products(i, NC - 1, CW))
                gate_products(i, NC, TW)
            pe.wait_ge(g_new, CH * LAYERS + 1)
            for t in range(NT):
                turn_back(LAYERS, t)

            pe.wait_ge(nat_ready, 4)
            pe.wait_ge(back_out, NT * (LAYERS + 1) + 2)
            for k in range(KD):
                for t in range(NT):
                    rows = 128 if t < NT - 1 else LAST
                    last = mm(bank[0][:, k:k + 1], nat[0:rows, t, k * 128:(k + 1) * 128], ones[0:rows, 0:1], start=(t == 0), stop=(t == NT - 1))
            last.then_inc(f_mean, 1)
            transpose_in(nat)
            pe.wait_ge(f_meanT, 1)
            pe.wait_ge(f_in, 64)
            for k in range(KD):
                last = mm(bank[1][0:1, 0:X0], fmean[:, k:k + 1], fwr[:, k, :], start=(k == 0), stop=(k == KD - 1))
            last.then_inc(f_lg, 1)
            pe.wait_ge(f_top, 1)
            mm(bank[1][:, 16:18], ones[0:1, 0:128], tw[0:1, 0:2], start=True, stop=True).then_inc(f_twb, 1)
            pe.wait_ge(tr_out, 4 * NT)
            pe.wait_ge(fw_rdy, 1)

            HB = F1 // 128

            def second(c, width):
                at = bass.ds(c * CW, width)
                for x in range(2):
                    for h in range(HB):
                        m = x * HB + h
                        pe.wait_ge(fh_rdy, 2 * HB * c + m + 1)
                        for k in range(KD):
                            last = mm(gate_ps[m % 4][:, 0:width], fw1[:, x, k, h * 128:(h + 1) * 128], xT[:, k, at], start=(k == 0), stop=(k == KD - 1))
                        last.then_inc(fh_ps, 1)
                pe.wait_ge(fy_taken, c + 1)
                for m in range(2 * HB):
                    pe.wait_ge(fh_rdy, 2 * HB * c + m + 5)
                    for j in range(width // 128):
                        last = mm(y_ps[j][:, 0:D], fhid[:, m // HB, m % HB, j * 128:(j + 1) * 128], fw2s[:, m // HB, m % HB, :], start=(m == 0), stop=(m == 2 * HB - 1))
                last.then_inc(fy, 1)

            with pe.Fori(0, NC) as c:
                second(c, CW)
            second(NC, TW)

        @block.scalar
        def _(act):
            A = nc.scalar.activation
            roots = [0]

            def root(view, src):
                act.wait_ge(var_ready, roots[0] + 1)
                roots[0] += 1
                A(view, src, ACT.Sqrt).then_inc(std_ready, 1)

            root(std[:, :], var[:, :])
            act.sem_inc(sums_out, 2)
            act.wait_ge(keyT_ps, 1)
            A(keyT[:, :, :], bank[3][0:100, 0:4 * EP].rearrange("p (c k) -> p c k", c=4), ACT.Copy).then_inc(keyT_sb, 1)
            with act.Fori(0, ET // G // KB) as i:
                for b in range(KB):
                    act.wait_ge(summed, KB * i + b + 3)
                    act.wait_ge(placed, KB * i + b + 1)
                    A(sums[:, b % 2, :, :], bank[b % 2][0:EP, 0:8 * G].rearrange("p (g k) -> p g k", k=8), ACT.Copy).then_inc(sums_out, 1)
            root(std[:, :], var[:, :])

            act.sem_inc(planes, RB)
            for l in range(2):
                act.sem_inc(aggT_rdy[l], 1)

                def chunk(c, width):
                    if l == 0:
                        for t in range(NT):
                            if t % RB == 0:
                                act.wait_ge(staged, 16 * (RR * c + t // RB) + 16)
                            act.wait_ge(ring_in[0][t % RB], (RR * c + t // RB) * 16 + 16)
                            A(stage[:, t % RB, 0:width], ring2[:, t % RB, 0:width, 0], ACT.Copy).then_inc(planes, 1)
                    act.wait_ge(used[l], NT * c + NT + RB)
                    act.wait_ge(projd[l], c + 1)
                    for f in range(KD):
                        last = A(aggT[:, f, 0:width], agg_ps[f][:, 0:width], ACT.Copy)
                    last.then_inc(aggT_rdy[l], 1)

                def chunk_root(c, tiles):
                    act.wait_ge(cvar[l], c + 1)
                    A(std[:, 0:tiles], var[:, 0:tiles], ACT.Sqrt).then_inc(cstd[l], 1)

                act.sem_inc(projd[l], 1)
                chunk(0, CW)
                with act.Fori(0, NC - 1) as c:
                    chunk(c + 1, CW)
                    chunk_root(c, CT)
                chunk(NC, TW)
                chunk_root(NC - 1, CT)
                chunk_root(NC, TW // 128)

            evicted = [0]

            def evict_turned():
                for t in range(NT):
                    n = evicted[0]
                    act.wait_ge(tr_done, n + 1)
                    A(xT[:, :, t * 128:(t + 1) * 128], tr_ps[n % 2][:, 0:D].rearrange("p (k n) -> p k n", k=KD), ACT.Copy).then_inc(tr_out, 1)
                    evicted[0] += 1

            root(std[:, :], var[:, :])
            root(std[:, :], var[:, :])
            evict_turned()
            act.wait_ge(lmax, 1)
            A(pr[:, :, :], t8[:, :, :], ACT.Exp).then_inc(lexp, 1)
            act.wait_ge(logits_done, 1)
            evict_turned()
            for n in range(-(-NT // 4)):
                act.wait_ge(wdT_done, n + 1)
                wide = min(512, NP - n * 512)
                A(wdT[:, n * 512:n * 512 + wide], bank[n % 2][0:X0, 0:wide], ACT.Copy).then_inc(wdT_out, 1)

            act.sem_inc(hid_rdy, 4)
            act.sem_inc(y_done, 1)

            def gelu_chunk(n, e, width):
                for h in range(H0 // 128):
                    act.wait_ge(hid_ps, 8 * n + h + 1)
                    if h == 0:
                        act.wait_ge(y_done, n + 1)
                    A(hid[:, h, 0:width], gate_ps[h % 4][:, 0:width], ACT.Gelu,
                      bias=eb1[:, bass.ds(e, 1), h:h + 1].rearrange("p a b -> p (a b)")).then_inc(hid_rdy, 1)

            with act.Fori(0, X0) as e:
                with act.Fori(0, NC) as c:
                    gelu_chunk(CH * e + c, e, CW)
                gelu_chunk(CH * e + NC, e, TW)

            root(std[:, :], var[:, :])
            act.wait_ge(gru_in, 16 * (4 + LAYERS))
            n = 0
            for i in range(LAYERS):
                for m in range(KD):
                    for lo, hi in ((0, 512), (512, 768)):
                        act.wait_ge(v_ps, n + 1)
                        A(v_all[:, i, m, lo:hi], gate_ps[n % 4][:, 0:hi - lo], ACT.Copy).then_inc(v_out, 1)
                        n += 1
            evict_turned()
            act.sem_inc(back_out, 2)
            act.sem_inc(gT_rdy, 1)
            act.sem_inc(g_act, 1)
            act.wait_ge(v_out, n)

            def back(i, t):
                act.wait_ge(back_ps, NT * i + t + 1)
                A(nat[:, t, :], tr_ps[t % 2][:, 0:D], ACT.Copy).then_inc(back_out, 1)

            def gru_evict(i, c, width):
                q = CH * i + c
                act.wait_ge(rw_used, RR * (q + 2))
                act.wait_ge(gates, 2 * q + 1)
                for f in range(KD):
                    last = A(gT[:, f, 0:width], agg_ps[f][:, 0:width], ACT.Copy)
                last.then_inc(gT_rdy, 1)

            def gru_act(i, c, width):
                q = CH * i + c
                act.wait_ge(g_new, q + 1)
                for j in range(KD):
                    act.wait_ge(gates, 2 * q + j + 2)
                    A(gr[:, j, 0:width], gate_ps[0][:, 0:width], ACT.Sigmoid, bias=brz[:, j:j + 1])
                    A(gz[:, j, 0:width], gate_ps[1][:, 0:width], ACT.Sigmoid, bias=brz[:, KD + j:KD + j + 1]).then_inc(g_act, 1)
                for j in range(KD):
                    act.wait_ge(g_dve, 2 * q + j + 2)
                    A(gn[:, j, 0:width], gb[:, j, 0:width], ACT.Tanh, bias=bih[:, 2 * KD + j:2 * KD + j + 1]).then_inc(g_tanh, 1)

            act.sem_inc(gates, 1)
            with act.Fori(0, LAYERS) as i:
                for t in range(NT):
                    back(i, t)
                    if t == 2:
                        A(v_now[:, :, :], v_all[:, bass.ds(i, 1), :, :].rearrange("p a k g -> p (a k) g"), ACT.Copy).then_inc(v_set, 1)
                gru_evict(i, 0, CW)
                with act.Fori(0, NC - 1) as c:
                    gru_act(i, c, CW)
                    gru_evict(i, c + 1, CW)
                gru_act(i, NC - 1, CW)
                gru_evict(i, NC, TW)
                gru_act(i, NC, TW)
            for t in range(NT):
                back(LAYERS, t)

            root(std[:, :], var[:, :])
            evict_turned()
            act.wait_ge(f_e, 1)
            A(r8[1][:, :], r8[0][:, :], ACT.Exp, accum_out=r1[1][:, :]).then_inc(f_a, 1)
            act.wait_ge(f_e, 2)
            A(r8[6][:, :], r8[5][:, :], ACT.Exp, accum_out=r1[3][:, :]).then_inc(f_a, 1)
            act.wait_ge(f_e, 3)
            A(te[:, :], te[:, :], ACT.Exp, accum_out=r1[4][:, :]).then_inc(f_a, 1)

            act.sem_inc(fh_rdy, 4)
            act.sem_inc(fy, 1)
            act.wait_ge(fw_in, 16 * 8)
            HB = F1 // 128

            def second(c, width):
                for m in range(2 * HB):
                    act.wait_ge(fh_ps, 2 * HB * c + m + 1)
                    if m == 0:
                        act.wait_ge(fy, c + 1)
                    A(fhid[:, m // HB, m % HB, 0:width], gate_ps[m % 4][:, 0:width], ACT.Gelu, bias=fb1[:, m // HB, m % HB:m % HB + 1]).then_inc(fh_rdy, 1)

            def second_root(c, tiles):
                act.wait_ge(fvar, c + 1)
                A(std[:, 0:tiles], var[:, 0:tiles], ACT.Sqrt).then_inc(fstd, 1)

            with act.Fori(0, NC) as c:
                second(c, CW)
                second_root(c, CT)
            second(NC, TW)
            second_root(NC, TW // 128)

        @block.vector
        def _(v):
            V = nc.vector
            ch = Count(v, dve_n)
            link, go = ch.link, ch.go

            def moments(tiles):
                s = lambda k: stats[:, 0:tiles, k]
                go(V.tensor_tensor(st_sum[:, 0:tiles], s(1), s(4), ALU.add))
                go(V.tensor_tensor(st_dif[:, 0:tiles], s(1), s(4), ALU.subtract))
                link(V.tensor_tensor(st_m2[:, 0:tiles], s(2), s(5), ALU.add))
                go(V.tensor_scalar(mean[:, 0:tiles], st_sum[:, 0:tiles], 0.5, None, ALU.mult))
                go(V.tensor_tensor(st_sq[:, 0:tiles], st_dif[:, 0:tiles], st_dif[:, 0:tiles], ALU.mult))
                link(V.tensor_scalar(st_m2[:, 0:tiles], st_m2[:, 0:tiles], 1.0 / D, EPS, ALU.mult, ALU.add))
                return V.scalar_tensor_tensor(var[:, 0:tiles], st_sq[:, 0:tiles], 0.25, st_m2[:, 0:tiles], ALU.mult, ALU.add)

            roots = [0]

            def inverse_root():
                v.wait_ge(std_ready, roots[0] + 1)
                roots[0] += 1
                link(V.reciprocal(rstd[:, :], std[:, :]))

            def layernorm(dst, src):
                with ch.loop(0, NT, 1) as t:
                    go(V.bn_stats(stats[:, bass.ds(t, 1), :].rearrange("p a k -> p (a k)"), src[:, bass.ds(t, 1), :].rearrange("p a f -> p (a f)")))
                v.wait_ge(ch.sem, ch.base + ch.k)
                moments(NT).then_inc(var_ready, 1)
                inverse_root()
                with ch.loop(0, NT, 1) as t:
                    go(V.tensor_scalar(dst[:, bass.ds(t, 1), :].rearrange("p a f -> p (a f)"), src[:, bass.ds(t, 1), :].rearrange("p a f -> p (a f)"),
                                       mean[:, bass.ds(t, 1)], rstd[:, bass.ds(t, 1)], ALU.subtract, ALU.mult))
                v.wait_ge(ch.sem, ch.base + ch.k)

            v.sem_inc(placed, 2)
            v.wait_ge(edges_in, 48)
            go(V.tensor_copy(srcf[:, :], srci[:, :]))
            link(V.tensor_copy(dstf[:, :], dsti[:, :]))
            V.scalar_tensor_tensor(key[:, :], srcf[:, :], float(NP), dstf[:, :], ALU.mult, ALU.add).then_inc(key_done, 1)
            go(V.tensor_scalar(lo_i[:, :], dsti[:, :], 127, None, ALU.bitwise_and))
            go(V.tensor_scalar(hi_i[:, :], dsti[:, :], 7, None, ALU.logical_shift_right))
            go(V.tensor_scalar(wbits[:, :].bitcast(I32), w[:, :].bitcast(I32), 0x7fffffff, None, ALU.bitwise_and))
            go(V.memset(wabs[:, :], 1e-6))
            go(V.memset(parts0[:, :, :], 0.0))
            link(V.memset(parts1[:, :, :], 1.0))
            go(V.tensor_copy(dlo[:, :], lo_i[:, :]))
            go(V.tensor_copy(dhi[:, :], hi_i[:, :]))
            go(V.tensor_scalar(finite[:, :], wbits[:, :], FLT_MAX, None, ALU.is_le))
            v.wait_ge(consts, 9)
            link(V.tensor_copy(to_spare[:, :], spare_i[:, :]))
            go(V.tensor_tensor(to_spare[:, :], to_spare[:, :], key[:, :], ALU.subtract))
            link(V.copy_predicated(wabs[:, :], finite[:, :], wbits[:, :]))
            link(V.tensor_scalar(wabs[:, :], wabs[:, :], 1e-6, None, ALU.max))
            for k, x in enumerate((w, wabs)):
                link(V.tensor_copy(parts0[:, :, 3 * k], x[:, :]))
                link(V.tensor_tensor(rest[:, :], x[:, :], parts0[:, :, 3 * k], ALU.subtract))
                link(V.tensor_copy(parts0[:, :, 3 * k + 1], rest[:, :]))
                link(V.tensor_tensor(rest[:, :], rest[:, :], parts0[:, :, 3 * k + 1], ALU.subtract))
                link(V.tensor_copy(parts0[:, :, 3 * k + 2], rest[:, :]))
            link(V.tensor_copy(parts1[:, :, 0:6], parts0[:, :, 0:6]))
            v.sem_inc(compared, KB)
            v.wait_ge(x_in, 32)
            layernorm(res, res)

            def compare(i, b):
                c = b % 2
                v.wait_ge(keyrow_in[b], 16 * i + 16)
                v.wait_ge(summed, KB * i + b + 1)
                at = lambda x, g: x[:, bass.ds(KB * G * i + G * b + g, 1)]
                for g in range(G):
                    V.tensor_scalar(eq[:, c, g, :], keyrow[:, b, :], at(key, g), None, ALU.is_equal)
                for g in range(G):
                    V.scalar_tensor_tensor(own[:, c, g, :], keyrow[:, b, g * EP:(g + 1) * EP], at(key, g), before[:, :], ALU.is_equal, ALU.mult, accum_out=own_n[:, c, g:g + 1])
                for g in range(G):
                    V.tensor_scalar(hit_lo[:, c, g, :], row[0:EP, :], at(dlo, g), None, ALU.is_equal)
                    last = V.tensor_scalar(hit_hi[:, c, g, :], row[0:EP, 0:NT], at(dhi, g), at(wabs, g), ALU.is_equal, ALU.mult)
                last.then_inc(compared, 1)

            def place(i, b):
                c = b % 2
                v.wait_ge(sums_out, KB * i + b + 3)
                v.wait_ge(turn, KB * i + b + 1)
                at = lambda x: x[:, bass.ds(KB * G * i + G * b, G)]
                V.tensor_tensor(half[:, c, :, :], sums[:, c, :, 1:5:3], sums[:, c, :, 2:6:3], ALU.add)
                link(V.tensor_tensor(earlier[:, c, :], sums[:, c, :, 6], own_n[:, c, :], ALU.add))
                V.tensor_tensor(pair[:, c, :, :], sums[:, c, :, 0:4:3], half[:, c, :, :], ALU.add)
                link(V.scalar_tensor_tensor(shift[:, c, :], earlier[:, c, :], 1.0, at(to_spare), ALU.min, ALU.mult))
                V.tensor_tensor(slot[:, c, :], shift[:, c, :], at(key), ALU.add).then_inc(placed, 1)

            with ch.loop(0, ET // G // KB, 2 * KB) as i:
                for b in range(0, KB, 2):
                    compare(i, b)
                    compare(i, b + 1)
                    place(i, b)
                    place(i, b + 1)
            v.wait_ge(deg_done, 1)
            V.tensor_scalar(var[:, :], bank[2][:, 0:NT], 1.0, None, ALU.add).then_inc(var_ready, 1)
            v.wait_ge(std_ready, roots[0] + 1)
            roots[0] += 1
            link(V.reciprocal(dis[:, :], std[:, :]))
            v.wait_ge(scattered, 16 * ET)
            with ch.loop(0, NT, 1) as t:
                go(V.tensor_scalar(nat[:, bass.ds(t, 1), :].rearrange("p a f -> p (a f)"), res[:, bass.ds(t, 1), :].rearrange("p a f -> p (a f)"), dis[:, bass.ds(t, 1)], None, ALU.mult))
            v.wait_ge(ch.sem, ch.base + ch.k)
            v.sem_inc(hs_ready, 1)

            v.wait_ge(gcn_in, 16 * 8)
            for l in range(2):
                v.sem_inc(conv_taken[l], 1)

                def finish(c, tiles):
                    at = lambda x: x[:, bass.ds(c * CT, tiles), :]
                    rows = lambda m: grow[:, l, m:m + 1, :].to_broadcast([128, tiles, D])
                    v.wait_ge(projd[l], c + 2)
                    for j in range(tiles):
                        last = V.scalar_tensor_tensor(conv[:, j, :], gate_ps[j][:, 0:D], dis[:, bass.ds(c * CT + j, 1)], grow[:, l, 0, :], ALU.mult, ALU.add)
                    last.then_inc(conv_taken[l], 1)
                    v.wait_ge(conv_taken[l], c + 2)
                    go(V.memset(safe[:, 0:tiles, :], 0.0))
                    link(V.tensor_tensor(conv_d[:, 0:tiles, :], conv[:, 0:tiles, :], conv[:, 0:tiles, :], ALU.subtract))
                    link(V.tensor_scalar(fin_mask[:, 0:tiles, :], conv_d[:, 0:tiles, :], 0.0, None, ALU.is_equal))
                    hold(v)
                    link(V.copy_predicated(safe[:, 0:tiles, :], fin_mask[:, 0:tiles, :], conv[:, 0:tiles, :]))
                    for j in range(tiles):
                        last = V.bn_stats(stats[:, j, :], safe[:, j, :])
                    link(last)
                    moments(tiles).then_inc(cvar[l], 1)
                    v.wait_ge(cstd[l], c + 1)
                    link(V.reciprocal(rstd[:, 0:tiles], std[:, 0:tiles]))
                    for j in range(tiles):
                        last = V.tensor_scalar(normed[:, j, :], safe[:, j, :], mean[:, j:j + 1], rstd[:, j:j + 1], ALU.subtract, ALU.mult)
                    link(last)
                    link(V.tensor_tensor(normed[:, 0:tiles, :], normed[:, 0:tiles, :], rows(1), ALU.mult))
                    link(V.tensor_tensor(normed[:, 0:tiles, :], normed[:, 0:tiles, :], rows(2), ALU.add))
                    last = V.scalar_tensor_tensor(at(res), normed[:, 0:tiles, :], 0.0, at(res), ALU.max, ALU.add)
                    if l == 0:
                        link(last)
                        for j in range(tiles):
                            last = V.tensor_scalar(nat2[:, bass.ds(c * CT + j, 1), :].rearrange("p a f -> p (a f)"), res[:, bass.ds(c * CT + j, 1), :].rearrange("p a f -> p (a f)"), dis[:, bass.ds(c * CT + j, 1)], None, ALU.mult)
                    last.then_inc(chunk_done[l], 1)

                with ch.loop(0, NC, 16 if l == 0 else 15) as c:
                    finish(c, CT)
                finish(NC, TW // 128)

            v.wait_ge(chunk_done[1], CH)
            v.wait_ge(x_in, 64)
            link(V.tensor_tensor(res[:, :, :], res[:, :, :], nat[:, :, :], ALU.add))
            layernorm(nat, res)
            v.sem_inc(nat_ready, 1)
            layernorm(nat2, nat)
            v.sem_inc(nat_ready, 1)

            v.wait_ge(logits_done, 1)
            v.wait_ge(moe_in, 16 * 6)
            wide = lambda x: x[:, :].rearrange("p (t a) -> p t a", a=1).to_broadcast([128, NT, X0])
            pos = row[:, 0:X0].rearrange("p (a e) -> p a e", a=1).to_broadcast([128, NT, X0])
            link(V.tensor_tensor(lg[:, :, :], bank[0][:, 0:NT * X0].rearrange("p (t e) -> p t e", e=X0), ebr[:, :].rearrange("p (a e) -> p a e", a=1).to_broadcast([128, NT, X0]), ALU.add))
            link(V.reduce_max(m1[:, :], lg[:, :, :], AX))
            V.tensor_tensor(t8[:, :, :], lg[:, :, :], wide(m1), ALU.subtract).then_inc(lmax, 1)
            v.wait_ge(lexp, 1)

            def first_of_max(hit, probs, best):
                link(V.reduce_max(best[:, :], probs[:, :, :], AX))
                link(V.tensor_tensor(u8[:, :, :], probs[:, :, :], wide(best), ALU.is_lt))
                link(V.scalar_tensor_tensor(u8[:, :, :], u8[:, :, :], 16.0, pos, ALU.mult, ALU.add))
                link(V.tensor_reduce(ix[:, :], u8[:, :, :], AX, ALU.min))
                link(V.tensor_tensor(hit[:, :, :], u8[:, :, :], wide(ix), ALU.is_equal))

            first_of_max(oh1, pr, m1)
            link(V.scalar_tensor_tensor(t8[:, :, :], oh1[:, :, :], -4.0, pr[:, :, :], ALU.mult, ALU.add))
            first_of_max(oh2, t8, m2)
            link(V.tensor_tensor(q1[:, :], m1[:, :], m2[:, :], ALU.add))
            link(V.reciprocal(q1[:, :], q1[:, :]))
            go(V.tensor_tensor(q2[:, :], m2[:, :], q1[:, :], ALU.mult))
            link(V.tensor_tensor(ix[:, :], m1[:, :], q1[:, :], ALU.mult))
            go(V.tensor_tensor(u8[:, :, :], oh2[:, :, :], wide(q2), ALU.mult))
            link(V.tensor_tensor(wd[:, :, :], oh1[:, :, :], wide(ix), ALU.mult))
            link(V.tensor_tensor(wd[:, :, :], wd[:, :, :], u8[:, :, :], ALU.add))
            v.sem_inc(wd_ready, 1)
            for t in range(NT):
                v.wait_ge(b2_done, t + 1)
                V.tensor_tensor(res[:, t, :], res[:, t, :], gate_ps[t % 4][:, 0:D], ALU.add).then_inc(b2_taken, 1)
            v.wait_ge(b2_taken, NT)
            v.wait_ge(tr_out, 2 * NT)

            v.sem_inc(y_taken, 1)

            def scale_in(n, e, c, width):
                if n is not None:
                    v.wait_ge(hid_ps, 8 * n)
                for k in range(KD):
                    last = V.tensor_scalar(xe[:, k, 0:width], xT[:, k, bass.ds(c * CW, width)],
                                           eg[:, k, bass.ds(e, 1)], eb[:, k, bass.ds(e, 1)], ALU.mult, ALU.add)
                last.then_inc(xe_ready, 1)

            def add_in(n, e, c, width):
                v.wait_ge(y_done, n + 2)
                for j in range(width // 128):
                    t = c * CT + j
                    at = res[:, bass.ds(t, 1), :].rearrange("p a f -> p (a f)")
                    last = V.scalar_tensor_tensor(at, y_ps[j][:, 0:D], wd[:, bass.ds(t, 1), bass.ds(e, 1)].rearrange("p a b -> p (a b)"), at, ALU.mult, ALU.add)
                last.then_inc(y_taken, 1)

            y_ps = [bank[0], bank[1], bank[6], bank[7]]
            go(V.memset(eg[:, :, X0:X0 + 1], 0.0))
            link(V.memset(eb[:, :, X0:X0 + 1], 0.0))
            scale_in(None, 0, 0, CW)
            with v.Fori(0, X0) as e:
                with v.Fori(0, NC - 1) as c:
                    n = CH * e + c
                    scale_in(n + 1, e, c + 1, CW)
                    add_in(n, e, c, CW)
                n = CH * e + NC - 1
                scale_in(n + 1, e, NC, TW)
                add_in(n, e, NC - 1, CW)
                scale_in(n + 2, e + 1, 0, CW)
                add_in(n + 1, e, NC, TW)
            v.wait_ge(y_taken, X0 * CH + 1)
            layernorm(nat, res)
            v.sem_inc(nat_ready, 1)

            v.wait_ge(gru_in, 16 * (4 + LAYERS))
            V.tensor_tensor(brz[:, :], bih[:, 0:4], bhh[:, 0:4], ALU.add).then_inc(g_dve, 1)
            v.wait_ge(g_dve, 1)
            v.sem_inc(g_new, 1)

            def gru(i, c, width):
                q = CH * i + c
                for j in range(KD):
                    v.wait_ge(g_act, 2 * q + j + 2)
                    link(V.scalar_tensor_tensor(ga[:, j, 0:width], gate_ps[3][:, 0:width], bhh[:, 2 * KD + j:2 * KD + j + 1], gr[:, j, 0:width], ALU.add, ALU.mult))
                    V.tensor_tensor(gb[:, j, 0:width], gate_ps[2][:, 0:width], ga[:, j, 0:width], ALU.add).then_inc(g_dve, 1)
                at = xT[:, :, bass.ds(c * CW, width)]
                v.wait_ge(g_tanh, 2 * q + 2)
                link(V.tensor_tensor(ga[:, :, 0:width], at, gn[:, :, 0:width], ALU.subtract))
                link(V.tensor_tensor(ga[:, :, 0:width], ga[:, :, 0:width], gz[:, :, 0:width], ALU.mult))
                V.tensor_tensor(at, ga[:, :, 0:width], gn[:, :, 0:width], ALU.add).then_inc(g_new, 1)

            with ch.loop(0, LAYERS, 4 * CH) as i:
                with ch.loop(0, NC, 4) as c:
                    gru(i, c, CW)
                gru(i, NC, TW)
            v.wait_ge(back_out, NT * (LAYERS + 1) + 2)
            link(V.tensor_tensor(res[:, :, :], res[:, :, :], nat[:, :, :], ALU.add))
            layernorm(nat, res)
            v.sem_inc(nat_ready, 1)

            v.wait_ge(f_mean, 1)
            V.tensor_scalar(fmean[:, :], bank[0][:, 0:KD], 1.0 / N, None, ALU.mult).then_inc(f_meanT, 1)
            v.wait_ge(f_lg, 1)
            v.wait_ge(f_in, 64)
            one = lambda x: x[0:1, 0:1]
            link(V.tensor_tensor(r8[2][:, :], bank[1][0:1, 0:X0], fbr[:, :], ALU.add))
            link(V.reduce_max(r1[0][:, :], r8[2][:, :], AX))
            V.tensor_scalar(r8[0][:, :], r8[2][:, :], one(r1[0]), None, ALU.subtract).then_inc(f_e, 1)
            v.wait_ge(f_a, 1)
            link(V.reciprocal(r1[2][:, :], r1[1][:, :]))
            link(V.tensor_scalar(r8[2][:, :], r8[1][:, :], one(r1[2]), None, ALU.mult))
            link(V.tensor_scalar(r8[3][:, :], r8[2][:, :], float(N), None, ALU.mult))
            link(V.tensor_scalar(r8[4][:, :], r8[3][:, :], CAPACITY, None, ALU.max))
            link(V.reciprocal(r8[4][:, :], r8[4][:, :]))
            link(V.tensor_scalar(r8[4][:, :], r8[4][:, :], CAPACITY, None, ALU.mult))
            link(V.tensor_scalar(r8[7][:, :], r8[3][:, :], CAPACITY, None, ALU.is_gt))
            link(V.tensor_scalar(r8[4][:, :], r8[4][:, :], 1.0, None, ALU.subtract))
            link(V.tensor_tensor(r8[4][:, :], r8[4][:, :], r8[7][:, :], ALU.mult))
            link(V.scalar_tensor_tensor(r8[2][:, :], r8[4][:, :], 1.0, r8[2][:, :], ALU.add, ALU.mult))
            link(V.reduce_max(r1[0][:, :], r8[2][:, :], AX))
            V.tensor_scalar(r8[5][:, :], r8[2][:, :], one(r1[0]), None, ALU.subtract).then_inc(f_e, 1)
            v.wait_ge(f_a, 2)
            link(V.reciprocal(r1[2][:, :], r1[3][:, :]))
            link(V.tensor_scalar(r8[3][:, :], r8[6][:, :], one(r1[2]), None, ALU.mult))
            link(V.max(top[:, :], r8[3][:, :]))
            link(V.max_index(topi[:, :], top[:, :], r8[3][:, :]))
            V.tensor_scalar(te[:, :], top[:, 0:2], one(top), None, ALU.subtract).then_inc(f_e, 1)
            v.wait_ge(f_a, 3)
            link(V.reciprocal(r1[5][:, :], r1[4][:, :]))
            V.tensor_scalar(tw[:, :], te[:, :], one(r1[5]), None, ALU.mult).then_inc(f_top, 1)
            v.wait_ge(f_twb, 1)
            link(V.tensor_copy(twb[:, :], bank[1][:, 16:18]))
            v.wait_ge(fw_in, 16 * 8)
            for k in range(2):
                go(V.tensor_scalar(fw2s[:, k, :, :], fw2[:, k, :, :], twb[:, k:k + 1], None, ALU.mult))
            link(V.tensor_scalar(fmix[:, :], fb2[:, 0, :], twb[:, 0:1], None, ALU.mult))
            link(V.scalar_tensor_tensor(fmix[:, :], fb2[:, 1, :], twb[:, 1:2], fmix[:, :], ALU.mult, ALU.add))
            v.sem_inc(fw_rdy, 1)
            v.sem_inc(fy_taken, 1)

            def second(c, tiles):
                at = lambda x: x[:, bass.ds(c * CT, tiles), :]
                v.wait_ge(fy, c + 2)
                for j in range(tiles):
                    last = V.tensor_tensor(fo[:, j, :], y_ps[j][:, 0:D], fmix[:, :], ALU.add)
                last.then_inc(fy_taken, 1)
                v.wait_ge(fy_taken, c + 2)
                link(V.tensor_tensor(fo[:, 0:tiles, :], fo[:, 0:tiles, :], at(nat), ALU.add))
                for j in range(tiles):
                    last = V.bn_stats(stats[:, j, :], fo[:, j, :])
                link(last)
                moments(tiles).then_inc(fvar, 1)
                v.wait_ge(fstd, c + 1)
                link(V.reciprocal(rstd[:, 0:tiles], std[:, 0:tiles]))
                for j in range(tiles):
                    last = V.tensor_scalar(fn[:, j, :], fo[:, j, :], mean[:, j:j + 1], rstd[:, j:j + 1], ALU.subtract, ALU.mult)
                link(last)
                rows = lambda m: fgb[:, m:m + 1, :].to_broadcast([128, tiles, D])
                link(V.tensor_tensor(fn[:, 0:tiles, :], fn[:, 0:tiles, :], rows(0), ALU.mult))
                link(V.tensor_tensor(fn[:, 0:tiles, :], fn[:, 0:tiles, :], rows(1), ALU.add))
                V.tensor_tensor(at(res), at(res), fn[:, 0:tiles, :], ALU.add).then_inc(o_ready, 1)

            with ch.loop(0, NC, 12) as c:
                second(c, CT)
            second(NC, TW // 128)


_INS = ['x', 'src', 'dst', 'edge_weight', 'L0_gnn_W1', 'L0_gnn_b1', 'L0_gnn_ln_g1', 'L0_gnn_ln_b1', 'L0_gnn_W2', 'L0_gnn_b2', 'L0_gnn_ln_g2', 'L0_gnn_ln_b2',
        'L0_ffn_Wr', 'L0_ffn_br', 'L0_ffn_W1', 'L0_ffn_W2', 'L0_ffn_b2', 
        'L1_ffn_Wr', 'L1_ffn_br', 'L1_ffn_W1', 'L1_ffn_W2', 'L1_ffn_b2', 'L1_ffn_gamma', 'L1_ffn_beta']


def kernel(**inputs):
    import numpy as _np
    import concourse.bacc as _bacc
    from concourse import mybir as _mybir
    from concourse.bass_utils import run_bass_kernel_spmd as _run

    nc = _bacc.Bacc("TRN2", target_bir_lowering=False, num_devices=1)
    laid = {name: _np.ascontiguousarray(inputs[name]) for name in _INS}
    tall = lambda v, rows: _np.ascontiguousarray(_np.transpose(_np.reshape(v, (rows, -1, 128)), (0, 2, 1)))
    laid["L0_ffn_ln_gT"] = _np.ascontiguousarray(_np.transpose(inputs["L0_ffn_ln_g"]))
    laid["L0_ffn_ln_bT"] = _np.ascontiguousarray(_np.transpose(inputs["L0_ffn_ln_b"]))
    laid["L0_ffn_b1T"] = _np.ascontiguousarray(_np.transpose(_np.reshape(inputs["L0_ffn_b1"], (-1, 128))))
    laid["L1_gnn_b_ihT"] = tall(inputs["L1_gnn_b_ih"], 1)[0]
    laid["L1_gnn_b_hhT"] = tall(inputs["L1_gnn_b_hh"], 1)[0]
    laid["L1_ffn_b1T"] = _np.reshape(tall(inputs["L1_ffn_b1"], X0), (X0 * 128, F1 // 128))
    laid["L1_gnn_weightT"] = _np.ascontiguousarray(_np.transpose(inputs["L1_gnn_weight"], (0, 2, 1)))
    laid["L1_gnn_w_ihT"] = _np.ascontiguousarray(_np.transpose(inputs["L1_gnn_w_ih"]))
    laid["L1_gnn_w_hhT"] = _np.ascontiguousarray(_np.transpose(inputs["L1_gnn_w_hh"]))
    aps = {name: nc.dram_tensor(f"in_{name}", v.shape, _mybir.dt.from_np(v.dtype), kind="ExternalInput").ap() for name, v in laid.items()}
    out = nc.dram_tensor("out_0", (N, D), _mybir.dt.from_np(_np.dtype("float32")), kind="ExternalOutput").ap()
    build(nc, aps, out)
    return _run(nc, [{f"in_{name}": v for name, v in laid.items()}], core_ids=[0]).results[0]["out_0"]
```

```python
import math

import concourse.bass as bass
from concourse import mybir
from contextlib import ExitStack, contextmanager

FP32 = mybir.dt.float32
BF16 = mybir.dt.bfloat16
I32 = mybir.dt.int32
U32 = mybir.dt.uint32
ALU = mybir.AluOpType
ACT = mybir.ActivationFunctionType
AX = mybir.AxisListType.X

N = 3125
D = 256
KD = D // 128
E = 50000
NT = -(-N // 128)
NP = NT * 128
EP = 125
ET = E // EP
G = 4
KB = 4
CW = 512
CT = CW // 128
NC = NP // CW
TW = NP - NC * CW
CH = NC + 1
RB = 5
RR = NT // RB
X0, H0 = 8, 1024
ST = 2 * NT + X0 - 1
F1 = 512
LAYERS = 5
EPS = 1e-5
FLT_MAX = 3.4028234663852886e38
CAPACITY = float(math.ceil(N * 1.25 / X0))


class Count:

    def __init__(self, eng, sem):
        self.eng, self.sem, self.base, self.k = eng, sem, 0, 0

    def go(self, ins):
        self.k += 1
        ins.then_inc(self.sem, 1)

    def link(self, ins):
        self.go(ins)
        self.eng.wait_ge(self.sem, self.base + self.k)

    @contextmanager
    def loop(self, start, end, steps):
        base, k = self.base, self.k
        with self.eng.Fori(start, end) as i:
            self.base, self.k = base + i * steps + k - start * steps, 0
            yield i
            assert self.k == steps, (self.k, steps)
        self.base, self.k = base, k + steps * (end - start)


def build(nc, a, out):
    adj = nc.dram_tensor("adj", [NP * NP + NP, 2], FP32).ap()
    adj_sd = adj[0:NP * NP, :].rearrange("(s d) k -> s d k", d=NP)
    adj_w = nc.dram_tensor("adj_w", [NP, NP], FP32).ap()
    slots_x = nc.dram_tensor("slots_x", [ST * 128, D], FP32).ap()
    slots_y = nc.dram_tensor("slots_y", [ST * 128, D], FP32).ap()
    key_rows = nc.dram_tensor("key_rows", [ET, EP], FP32).ap()

    ctx = ExitStack()
    with ctx:
        scope = [ctx]

        def sb(n, s, d=FP32):
            return scope[-1].enter_context(nc.sbuf_tensor(n, s, d))

        def sem(n):
            return ctx.enter_context(nc.semaphore(n))

        bank = [ctx.enter_context(nc.psum_tensor(f"bank{n}", [128, 512], FP32)) for n in range(8)]
        agg_ps, gate_ps, tr_ps = bank[0:2], bank[2:6], bank[6:8]

        ident = sb("ident", [128, 128])
        row = sb("row", [128, 128])
        below = sb("below", [128, 128])
        ones = sb("ones", [128, 128])
        dis = sb("dis", [128, NT])
        stats = sb("stats", [128, NT, 6])
        st_sum = sb("st_sum", [128, NT]); st_dif = sb("st_dif", [128, NT]); st_m2 = sb("st_m2", [128, NT]); st_sq = sb("st_sq", [128, NT])
        mean = sb("mean", [128, NT]); var = sb("var", [128, NT]); std = sb("std", [128, NT]); rstd = sb("rstd", [128, NT])
        res = sb("res", [128, NT, D])
        nat = sb("nat", [128, NT, D])
        nat2 = sb("nat2", [128, NT, D])
        scope.append(ExitStack())
        zeros = sb("zeros", [128, 2 * NP])
        srci = sb("srci", [EP, ET], I32); dsti = sb("dsti", [EP, ET], I32); w = sb("w", [EP, ET])
        wabs = sb("wabs", [EP, ET]); wbits = sb("wbits", [EP, ET]); finite = sb("finite", [EP, ET], U32)
        srcf = sb("srcf", [EP, ET]); dstf = sb("dstf", [EP, ET]); key = sb("key", [EP, ET])
        lo_i = sb("lo_i", [EP, ET], I32); hi_i = sb("hi_i", [EP, ET], I32)
        dlo = sb("dlo", [EP, ET]); dhi = sb("dhi", [EP, ET])
        spare_i = sb("spare_i", [EP, ET], I32); to_spare = sb("to_spare", [EP, ET]); rest = sb("rest", [EP, ET])
        parts0 = sb("parts0", [EP, ET, 8], BF16); parts1 = sb("parts1", [EP, ET, 8], BF16)
        before = sb("before", [EP, EP])
        keyT = sb("keyT", [100, 4, EP])
        keyrow = sb("keyrow", [EP, KB, G * EP])
        eq = sb("eq", [EP, 2, G, G * EP], BF16)
        hit_lo = sb("hit_lo", [EP, 2, G, 128]); hit_hi = sb("hit_hi", [EP, 2, G, NT])
        own = sb("own", [EP, 2, G, EP], BF16); own_n = sb("own_n", [EP, 2, G])
        sums = sb("sums", [EP, 2, G, 8]); half = sb("half", [EP, 2, G, 2]); pair = sb("pair", [EP, 2, G, 2])
        earlier = sb("earlier", [EP, 2, G]); shift = sb("shift", [EP, 2, G]); slot = sb("slot", [EP, 2, G], U32)
        scope.pop().close()
        xT = sb("xT", [128, KD, NP])
        scope.append(ExitStack())
        ring2 = sb("ring2", [128, RB, CW, 2])
        stage = sb("stage", [128, RB, CW])
        aggT = sb("aggT", [128, KD, CW])
        gw = sb("gw", [128, 2, KD, D])
        grow = sb("grow", [128, 2, 3, D])
        conv = sb("conv", [128, CT, D]); conv_d = sb("conv_d", [128, CT, D]); fin_mask = sb("fin_mask", [128, CT, D], U32)
        safe = sb("safe", [128, CT, D]); normed = sb("normed", [128, CT, D])
        scope.pop().close()
        scope.append(ExitStack())
        w1 = sb("w1", [128, 2, KD, H0]); w2 = sb("w2", [128, 2, H0 // 128, D])
        erow = sb("erow", [128, 2, H0 + D])
        xtile = sb("xtile", [128, D]); xe = sb("xe", [128, KD, 128])
        hb = sb("hb", [128, H0]); hg = sb("hg", [128, H0]); hT = sb("hT", [128, H0 // 128, 128]); ytile = sb("ytile", [128, D])
        yg = sb("yg", [128, 4, 2, D]); acc = sb("acc", [128, 2, D])
        ewr = sb("ewr", [128, KD, X0]); ebr = sb("ebr", [128, X0])
        eg = sb("eg", [128, KD, X0]); eb = sb("eb", [128, KD, X0])
        lg = sb("lg", [128, NT, X0]); pr = sb("pr", [128, NT, X0]); t8 = sb("t8", [128, NT, X0]); u8 = sb("u8", [128, NT, X0])
        oh1 = sb("oh1", [128, NT, X0]); oh2 = sb("oh2", [128, NT, X0]); both = sb("both", [128, NT, X0])
        pre = [sb(f"pre{n}", [128, NT, X0]) for n in range(2)]; rank = sb("rank", [128, NT, X0]); tot = sb("tot", [128, NT, X0])
        nf = sb("nf", [128, X0]); ni = sb("ni", [128, X0], I32); ns = sb("ns", [128, X0]); first = [sb(f"first{n}", [128, X0 + 1]) for n in range(2)]
        first_i = sb("first_i", [1, X0 + 1], I32); of_t = sb("of_t", [1, ST, X0]); of_f = sb("of_f", [1, ST])
        of_i = sb("of_i", [1, ST], I32); par_i = sb("par_i", [1, ST], I32)
        slot_f = sb("slot_f", [128, 2, NT]); slot_u = sb("slot_u", [128, 2, NT], U32)
        wt = sb("wt", [128, NT]); m1 = sb("m1", [128, NT]); m2 = sb("m2", [128, NT]); ix = sb("ix", [128, NT]); q1 = sb("q1", [128, NT]); q2 = sb("q2", [128, NT])
        scope.pop().close()
        scope.append(ExitStack())
        ringw = sb("ringw", [128, RB, RB, CW])
        gT = sb("gT", [128, KD, CW])
        spare = nat2[:, :, :].rearrange("p t f -> p (t f)")
        wt_sb = spare[:, 0:LAYERS * KD * D].rearrange("p (i k f) -> p i k f", i=LAYERS, k=KD)
        wih = sb("wih", [128, KD, 3 * D]); whh = sb("whh", [128, KD, 3 * D])
        v_all = sb("v_all", [128, LAYERS, KD, 3 * D]); v_now = sb("v_now", [128, KD, 3 * D])
        bih = sb("bih", [128, 6]); bhh = sb("bhh", [128, 6]); brz = sb("brz", [128, 4])
        gr, gz, gn, ga, gb = (spare[:, n * KD * CW:(n + 1) * KD * CW].rearrange("p (k c) -> p k c", k=KD) for n in range(5))
        scope.pop().close()
        scope.append(ExitStack())
        fw1 = sb("fw1", [128, 2, KD, F1]); fw2 = sb("fw2", [128, 2, F1 // 128, D]); fw2s = sb("fw2s", [128, 2, F1 // 128, D])
        fb1 = sb("fb1", [128, 2, F1 // 128]); fb2 = sb("fb2", [128, 2, D]); fmix = sb("fmix", [128, D])
        fwr = sb("fwr", [128, KD, X0]); fbr = sb("fbr", [1, X0]); fgb = sb("fgb", [128, 2, D])
        fhid = sb("fhid", [128, 2, F1 // 128, CW])
        fmean = sb("fmean", [128, KD]); r8 = [sb(f"r8_{n}", [1, X0]) for n in range(8)]; r1 = [sb(f"r1_{n}", [1, 1]) for n in range(6)]
        top = sb("top", [1, 8]); topi = sb("topi", [1, 8], U32); tw = sb("tw", [1, 2]); te = sb("te", [1, 2]); twb = sb("twb", [128, 2])
        fo = sb("fo", [128, CT, D]); fn = sb("fn", [128, CT, D])
        scope.pop().close()

        consts = sem("consts"); edges_in = sem("edges_in"); x_in = sem("x_in")
        zeroed = sem("zeroed"); diag_in = sem("diag_in"); dve_n = sem("dve_n")
        key_done = sem("key_done"); keyT_ps = sem("keyT_ps"); keyT_sb = sem("keyT_sb"); keyT_out = sem("keyT_out")
        keyrow_in = [sem(f"keyrow_in{b}") for b in range(KB)]
        compared = sem("compared"); summed = sem("summed"); sums_out = sem("sums_out"); placed = sem("placed")
        turn = sem("turn"); scattered = sem("scattered"); deg_done = sem("deg_done")
        var_ready = sem("var_ready"); std_ready = sem("std_ready")
        gcn_in = sem("gcn_in")
        hs_ready = sem("hs_ready"); chunk_done = [sem(f"chunk_done{l}") for l in range(2)]
        ring_in = [[sem(f"ring_in{l}_{b}") for b in range(RB)] for l in range(2)]
        used = [sem(f"used{l}") for l in range(2)]
        planes = sem("planes"); staged = sem("staged")
        aggT_rdy = [sem(f"aggT_rdy{l}") for l in range(2)]
        projd = [sem(f"projd{l}") for l in range(2)]; conv_taken = [sem(f"conv_taken{l}") for l in range(2)]
        cvar = [sem(f"cvar{l}") for l in range(2)]; cstd = [sem(f"cstd{l}") for l in range(2)]
        nat_ready = sem("nat_ready"); tr_done = sem("tr_done"); tr_out = sem("tr_out"); logits_done = sem("logits_done")
        moe_in = sem("moe_in"); lmax = sem("lmax"); lexp = sem("lexp"); counted = sem("counted"); ranked = sem("ranked"); xs_zeroed = sem("xs_zeroed"); slots_ready = sem("slots_ready"); x_sorted = sem("x_sorted")
        w_in = [sem(f"w_in{b}") for b in range(2)]; w_ready = sem("w_ready")
        xt_in = sem("xt_in"); x_turned = sem("x_turned"); xe_rdy = sem("xe_rdy"); h_ps = sem("h_ps"); hb_rdy = sem("hb_rdy"); hg_rdy = sem("hg_rdy")
        hT_ps = sem("hT_ps"); hT_act = sem("hT_act"); hT_dve = sem("hT_dve"); y_ps_rdy = sem("y_ps_rdy"); y_rdy = sem("y_rdy"); y_out = sem("y_out")
        y_got = [sem(f"y_got{b}") for b in range(4)]; y_free = sem("y_free"); moe_done = sem("moe_done")
        gru_in = sem("gru_in"); v_ps = sem("v_ps"); v_out = sem("v_out"); v_set = sem("v_set")
        rw_in = [sem(f"rw_in{b}") for b in range(RB)]; rw_used = sem("rw_used")
        gT_rdy = sem("gT_rdy"); gates = sem("gates"); g_act = sem("g_act"); g_dve = sem("g_dve"); g_tanh = sem("g_tanh"); g_new = sem("g_new"); back_ps = sem("back_ps"); back_out = sem("back_out")
        f_in = sem("f_in"); f_mean = sem("f_mean"); f_meanT = sem("f_meanT"); f_lg = sem("f_lg"); f_e = sem("f_e"); f_a = sem("f_a"); f_top = sem("f_top"); f_twb = sem("f_twb"); fw_in = sem("fw_in"); fw_rdy = sem("fw_rdy")
        fh_ps = sem("fh_ps"); fh_rdy = sem("fh_rdy"); fy = sem("fy"); fy_taken = sem("fy_taken"); fvar = sem("fvar"); fstd = sem("fstd"); o_ready = sem("o_ready"); stored = sem("stored")

        held = sem("held")

        def hold(eng):
            eng.sem_inc(held, 1)

        block = ctx.enter_context(nc.Block())
        x_tiles = a["x"][0:(NT - 1) * 128, :].rearrange("(t p) f -> p t f", p=128)
        LAST = N - (NT - 1) * 128

        def bcast(v, rows=128):
            return v.rearrange("(a n) -> a n", a=1).to_broadcast([rows, v.shape[0]])

        @block.sync
        def _(sp):
            e = lambda v: v.rearrange("(p t) -> p t", p=EP)
            sp.dma_start(srci[:, :], e(a["src"])).then_inc(edges_in, 16)
            sp.dma_start(dsti[:, :], e(a["dst"])).then_inc(edges_in, 16)
            sp.dma_start(w[:, :], e(a["edge_weight"])).then_inc(edges_in, 16)
            sp.wait_ge(consts, 1)
            sp.dma_start(res[:, 0:NT - 1, :], x_tiles).then_inc(x_in, 16)
            sp.dma_start(res[0:LAST, NT - 1, :], a["x"][(NT - 1) * 128:N, :]).then_inc(x_in, 16)
            sp.wait_ge(consts, 2)
            for t in range(NT):
                sp.dma_start(adj[t * 128 * NP:(t + 1) * 128 * NP, :].rearrange("(p c) k -> p (c k)", p=128), zeros[:, :]).then_inc(zeroed, 16)
            sp.dma_start(adj[NP * NP:NP * NP + NP, :].rearrange("(p c) k -> p (c k)", p=128), zeros[:, 0:2 * NT]).then_inc(zeroed, 16)
            for t in range(3):
                sp.dma_start(slots_x[t * (ST // 3) * 128:(t + 1) * (ST // 3) * 128, :].rearrange("(p c) f -> p (c f)", p=128), zeros[:, 0:ST // 3 * D]).then_inc(xs_zeroed, 16)
            sp.wait_ge(zeroed, 16 * (NT + 1))
            sp.wait_ge(consts, 3)
            with nc.allow_non_contiguous_dma(reason="the diagonal"):
                sp.dma_start(bass.AP(tensor=adj.tensor, offset=1, ap=[[2 * (NP + 1) * NT, 128], [2 * (NP + 1), NT], [1, 1]]),
                             ones[:, 0:NT].rearrange("p (a b) -> p a b", b=1)).then_inc(diag_in, 16)
            sp.wait_ge(keyT_sb, 1)
            sp.dma_start(key_rows.rearrange("(c t) p -> t c p", c=4), keyT[:, :, :]).then_inc(keyT_out, 16)
            sp.wait_ge(keyT_out, 16)
            flat = key_rows.rearrange("t p -> (t p)").rearrange("(a n) -> a n", a=1)
            with sp.Fori(0, ET // G // KB) as i:
                for b in range(KB):
                    sp.wait_ge(compared, KB * i + b + 1)
                    hold(sp)
                    sp.dma_start(keyrow[:, b, :], flat[:, bass.ds((KB * i + b) * G * EP, G * EP)].to_broadcast([EP, G * EP])).then_inc(keyrow_in[b], 16)
            sp.wait_ge(scattered, 16 * ET)
            sp.wait_ge(hs_ready, 1)
            for l in range(2):
                k = l + 1
                sp.dma_start(gw[:, l, :, :], a[f"L0_gnn_W{k}"].rearrange("(k p) f -> p k f", p=128)).then_inc(gcn_in, 16)
                for m, n in enumerate((f"L0_gnn_b{k}", f"L0_gnn_ln_g{k}", f"L0_gnn_ln_b{k}")):
                    sp.dma_start(grow[:, l, m, :], bcast(a[n])).then_inc(gcn_in, 16)

            def load2(l, c, width, r, b):
                n = NT * c + RB * r + b
                sp.wait_ge(used[l], n + 1)
                if l == 0:
                    sp.wait_ge(planes, n + 1)
                hold(sp)
                t = RB * r + b
                sp.dma_start(ring2[:, b, 0:width, :], adj_sd[t * 128:(t + 1) * 128, bass.ds(c * CW, width), :]).then_inc(ring_in[l][b], 16)

            def store_plane(c, width, r):
                sp.wait_ge(planes, NT * c + RB * r + 2 * RB)
                hold(sp)
                sp.dma_start(adj_w[RB * r * 128:RB * (r + 1) * 128, bass.ds(c * CW, width)].rearrange("(b p) d -> p b d", p=128),
                             stage[:, :, 0:width]).then_inc(staged, 16)

            def loads2(l, c, width):
                for r in range(RR):
                    for b in range(RB):
                        load2(l, c, width, r, b)
                    if l == 0 and r:
                        store_plane(c, width, r - 1)
                if l == 0:
                    store_plane(c, width, RR - 1)

            sp.sem_inc(staged, 16)
            for l in range(2):
                with sp.Fori(0, NC) as c:
                    loads2(l, c, CW)
                loads2(l, NC, TW)
            sp.wait_ge(used[0], NT * CH + RB)
            sp.dma_start(nat[:, 0:NT - 1, :], x_tiles).then_inc(x_in, 16)
            sp.dma_start(nat[0:LAST, NT - 1, :], a["x"][(NT - 1) * 128:N, :]).then_inc(x_in, 16)
            sp.wait_ge(chunk_done[1], CH)
            sp.dma_start(ewr[:, :, :], a["L0_ffn_Wr"].rearrange("(k p) e -> p k e", p=128)).then_inc(moe_in, 16)
            sp.dma_start(ebr[:, :], bcast(a["L0_ffn_br"])).then_inc(moe_in, 16)
            sp.dma_start(eg[:, :, 0:X0], a["L0_ffn_ln_gT"].rearrange("(k p) e -> p k e", p=128)).then_inc(moe_in, 16)
            sp.dma_start(eb[:, :, 0:X0], a["L0_ffn_ln_bT"].rearrange("(k p) e -> p k e", p=128)).then_inc(moe_in, 16)
            sp.wait_ge(x_sorted, 16 * 2 * NT)
            sp.wait_ge(xs_zeroed, 48)
            def load_tokens(i):
                hold(sp)
                sp.dma_start(xtile[:, :], slots_x[bass.ds(i * 128, 128), :]).then_inc(xt_in, 16)

            def store_result(i):
                sp.wait_ge(y_rdy, i + 2)
                hold(sp)
                sp.dma_start(slots_y[bass.ds(i * 128, 128), :], ytile[:, :]).then_inc(y_out, 16)

            sp.sem_inc(y_out, 16)
            load_tokens(0)
            sp.wait_ge(x_turned, 1)
            load_tokens(1)
            with sp.Fori(1, ST - 1) as i:
                sp.wait_ge(x_turned, i + 1)
                load_tokens(i + 1)
                store_result(i - 1)
            store_result(ST - 2)
            store_result(ST - 1)
            sp.wait_ge(moe_done, 1)
            sp.dma_start(wih[:, :, :], a["L1_gnn_w_ihT"].rearrange("(k p) g -> p k g", p=128)).then_inc(gru_in, 16)
            sp.dma_start(whh[:, :, :], a["L1_gnn_w_hhT"].rearrange("(k p) g -> p k g", p=128)).then_inc(gru_in, 16)
            for i in range(LAYERS):
                sp.dma_start(wt_sb[:, i, :, :], a["L1_gnn_weightT"][i, :, :].rearrange("(k p) f -> p k f", p=128)).then_inc(gru_in, 16)
            sp.dma_start(bih[:, :], a["L1_gnn_b_ihT"]).then_inc(gru_in, 16)
            sp.dma_start(bhh[:, :], a["L1_gnn_b_hhT"]).then_inc(gru_in, 16)
            sp.wait_ge(staged, 16 * (RR * CH + 1))

            def loadw(i, c, width, r):
                n = RR * (CH * i + c) + r
                sp.wait_ge(rw_used, n + 1)
                hold(sp)
                sp.dma_start(ringw[:, r, :, 0:width], adj_w[RB * r * 128:RB * (r + 1) * 128, bass.ds(c * CW, width)].rearrange("(b p) d -> p b d", p=128)).then_inc(rw_in[r], 16)

            with sp.Fori(0, LAYERS) as i:
                with sp.Fori(0, NC) as c:
                    for r in range(RR):
                        loadw(i, c, CW, r)
                for r in range(RR):
                    loadw(i, NC, TW, r)
            sp.wait_ge(g_new, CH * LAYERS + 1)
            sp.wait_ge(back_out, NT * (LAYERS + 1) + 2)
            sp.dma_start(fwr[:, :, :], a["L1_ffn_Wr"].rearrange("(k p) e -> p k e", p=128)).then_inc(f_in, 16)
            sp.dma_start(fbr[:, :], bcast(a["L1_ffn_br"], 1)).then_inc(f_in, 16)
            sp.dma_start(fgb[:, 0, :], bcast(a["L1_ffn_gamma"])).then_inc(f_in, 16)
            sp.dma_start(fgb[:, 1, :], bcast(a["L1_ffn_beta"])).then_inc(f_in, 16)
            sp.wait_ge(f_top, 1)
            fw1_all = a["L1_ffn_W1"].rearrange("e d f -> (e d) f")
            fw2_all = a["L1_ffn_W2"].rearrange("e f d -> (e f) d")
            for k in range(2):
                x = sp.value_load(topi[0:1, k:k + 1], min_val=0, max_val=X0 - 1)
                sp.dma_start(fw1[:, k, :, :], fw1_all[bass.ds(x * D, D), :].rearrange("(k p) h -> p k h", p=128)).then_inc(fw_in, 16)
                sp.dma_start(fw2[:, k, :, :], fw2_all[bass.ds(x * F1, F1), :].rearrange("(k p) d -> p k d", p=128)).then_inc(fw_in, 16)
                sp.dma_start(fb2[:, k, :], a["L1_ffn_b2"][bass.ds(x, 1), :].to_broadcast([128, D])).then_inc(fw_in, 16)
                sp.dma_start(fb1[:, k, :], a["L1_ffn_b1T"][bass.ds(x * 128, 128), :]).then_inc(fw_in, 16)
            with sp.Fori(0, NC) as c:
                sp.wait_ge(o_ready, c + 1)
                hold(sp)
                sp.dma_start(out[bass.ds(c * CW, CW), :].rearrange("(t p) f -> p t f", p=128), res[:, bass.ds(c * CT, CT), :]).then_inc(stored, 16)
            sp.wait_ge(o_ready, CH)
            sp.dma_start(out[NC * CW:N, :], res[0:LAST, NT - 1, :]).then_inc(stored, 16)
            sp.wait_ge(stored, 16 * CH)

        @block.gpsimd
        def _(pool):
            g_ = nc.gpsimd
            g_.memset(res[:, :, :], 0.0).then_inc(consts, 1)
            g_.memset(zeros[:, :], 0.0).then_inc(consts, 1)
            g_.memset(ones[:, :], 1.0).then_inc(consts, 1)
            g_.memset(ident[:, :], 0.0).then_inc(consts, 1)
            g_.memset(before[:, :], 1.0).then_inc(consts, 1)
            g_.memset(below[:, :], 1.0).then_inc(consts, 1)
            g_.iota(row[:, :], [[1, 128]], base=0, channel_multiplier=0, allow_small_or_imprecise_dtypes=True).then_inc(consts, 1)
            g_.iota(spare_i[:, :], [[0, ET // G], [EP, G]], base=NP * NP, channel_multiplier=1).then_inc(consts, 1)
            pool.wait_ge(consts, 8)
            g_.affine_select(out=ident[:, :], in_=ident[:, :], compare_op=ALU.not_equal, fill=1.0, base=0, pattern=[[-1, 128]], channel_multiplier=1).then_inc(consts, 1)
            g_.affine_select(out=before[:, :], in_=before[:, :], compare_op=ALU.is_gt, fill=0.0, base=0, pattern=[[-1, EP]], channel_multiplier=1).then_inc(consts, 1)
            g_.affine_select(out=below[:, :], in_=below[:, :], compare_op=ALU.is_gt, fill=0.0, base=0, pattern=[[1, 128]], channel_multiplier=-1).then_inc(consts, 1)
            pool.wait_ge(diag_in, 16)
            pool.sem_inc(turn, 1)
            with pool.Fori(0, ET // G // KB) as i:
                for b in range(KB):
                    pool.wait_ge(placed, KB * i + b + 3)
                    pool.sem_inc(turn, 1)
                    for g in range(G):
                        g_.indirect_dma_start(out=adj, out_offset=bass.IndirectOffsetOnAxis(slot[:, b % 2, g:g + 1], 0),
                                              in_=pair[:, b % 2, g, :], in_offset=None, compute_op=ALU.add).then_inc(scattered, 16)
                    pool.wait_ge(scattered, 16 * G * (KB * i + b + 1))

            w1_all = a["L0_ffn_W1"].rearrange("e d h -> (e d) h")
            w2_all = a["L0_ffn_W2"].rearrange("e h d -> (e h) d")

            def load_expert(e, b):
                pool.dma_start(w1[:, b, :, :], w1_all[bass.ds(e * D, D), :].rearrange("(k p) h -> p k h", p=128)).then_inc(w_in[b], 16)
                pool.dma_start(w2[:, b, :, :], w2_all[bass.ds(e * H0, H0), :].rearrange("(k p) d -> p k d", p=128)).then_inc(w_in[b], 16)
                pool.dma_start(erow[:, b, 0:H0], a["L0_ffn_b1"][bass.ds(e, 1), :].to_broadcast([128, H0])).then_inc(w_in[b], 16)
                pool.dma_start(erow[:, b, H0:H0 + D], a["L0_ffn_b2"][bass.ds(e, 1), :].to_broadcast([128, D])).then_inc(w_in[b], 16)

            pool.wait_ge(chunk_done[1], CH)
            for e in range(2):
                load_expert(e, e)
            pool.wait_ge(slots_ready, 1)
            pool.wait_ge(xs_zeroed, 48)
            for k in range(2):
                for t in range(NT):
                    g_.indirect_dma_start(out=slots_x, out_offset=bass.IndirectOffsetOnAxis(slot_u[:, k, t:t + 1], 0),
                                          in_=nat2[:, t, :], in_offset=None).then_inc(x_sorted, 16)
            for e in range(2):
                pool.wait_ge(w_in[e], 64)
                pool.sem_inc(w_ready, 1)
            with pool.Fori(1, X0 // 2) as i:
                for b in range(2):
                    done = pool.value_load(first_i[0:1, bass.ds(2 * i + b - 1, 1)], min_val=1, max_val=ST)
                    pool.wait_ge(y_rdy, done + 1)
                    hold(pool)
                    load_expert(2 * i + b, b)
                    pool.wait_ge(w_in[b], 64 * i + 64)
                    pool.sem_inc(w_ready, 1)
            pool.wait_ge(y_out, 16 * (ST + 1))
            for t in range(NT):
                if t >= 4:
                    pool.wait_ge(y_free, t - 3)
                for k in range(2):
                    g_.indirect_dma_start(out=yg[:, t % 4, k, :], out_offset=None, in_=slots_y,
                                          in_offset=bass.IndirectOffsetOnAxis(slot_u[:, k, t:t + 1], 0)).then_inc(y_got[t % 4], 16)

        @block.tensor
        def _(pe):
            mm, tr = nc.tensor.matmul, nc.tensor.transpose
            ps_sum = [bank[b][0:EP, 0:8 * G].rearrange("p (g k) -> p g k", k=8) for b in range(2)]
            ps_deg = bank[2][:, 0:NT]
            ps_key = bank[3][0:100, 0:4 * EP].rearrange("p (c k) -> p c k", c=4)
            pe.sem_inc(summed, 2)
            pe.wait_ge(consts, 11)
            mm(ps_deg, zeros[0:EP, 0:128], zeros[0:EP, 0:NT], start=True, stop=False)
            pe.wait_ge(key_done, 1)
            for c in range(4):
                last = tr(ps_key[:, c, :], key[:, c * 100:(c + 1) * 100], ident[0:EP, 0:EP])
            last.then_inc(keyT_ps, 1)
            with pe.Fori(0, ET // G // KB) as i:
                for b in range(KB):
                    pe.wait_ge(compared, KB * i + b + 1 + KB)
                    pe.wait_ge(sums_out, KB * i + b + 1)
                    for g in range(G):
                        for q in range(G):
                            parts = (parts1 if q < g else parts0)[:, bass.ds(KB * G * i + G * b + q, 1), :].rearrange("p a k -> p (a k)")
                            mm(ps_sum[b % 2][:, g, :], eq[:, b % 2, q, g * EP:(g + 1) * EP], parts, start=(q == 0), stop=(q == G - 1))
                    for g in range(G):
                        last = mm(ps_deg, hit_lo[:, b % 2, g, :], hit_hi[:, b % 2, g, :], start=False, stop=False)
                    last.then_inc(summed, 1)
            mm(ps_deg, zeros[0:EP, 0:128], zeros[0:EP, 0:NT], start=False, stop=True).then_inc(deg_done, 1)

            for l in range(2):
                hs = (nat, nat2)[l]
                pe.sem_inc(used[l], RB)

                def project(c, tiles):
                    pe.wait_ge(aggT_rdy[l], c + 2)
                    pe.wait_ge(conv_taken[l], c + 1)
                    for j in range(tiles):
                        for k in range(KD):
                            last = mm(gate_ps[j][:, 0:D], aggT[:, k, j * 128:(j + 1) * 128], gw[:, l, k, :], start=(k == 0), stop=(k == KD - 1))
                    last.then_inc(projd[l], 1)

                def aggregate(c, width, first=False, mid=None):
                    for t in range(NT):
                        if t == 0:
                            pe.wait_ge(aggT_rdy[l], c + 1)
                        if first and l == 0 and t == 0:
                            pe.wait_ge(hs_ready, 1)
                        if first and l == 1 and t % CT == 0:
                            pe.wait_ge(chunk_done[0], t // CT + 1)
                        pe.wait_ge(ring_in[l][t % RB], (RR * c + t // RB) * 16 + 16)
                        for f in range(KD):
                            last = mm(agg_ps[f][:, 0:width], hs[:, t, f * 128:(f + 1) * 128], ring2[:, t % RB, 0:width, 1], start=(t == 0), stop=(t == NT - 1))
                        last.then_inc(used[l], 1)
                        if mid and t == NT // 3:
                            mid()

                aggregate(0, CW, first=True)
                if l == 0:
                    pe.wait_ge(gcn_in, 16 * 8)
                with pe.Fori(0, NC - 1) as c:
                    aggregate(c + 1, CW, mid=lambda: project(c, CT))
                aggregate(NC, TW, mid=lambda: project(NC - 1, CT))
                project(NC, TW // 128)

            turned = [0]

            def transpose_in(src):
                for t in range(NT):
                    n = turned[0]
                    if n >= 2:
                        pe.wait_ge(tr_out, n - 1)
                    for k in range(KD):
                        last = tr(tr_ps[n % 2][:, k * 128:(k + 1) * 128], src[:, t, k * 128:(k + 1) * 128], ident[:, :])
                    last.then_inc(tr_done, 1)
                    turned[0] += 1

            pe.wait_ge(nat_ready, 1)
            transpose_in(nat)
            pe.wait_ge(tr_out, NT)
            pe.wait_ge(moe_in, 16 * 4)
            for t in range(NT):
                for k in range(KD):
                    last = mm(bank[0][:, t * X0:(t + 1) * X0], xT[:, k, t * 128:(t + 1) * 128], ewr[:, k, :], start=(k == 0), stop=(k == KD - 1))
            last.then_inc(logits_done, 1)
            pe.wait_ge(counted, 1)
            mm(bank[2][:, 0:NT * X0], below[:, :], both[:, :, :].rearrange("p t e -> p (t e)"), start=True, stop=True)
            mm(bank[3][:, 0:NT * X0], ones[:, :], both[:, :, :].rearrange("p t e -> p (t e)"), start=True, stop=True).then_inc(ranked, 1)

            pe.wait_ge(slots_ready, 1)

            def turn_tokens(i):
                pe.wait_ge(xt_in, 16 * i + 16)
                pe.wait_ge(xe_rdy, i + 1)
                for k in range(KD):
                    last = tr(bank[6][:, k * 128:(k + 1) * 128], xtile[:, k * 128:(k + 1) * 128], ident[:, :])
                last.then_inc(x_turned, 1)

            def turn_hidden(i):
                pe.wait_ge(hg_rdy, i + 2)
                pe.wait_ge(hT_act, i + 1)
                pe.wait_ge(hT_dve, i + 1)
                for h in range(H0 // 128):
                    last = tr(bank[2 + h // 4][:, h % 4 * 128:(h % 4 + 1) * 128], hg[:, h * 128:(h + 1) * 128], ident[:, :])
                last.then_inc(hT_ps, 1)

            def first_product(i):
                pe.wait_ge(w_ready, pe.value_load(of_i[0:1, bass.ds(i, 1)], min_val=0, max_val=X0 - 1) + 1)
                hold(pe)
                b = pe.value_load(par_i[0:1, bass.ds(i, 1)], min_val=0, max_val=1)
                pe.wait_ge(xe_rdy, i + 2)
                pe.wait_ge(hb_rdy, i + 1)
                for k in range(KD):
                    for h in range(2):
                        last = mm(bank[h][:, :], xe[:, k, :], w1[:, bass.ds(b, 1), k, h * 512:(h + 1) * 512].rearrange("p a h -> p (a h)"), start=(k == 0), stop=(k == KD - 1))
                last.then_inc(h_ps, 1)

            def second_product(i):
                b = pe.value_load(par_i[0:1, bass.ds(i, 1)], min_val=0, max_val=1)
                pe.wait_ge(hT_act, i + 2)
                pe.wait_ge(hT_dve, i + 2)
                pe.wait_ge(y_rdy, i + 1)
                for h in range(H0 // 128):
                    last = mm(bank[4][:, 0:D], hT[:, h, :], w2[:, bass.ds(b, 1), h, :].rearrange("p a d -> p (a d)"), start=(h == 0), stop=(h == H0 // 128 - 1))
                last.then_inc(y_ps_rdy, 1)

            pe.sem_inc(h_ps, 1)
            turn_tokens(0)
            first_product(0)
            with pe.Fori(1, ST) as i:
                turn_tokens(i)
                turn_hidden(i - 1)
                first_product(i)
                second_product(i - 1)
            turn_hidden(ST - 1)
            second_product(ST - 1)

            pe.wait_ge(gru_in, 16 * (4 + LAYERS))
            pe.wait_ge(moe_done, 1)
            n = 0
            for i in range(LAYERS):
                for m in range(KD):
                    for lo, hi in ((0, 512), (512, 768)):
                        if n >= 4:
                            pe.wait_ge(v_out, n - 3)
                        for k in range(KD):
                            last = mm(gate_ps[n % 4][:, 0:hi - lo], wt_sb[:, i, k, m * 128:(m + 1) * 128], wih[:, k, lo:hi], start=(k == 0), stop=(k == KD - 1))
                        last.then_inc(v_ps, 1)
                        n += 1
            pe.wait_ge(nat_ready, 2)
            transpose_in(nat)
            pe.wait_ge(tr_out, 2 * NT)
            pe.wait_ge(v_out, n)
            pe.sem_inc(rw_used, RR)

            def turn_back(i, t):
                pe.wait_ge(back_out, NT * i + t + (2 if t == 0 else 1))
                for k in range(KD):
                    last = tr(tr_ps[t % 2][:, k * 128:(k + 1) * 128], xT[:, k, t * 128:(t + 1) * 128], ident[:, :])
                last.then_inc(back_ps, 1)

            def aggregate_w(i, c, width, back=False, mid=None):
                q = CH * i + c
                for t in range(NT):
                    if t == 0:
                        pe.wait_ge(gT_rdy, q + 1)
                    if back and t + 2 < NT:
                        turn_back(i, t + 2)
                    if back:
                        pe.wait_ge(back_out, NT * i + t + 3)
                    if t % RB == 0:
                        pe.wait_ge(rw_in[t // RB], q * 16 + 16)
                    for f in range(KD):
                        last = mm(agg_ps[f][:, 0:width], nat[:, t, f * 128:(f + 1) * 128], ringw[:, t // RB, t % RB, 0:width], start=(t == 0), stop=(t == NT - 1))
                    if t % RB == RB - 1:
                        last.then_inc(rw_used, 1)
                    if mid and t == NT // 3:
                        mid()

            def gate_products(i, c, width):
                q = CH * i + c
                pe.wait_ge(gT_rdy, q + 2)
                at = bass.ds(c * CW, width)
                for j in range(KD):
                    pe.wait_ge(g_act, 2 * q + j + 1)
                    pe.wait_ge(g_dve, 2 * q + j + 1)
                    for b, blk, parts in ((0, j, "ih"), (1, KD + j, "ih"), (2, 2 * KD + j, "i"), (3, 2 * KD + j, "h")):
                        cols = slice(blk * 128, (blk + 1) * 128)
                        ops = [(v_now[:, k, cols], gT[:, k, 0:width]) for k in range(KD)] * ("i" in parts)
                        ops += [(whh[:, k, cols], xT[:, k, at]) for k in range(KD)] * ("h" in parts)
                        for m, (lhs, rhs) in enumerate(ops):
                            last = mm(gate_ps[b][:, 0:width], lhs, rhs, start=(m == 0), stop=(m == len(ops) - 1))
                    last.then_inc(gates, 1)

            with pe.Fori(0, LAYERS) as i:
                pe.wait_ge(g_new, CH * i + 1)
                turn_back(i, 0)
                turn_back(i, 1)
                aggregate_w(i, 0, CW, back=True)
                pe.wait_ge(v_set, i + 1)
                hold(pe)
                with pe.Fori(0, NC - 1) as c:
                    aggregate_w(i, c + 1, CW, mid=lambda: gate_products(i, c, CW))
                aggregate_w(i, NC, TW, mid=lambda: gate_products(i, NC - 1, CW))
                gate_products(i, NC, TW)
            pe.wait_ge(g_new, CH * LAYERS + 1)
            for t in range(NT):
                turn_back(LAYERS, t)

            pe.wait_ge(nat_ready, 3)
            pe.wait_ge(back_out, NT * (LAYERS + 1) + 2)
            for k in range(KD):
                for t in range(NT):
                    rows = 128 if t < NT - 1 else LAST
                    last = mm(bank[0][:, k:k + 1], nat[0:rows, t, k * 128:(k + 1) * 128], ones[0:rows, 0:1], start=(t == 0), stop=(t == NT - 1))
            last.then_inc(f_mean, 1)
            transpose_in(nat)
            pe.wait_ge(f_meanT, 1)
            pe.wait_ge(f_in, 64)
            for k in range(KD):
                last = mm(bank[1][0:1, 0:X0], fmean[:, k:k + 1], fwr[:, k, :], start=(k == 0), stop=(k == KD - 1))
            last.then_inc(f_lg, 1)
            pe.wait_ge(f_top, 1)
            mm(bank[1][:, 16:18], ones[0:1, 0:128], tw[0:1, 0:2], start=True, stop=True).then_inc(f_twb, 1)
            pe.wait_ge(tr_out, 3 * NT)
            pe.wait_ge(fw_rdy, 1)

            HB = F1 // 128
            y_ps = [bank[0], bank[1], bank[6], bank[7]]

            def second(c, width):
                at = bass.ds(c * CW, width)
                for x in range(2):
                    for h in range(HB):
                        m = x * HB + h
                        pe.wait_ge(fh_rdy, 2 * HB * c + m + 1)
                        for k in range(KD):
                            last = mm(gate_ps[m % 4][:, 0:width], fw1[:, x, k, h * 128:(h + 1) * 128], xT[:, k, at], start=(k == 0), stop=(k == KD - 1))
                        last.then_inc(fh_ps, 1)
                pe.wait_ge(fy_taken, c + 1)
                for m in range(2 * HB):
                    pe.wait_ge(fh_rdy, 2 * HB * c + m + 5)
                    for j in range(width // 128):
                        last = mm(y_ps[j][:, 0:D], fhid[:, m // HB, m % HB, j * 128:(j + 1) * 128], fw2s[:, m // HB, m % HB, :], start=(m == 0), stop=(m == 2 * HB - 1))
                last.then_inc(fy, 1)

            with pe.Fori(0, NC) as c:
                second(c, CW)
            second(NC, TW)

        @block.scalar
        def _(act):
            A = nc.scalar.activation
            roots = [0]

            def root(view, src):
                act.wait_ge(var_ready, roots[0] + 1)
                roots[0] += 1
                A(view, src, ACT.Sqrt).then_inc(std_ready, 1)

            root(std[:, :], var[:, :])
            act.sem_inc(sums_out, 2)
            act.wait_ge(keyT_ps, 1)
            A(keyT[:, :, :], bank[3][0:100, 0:4 * EP].rearrange("p (c k) -> p c k", c=4), ACT.Copy).then_inc(keyT_sb, 1)
            with act.Fori(0, ET // G // KB) as i:
                for b in range(KB):
                    act.wait_ge(summed, KB * i + b + 3)
                    act.wait_ge(placed, KB * i + b + 1)
                    A(sums[:, b % 2, :, :], bank[b % 2][0:EP, 0:8 * G].rearrange("p (g k) -> p g k", k=8), ACT.Copy).then_inc(sums_out, 1)
            root(std[:, :], var[:, :])

            act.sem_inc(planes, RB)
            for l in range(2):
                act.sem_inc(aggT_rdy[l], 1)

                def chunk(c, width):
                    if l == 0:
                        for t in range(NT):
                            if t % RB == 0:
                                act.wait_ge(staged, 16 * (RR * c + t // RB) + 16)
                            act.wait_ge(ring_in[0][t % RB], (RR * c + t // RB) * 16 + 16)
                            A(stage[:, t % RB, 0:width], ring2[:, t % RB, 0:width, 0], ACT.Copy).then_inc(planes, 1)
                    act.wait_ge(used[l], NT * c + NT + RB)
                    act.wait_ge(projd[l], c + 1)
                    for f in range(KD):
                        last = A(aggT[:, f, 0:width], agg_ps[f][:, 0:width], ACT.Copy)
                    last.then_inc(aggT_rdy[l], 1)

                def chunk_root(c, tiles):
                    act.wait_ge(cvar[l], c + 1)
                    A(std[:, 0:tiles], var[:, 0:tiles], ACT.Sqrt).then_inc(cstd[l], 1)

                act.sem_inc(projd[l], 1)
                chunk(0, CW)
                with act.Fori(0, NC - 1) as c:
                    chunk(c + 1, CW)
                    chunk_root(c, CT)
                chunk(NC, TW)
                chunk_root(NC - 1, CT)
                chunk_root(NC, TW // 128)

            evicted = [0]

            def evict_turned():
                for t in range(NT):
                    n = evicted[0]
                    act.wait_ge(tr_done, n + 1)
                    A(xT[:, :, t * 128:(t + 1) * 128], tr_ps[n % 2][:, 0:D].rearrange("p (k n) -> p k n", k=KD), ACT.Copy).then_inc(tr_out, 1)
                    evicted[0] += 1

            root(std[:, :], var[:, :])
            root(std[:, :], var[:, :])
            evict_turned()
            act.wait_ge(lmax, 1)
            A(pr[:, :, :], t8[:, :, :], ACT.Exp).then_inc(lexp, 1)
            act.sem_inc(hT_act, 1)

            def turned_hidden(i):
                act.wait_ge(hT_ps, i + 1)
                act.wait_ge(y_ps_rdy, i + 1)
                A(hT[:, 0:4, :].rearrange("p h n -> p (h n)"), bank[2][:, :], ACT.Copy).then_inc(hT_act, 1)

            def gelu(i):
                act.wait_ge(hb_rdy, i + 2)
                act.wait_ge(hT_ps, i)
                A(hg[:, :], hb[:, :], ACT.Gelu).then_inc(hg_rdy, 1)

            act.sem_inc(y_ps_rdy, 1)
            act.sem_inc(hg_rdy, 1)
            act.wait_ge(hb_rdy, 2)
            A(hg[:, :], hb[:, :], ACT.Gelu).then_inc(hg_rdy, 1)
            with act.Fori(1, ST) as i:
                turned_hidden(i - 1)
                gelu(i)
            turned_hidden(ST - 1)

            root(std[:, :], var[:, :])
            act.wait_ge(gru_in, 16 * (4 + LAYERS))
            n = 0
            for i in range(LAYERS):
                for m in range(KD):
                    for lo, hi in ((0, 512), (512, 768)):
                        act.wait_ge(v_ps, n + 1)
                        A(v_all[:, i, m, lo:hi], gate_ps[n % 4][:, 0:hi - lo], ACT.Copy).then_inc(v_out, 1)
                        n += 1
            evict_turned()
            act.sem_inc(back_out, 2)
            act.sem_inc(gT_rdy, 1)
            act.sem_inc(g_act, 1)
            act.wait_ge(v_out, n)

            def back(i, t):
                act.wait_ge(back_ps, NT * i + t + 1)
                A(nat[:, t, :], tr_ps[t % 2][:, 0:D], ACT.Copy).then_inc(back_out, 1)

            def gru_evict(i, c, width):
                q = CH * i + c
                act.wait_ge(rw_used, RR * (q + 2))
                act.wait_ge(gates, 2 * q + 1)
                for f in range(KD):
                    last = A(gT[:, f, 0:width], agg_ps[f][:, 0:width], ACT.Copy)
                last.then_inc(gT_rdy, 1)

            def gru_act(i, c, width):
                q = CH * i + c
                act.wait_ge(g_new, q + 1)
                for j in range(KD):
                    act.wait_ge(gates, 2 * q + j + 2)
                    A(gr[:, j, 0:width], gate_ps[0][:, 0:width], ACT.Sigmoid, bias=brz[:, j:j + 1])
                    A(gz[:, j, 0:width], gate_ps[1][:, 0:width], ACT.Sigmoid, bias=brz[:, KD + j:KD + j + 1]).then_inc(g_act, 1)
                for j in range(KD):
                    act.wait_ge(g_dve, 2 * q + j + 2)
                    A(gn[:, j, 0:width], gb[:, j, 0:width], ACT.Tanh, bias=bih[:, 2 * KD + j:2 * KD + j + 1]).then_inc(g_tanh, 1)

            act.sem_inc(gates, 1)
            with act.Fori(0, LAYERS) as i:
                for t in range(NT):
                    back(i, t)
                    if t == 2:
                        A(v_now[:, :, :], v_all[:, bass.ds(i, 1), :, :].rearrange("p a k g -> p (a k) g"), ACT.Copy).then_inc(v_set, 1)
                gru_evict(i, 0, CW)
                with act.Fori(0, NC - 1) as c:
                    gru_act(i, c, CW)
                    gru_evict(i, c + 1, CW)
                gru_act(i, NC - 1, CW)
                gru_evict(i, NC, TW)
                gru_act(i, NC, TW)
            for t in range(NT):
                back(LAYERS, t)

            root(std[:, :], var[:, :])
            evict_turned()
            act.wait_ge(f_e, 1)
            A(r8[1][:, :], r8[0][:, :], ACT.Exp, accum_out=r1[1][:, :]).then_inc(f_a, 1)
            act.wait_ge(f_e, 2)
            A(r8[6][:, :], r8[5][:, :], ACT.Exp, accum_out=r1[3][:, :]).then_inc(f_a, 1)
            act.wait_ge(f_e, 3)
            A(te[:, :], te[:, :], ACT.Exp, accum_out=r1[4][:, :]).then_inc(f_a, 1)

            act.sem_inc(fh_rdy, 4)
            act.sem_inc(fy, 1)
            act.wait_ge(fw_in, 16 * 8)
            HB = F1 // 128

            def second(c, width):
                for m in range(2 * HB):
                    act.wait_ge(fh_ps, 2 * HB * c + m + 1)
                    if m == 0:
                        act.wait_ge(fy, c + 1)
                    A(fhid[:, m // HB, m % HB, 0:width], gate_ps[m % 4][:, 0:width], ACT.Gelu, bias=fb1[:, m // HB, m % HB:m % HB + 1]).then_inc(fh_rdy, 1)

            def second_root(c, tiles):
                act.wait_ge(fvar, c + 1)
                A(std[:, 0:tiles], var[:, 0:tiles], ACT.Sqrt).then_inc(fstd, 1)

            with act.Fori(0, NC) as c:
                second(c, CW)
                second_root(c, CT)
            second(NC, TW)
            second_root(NC, TW // 128)

        @block.vector
        def _(v):
            V = nc.vector
            ch = Count(v, dve_n)
            link, go = ch.link, ch.go

            def moments(tiles):
                s = lambda k: stats[:, 0:tiles, k]
                go(V.tensor_tensor(st_sum[:, 0:tiles], s(1), s(4), ALU.add))
                go(V.tensor_tensor(st_dif[:, 0:tiles], s(1), s(4), ALU.subtract))
                link(V.tensor_tensor(st_m2[:, 0:tiles], s(2), s(5), ALU.add))
                go(V.tensor_scalar(mean[:, 0:tiles], st_sum[:, 0:tiles], 0.5, None, ALU.mult))
                go(V.tensor_tensor(st_sq[:, 0:tiles], st_dif[:, 0:tiles], st_dif[:, 0:tiles], ALU.mult))
                link(V.tensor_scalar(st_m2[:, 0:tiles], st_m2[:, 0:tiles], 1.0 / D, EPS, ALU.mult, ALU.add))
                return V.scalar_tensor_tensor(var[:, 0:tiles], st_sq[:, 0:tiles], 0.25, st_m2[:, 0:tiles], ALU.mult, ALU.add)

            roots = [0]

            def inverse_root():
                v.wait_ge(std_ready, roots[0] + 1)
                roots[0] += 1
                link(V.reciprocal(rstd[:, :], std[:, :]))

            def layernorm(dst, src):
                with ch.loop(0, NT, 1) as t:
                    go(V.bn_stats(stats[:, bass.ds(t, 1), :].rearrange("p a k -> p (a k)"), src[:, bass.ds(t, 1), :].rearrange("p a f -> p (a f)")))
                v.wait_ge(ch.sem, ch.base + ch.k)
                moments(NT).then_inc(var_ready, 1)
                inverse_root()
                with ch.loop(0, NT, 1) as t:
                    go(V.tensor_scalar(dst[:, bass.ds(t, 1), :].rearrange("p a f -> p (a f)"), src[:, bass.ds(t, 1), :].rearrange("p a f -> p (a f)"),
                                       mean[:, bass.ds(t, 1)], rstd[:, bass.ds(t, 1)], ALU.subtract, ALU.mult))
                v.wait_ge(ch.sem, ch.base + ch.k)

            v.sem_inc(placed, 2)
            v.wait_ge(edges_in, 48)
            go(V.tensor_copy(srcf[:, :], srci[:, :]))
            link(V.tensor_copy(dstf[:, :], dsti[:, :]))
            V.scalar_tensor_tensor(key[:, :], srcf[:, :], float(NP), dstf[:, :], ALU.mult, ALU.add).then_inc(key_done, 1)
            go(V.tensor_scalar(lo_i[:, :], dsti[:, :], 127, None, ALU.bitwise_and))
            go(V.tensor_scalar(hi_i[:, :], dsti[:, :], 7, None, ALU.logical_shift_right))
            go(V.tensor_scalar(wbits[:, :].bitcast(I32), w[:, :].bitcast(I32), 0x7fffffff, None, ALU.bitwise_and))
            go(V.memset(wabs[:, :], 1e-6))
            go(V.memset(parts0[:, :, :], 0.0))
            link(V.memset(parts1[:, :, :], 1.0))
            go(V.tensor_copy(dlo[:, :], lo_i[:, :]))
            go(V.tensor_copy(dhi[:, :], hi_i[:, :]))
            go(V.tensor_scalar(finite[:, :], wbits[:, :], FLT_MAX, None, ALU.is_le))
            v.wait_ge(consts, 11)
            link(V.tensor_copy(to_spare[:, :], spare_i[:, :]))
            go(V.tensor_tensor(to_spare[:, :], to_spare[:, :], key[:, :], ALU.subtract))
            link(V.copy_predicated(wabs[:, :], finite[:, :], wbits[:, :]))
            link(V.tensor_scalar(wabs[:, :], wabs[:, :], 1e-6, None, ALU.max))
            for k, x in enumerate((w, wabs)):
                link(V.tensor_copy(parts0[:, :, 3 * k], x[:, :]))
                link(V.tensor_tensor(rest[:, :], x[:, :], parts0[:, :, 3 * k], ALU.subtract))
                link(V.tensor_copy(parts0[:, :, 3 * k + 1], rest[:, :]))
                link(V.tensor_tensor(rest[:, :], rest[:, :], parts0[:, :, 3 * k + 1], ALU.subtract))
                link(V.tensor_copy(parts0[:, :, 3 * k + 2], rest[:, :]))
            link(V.tensor_copy(parts1[:, :, 0:6], parts0[:, :, 0:6]))
            v.sem_inc(compared, KB)
            v.wait_ge(x_in, 32)
            layernorm(res, res)

            def compare(i, b):
                c = b % 2
                v.wait_ge(keyrow_in[b], 16 * i + 16)
                v.wait_ge(summed, KB * i + b + 1)
                at = lambda x, g: x[:, bass.ds(KB * G * i + G * b + g, 1)]
                for g in range(G):
                    V.tensor_scalar(eq[:, c, g, :], keyrow[:, b, :], at(key, g), None, ALU.is_equal)
                for g in range(G):
                    V.scalar_tensor_tensor(own[:, c, g, :], keyrow[:, b, g * EP:(g + 1) * EP], at(key, g), before[:, :], ALU.is_equal, ALU.mult, accum_out=own_n[:, c, g:g + 1])
                for g in range(G):
                    V.tensor_scalar(hit_lo[:, c, g, :], row[0:EP, :], at(dlo, g), None, ALU.is_equal)
                    last = V.tensor_scalar(hit_hi[:, c, g, :], row[0:EP, 0:NT], at(dhi, g), at(wabs, g), ALU.is_equal, ALU.mult)
                last.then_inc(compared, 1)

            def place(i, b):
                c = b % 2
                v.wait_ge(sums_out, KB * i + b + 3)
                v.wait_ge(turn, KB * i + b + 1)
                at = lambda x: x[:, bass.ds(KB * G * i + G * b, G)]
                V.tensor_tensor(half[:, c, :, :], sums[:, c, :, 1:5:3], sums[:, c, :, 2:6:3], ALU.add)
                link(V.tensor_tensor(earlier[:, c, :], sums[:, c, :, 6], own_n[:, c, :], ALU.add))
                V.tensor_tensor(pair[:, c, :, :], sums[:, c, :, 0:4:3], half[:, c, :, :], ALU.add)
                link(V.scalar_tensor_tensor(shift[:, c, :], earlier[:, c, :], 1.0, at(to_spare), ALU.min, ALU.mult))
                V.tensor_tensor(slot[:, c, :], shift[:, c, :], at(key), ALU.add).then_inc(placed, 1)

            with ch.loop(0, ET // G // KB, 2 * KB) as i:
                for b in range(0, KB, 2):
                    compare(i, b)
                    compare(i, b + 1)
                    place(i, b)
                    place(i, b + 1)
            v.wait_ge(deg_done, 1)
            V.tensor_scalar(var[:, :], bank[2][:, 0:NT], 1.0, None, ALU.add).then_inc(var_ready, 1)
            v.wait_ge(std_ready, roots[0] + 1)
            roots[0] += 1
            link(V.reciprocal(dis[:, :], std[:, :]))
            v.wait_ge(scattered, 16 * ET)
            with ch.loop(0, NT, 1) as t:
                go(V.tensor_scalar(nat[:, bass.ds(t, 1), :].rearrange("p a f -> p (a f)"), res[:, bass.ds(t, 1), :].rearrange("p a f -> p (a f)"), dis[:, bass.ds(t, 1)], None, ALU.mult))
            v.wait_ge(ch.sem, ch.base + ch.k)
            v.sem_inc(hs_ready, 1)

            v.wait_ge(gcn_in, 16 * 8)
            for l in range(2):
                v.sem_inc(conv_taken[l], 1)

                def finish(c, tiles):
                    at = lambda x: x[:, bass.ds(c * CT, tiles), :]
                    rows = lambda m: grow[:, l, m:m + 1, :].to_broadcast([128, tiles, D])
                    v.wait_ge(projd[l], c + 2)
                    for j in range(tiles):
                        last = V.scalar_tensor_tensor(conv[:, j, :], gate_ps[j][:, 0:D], dis[:, bass.ds(c * CT + j, 1)], grow[:, l, 0, :], ALU.mult, ALU.add)
                    last.then_inc(conv_taken[l], 1)
                    v.wait_ge(conv_taken[l], c + 2)
                    go(V.memset(safe[:, 0:tiles, :], 0.0))
                    link(V.tensor_tensor(conv_d[:, 0:tiles, :], conv[:, 0:tiles, :], conv[:, 0:tiles, :], ALU.subtract))
                    link(V.tensor_scalar(fin_mask[:, 0:tiles, :], conv_d[:, 0:tiles, :], 0.0, None, ALU.is_equal))
                    hold(v)
                    link(V.copy_predicated(safe[:, 0:tiles, :], fin_mask[:, 0:tiles, :], conv[:, 0:tiles, :]))
                    for j in range(tiles):
                        last = V.bn_stats(stats[:, j, :], safe[:, j, :])
                    link(last)
                    moments(tiles).then_inc(cvar[l], 1)
                    v.wait_ge(cstd[l], c + 1)
                    link(V.reciprocal(rstd[:, 0:tiles], std[:, 0:tiles]))
                    for j in range(tiles):
                        last = V.tensor_scalar(normed[:, j, :], safe[:, j, :], mean[:, j:j + 1], rstd[:, j:j + 1], ALU.subtract, ALU.mult)
                    link(last)
                    link(V.tensor_tensor(normed[:, 0:tiles, :], normed[:, 0:tiles, :], rows(1), ALU.mult))
                    link(V.tensor_tensor(normed[:, 0:tiles, :], normed[:, 0:tiles, :], rows(2), ALU.add))
                    last = V.scalar_tensor_tensor(at(res), normed[:, 0:tiles, :], 0.0, at(res), ALU.max, ALU.add)
                    if l == 0:
                        link(last)
                        for j in range(tiles):
                            last = V.tensor_scalar(nat2[:, bass.ds(c * CT + j, 1), :].rearrange("p a f -> p (a f)"), res[:, bass.ds(c * CT + j, 1), :].rearrange("p a f -> p (a f)"), dis[:, bass.ds(c * CT + j, 1)], None, ALU.mult)
                    last.then_inc(chunk_done[l], 1)

                with ch.loop(0, NC, 16 if l == 0 else 15) as c:
                    finish(c, CT)
                finish(NC, TW // 128)

            v.wait_ge(chunk_done[1], CH)
            v.wait_ge(x_in, 64)
            link(V.tensor_tensor(res[:, :, :], res[:, :, :], nat[:, :, :], ALU.add))
            layernorm(nat, res)
            v.sem_inc(nat_ready, 1)
            layernorm(nat2, nat)

            v.wait_ge(logits_done, 1)
            v.wait_ge(moe_in, 16 * 4)
            wide = lambda x: x[:, :].rearrange("p (t a) -> p t a", a=1).to_broadcast([128, NT, X0])
            pos = row[:, 0:X0].rearrange("p (a e) -> p a e", a=1).to_broadcast([128, NT, X0])
            link(V.tensor_tensor(lg[:, :, :], bank[0][:, 0:NT * X0].rearrange("p (t e) -> p t e", e=X0), ebr[:, :].rearrange("p (a e) -> p a e", a=1).to_broadcast([128, NT, X0]), ALU.add))
            link(V.reduce_max(m1[:, :], lg[:, :, :], AX))
            V.tensor_tensor(t8[:, :, :], lg[:, :, :], wide(m1), ALU.subtract).then_inc(lmax, 1)
            v.wait_ge(lexp, 1)

            def first_of_max(hit, probs, best):
                link(V.reduce_max(best[:, :], probs[:, :, :], AX))
                link(V.tensor_tensor(u8[:, :, :], probs[:, :, :], wide(best), ALU.is_lt))
                link(V.scalar_tensor_tensor(u8[:, :, :], u8[:, :, :], 16.0, pos, ALU.mult, ALU.add))
                link(V.tensor_reduce(ix[:, :], u8[:, :, :], AX, ALU.min))
                link(V.tensor_tensor(hit[:, :, :], u8[:, :, :], wide(ix), ALU.is_equal))

            first_of_max(oh1, pr, m1)
            link(V.scalar_tensor_tensor(t8[:, :, :], oh1[:, :, :], -4.0, pr[:, :, :], ALU.mult, ALU.add))
            first_of_max(oh2, t8, m2)
            V.tensor_tensor(both[:, :, :], oh1[:, :, :], oh2[:, :, :], ALU.add).then_inc(counted, 1)
            link(V.tensor_tensor(q1[:, :], m1[:, :], m2[:, :], ALU.add))
            link(V.reciprocal(q1[:, :], q1[:, :]))
            go(V.tensor_tensor(q2[:, :], m2[:, :], q1[:, :], ALU.mult))
            link(V.tensor_tensor(wt[:, :], m1[:, :], q1[:, :], ALU.mult))
            v.wait_ge(ranked, 1)
            link(V.tensor_copy(tot[:, :, :], bank[3][:, 0:NT * X0].rearrange("p (t e) -> p t e", e=X0)))

            def prefix(bufs, n):
                old, new, s = bufs[0], bufs[1], 1
                while s < n:
                    go(V.tensor_copy(new(0, s), old(0, s)))
                    link(V.tensor_tensor(new(s, n), old(s, n), old(0, n - s), ALU.add))
                    old, new, s = new, old, 2 * s
                return old

            go(V.memset(pre[0][:, 0:1, :], 0.0))
            link(V.tensor_copy(pre[0][:, 1:NT, :], tot[:, 0:NT - 1, :]))
            ahead = prefix([lambda lo, hi, x=x: x[:, lo:hi, :] for x in pre], NT)
            go(V.tensor_tensor(rank[:, :, :], bank[2][:, 0:NT * X0].rearrange("p (t e) -> p t e", e=X0), ahead(0, NT), ALU.add))
            link(V.tensor_tensor(nf[:, :], ahead(NT - 1, NT).rearrange("p a e -> p (a e)"), tot[:, NT - 1, :], ALU.add))
            link(V.tensor_scalar(nf[:, :], nf[:, :], 127.0, None, ALU.add))
            link(V.tensor_copy(ni[:, :], nf[:, :]))
            link(V.tensor_scalar(ni[:, :], ni[:, :], 7, None, ALU.logical_shift_right))
            link(V.tensor_copy(ns[:, :], ni[:, :]))
            go(V.memset(first[0][:, 0:1], 0.0))
            link(V.tensor_scalar(first[0][:, 1:X0 + 1], ns[:, :], 1.0, None, ALU.max))
            start = prefix([lambda lo, hi, x=x: x[:, lo:hi] for x in first], X0 + 1)
            link(V.scalar_tensor_tensor(rank[:, :, :], start(0, X0).rearrange("p (a e) -> p a e", a=1).to_broadcast([128, NT, X0]), 128.0, rank[:, :, :], ALU.mult, ALU.add))
            for k, hit in enumerate((oh1, oh2)):
                link(V.tensor_tensor(u8[:, :, :], rank[:, :, :], hit[:, :, :], ALU.mult))
                link(V.reduce_sum(slot_f[:, k, :], u8[:, :, :], AX))
            link(V.tensor_copy(slot_u[:, :, :], slot_f[:, :, :]))
            go(V.tensor_copy(first_i[:, :], start(0, X0 + 1)[0:1, :]))
            link(V.tensor_tensor(of_t[:, :, :], row[0:1, 0:ST].rearrange("p (t a) -> p t a", a=1).to_broadcast([1, ST, X0]),
                                 start(0, X0)[0:1, :].rearrange("p (a e) -> p a e", a=1).to_broadcast([1, ST, X0]), ALU.is_ge))
            link(V.reduce_sum(of_f[:, :], of_t[:, :, :], AX))
            link(V.tensor_scalar(of_f[:, :], of_f[:, :], 1.0, None, ALU.subtract))
            link(V.tensor_copy(of_i[:, :], of_f[:, :]))
            link(V.tensor_scalar(par_i[:, :], of_i[:, :], 1, None, ALU.bitwise_and))
            v.sem_inc(slots_ready, 1)
            v.sem_inc(xe_rdy, 1)
            v.sem_inc(y_rdy, 1)
            v.sem_inc(hb_rdy, 1)
            v.sem_inc(hT_dve, 1)

            def scale_tokens(i):
                e = v.value_load(of_i[0:1, bass.ds(i, 1)], min_val=0, max_val=X0 - 1)
                v.wait_ge(x_turned, i + 1)
                v.wait_ge(h_ps, i + 1)
                for k in range(KD):
                    last = V.tensor_scalar(xe[:, k, :], bank[6][:, k * 128:(k + 1) * 128], eg[:, k, bass.ds(e, 1)], eb[:, k, bass.ds(e, 1)], ALU.mult, ALU.add)
                last.then_inc(xe_rdy, 1)

            def turned_hidden(i):
                v.wait_ge(hT_ps, i + 1)
                v.wait_ge(y_ps_rdy, i + 1)
                V.tensor_copy(hT[:, 4:8, :].rearrange("p h n -> p (h n)"), bank[3][:, :]).then_inc(hT_dve, 1)

            def add_bias1(i):
                b = v.value_load(par_i[0:1, bass.ds(i, 1)], min_val=0, max_val=1)
                v.wait_ge(h_ps, i + 2)
                v.wait_ge(hg_rdy, i + 1)
                for h in range(2):
                    last = V.tensor_tensor(hb[:, h * 512:(h + 1) * 512], bank[h][:, :], erow[:, bass.ds(b, 1), h * 512:(h + 1) * 512].rearrange("p a h -> p (a h)"), ALU.add)
                last.then_inc(hb_rdy, 1)

            def add_bias2(i):
                b = v.value_load(par_i[0:1, bass.ds(i, 1)], min_val=0, max_val=1)
                v.wait_ge(y_ps_rdy, i + 2)
                v.wait_ge(y_out, 16 * i + 16)
                V.tensor_tensor(ytile[:, :], bank[4][:, 0:D], erow[:, bass.ds(b, 1), H0:H0 + D].rearrange("p a d -> p (a d)"), ALU.add).then_inc(y_rdy, 1)

            scale_tokens(0)
            add_bias1(0)
            with v.Fori(1, ST) as i:
                scale_tokens(i)
                turned_hidden(i - 1)
                add_bias1(i)
                add_bias2(i - 1)
            turned_hidden(ST - 1)
            add_bias2(ST - 1)
            for t in range(NT):
                v.wait_ge(y_got[t % 4], 32 * (t // 4) + 32)
                link(V.scalar_tensor_tensor(acc[:, t % 2, :], yg[:, t % 4, 0, :], wt[:, t:t + 1], res[:, t, :], ALU.mult, ALU.add))
                V.scalar_tensor_tensor(res[:, t, :], yg[:, t % 4, 1, :], q2[:, t:t + 1], acc[:, t % 2, :], ALU.mult, ALU.add).then_inc(y_free, 1)
            v.wait_ge(y_free, NT)
            layernorm(nat, res)
            v.sem_inc(moe_done, 1)
            v.sem_inc(nat_ready, 1)

            v.wait_ge(gru_in, 16 * (4 + LAYERS))
            V.tensor_tensor(brz[:, :], bih[:, 0:4], bhh[:, 0:4], ALU.add).then_inc(g_dve, 1)
            v.wait_ge(g_dve, 1)
            v.sem_inc(g_new, 1)

            def gru(i, c, width):
                q = CH * i + c
                for j in range(KD):
                    v.wait_ge(g_act, 2 * q + j + 2)
                    link(V.scalar_tensor_tensor(ga[:, j, 0:width], gate_ps[3][:, 0:width], bhh[:, 2 * KD + j:2 * KD + j + 1], gr[:, j, 0:width], ALU.add, ALU.mult))
                    V.tensor_tensor(gb[:, j, 0:width], gate_ps[2][:, 0:width], ga[:, j, 0:width], ALU.add).then_inc(g_dve, 1)
                at = xT[:, :, bass.ds(c * CW, width)]
                v.wait_ge(g_tanh, 2 * q + 2)
                link(V.tensor_tensor(ga[:, :, 0:width], at, gn[:, :, 0:width], ALU.subtract))
                link(V.tensor_tensor(ga[:, :, 0:width], ga[:, :, 0:width], gz[:, :, 0:width], ALU.mult))
                V.tensor_tensor(at, ga[:, :, 0:width], gn[:, :, 0:width], ALU.add).then_inc(g_new, 1)

            with ch.loop(0, LAYERS, 4 * CH) as i:
                with ch.loop(0, NC, 4) as c:
                    gru(i, c, CW)
                gru(i, NC, TW)
            v.wait_ge(back_out, NT * (LAYERS + 1) + 2)
            link(V.tensor_tensor(res[:, :, :], res[:, :, :], nat[:, :, :], ALU.add))
            layernorm(nat, res)
            v.sem_inc(nat_ready, 1)

            v.wait_ge(f_mean, 1)
            V.tensor_scalar(fmean[:, :], bank[0][:, 0:KD], 1.0 / N, None, ALU.mult).then_inc(f_meanT, 1)
            v.wait_ge(f_lg, 1)
            v.wait_ge(f_in, 64)
            one = lambda x: x[0:1, 0:1]
            link(V.tensor_tensor(r8[2][:, :], bank[1][0:1, 0:X0], fbr[:, :], ALU.add))
            link(V.reduce_max(r1[0][:, :], r8[2][:, :], AX))
            V.tensor_scalar(r8[0][:, :], r8[2][:, :], one(r1[0]), None, ALU.subtract).then_inc(f_e, 1)
            v.wait_ge(f_a, 1)
            link(V.reciprocal(r1[2][:, :], r1[1][:, :]))
            link(V.tensor_scalar(r8[2][:, :], r8[1][:, :], one(r1[2]), None, ALU.mult))
            link(V.tensor_scalar(r8[3][:, :], r8[2][:, :], float(N), None, ALU.mult))
            link(V.tensor_scalar(r8[4][:, :], r8[3][:, :], CAPACITY, None, ALU.max))
            link(V.reciprocal(r8[4][:, :], r8[4][:, :]))
            link(V.tensor_scalar(r8[4][:, :], r8[4][:, :], CAPACITY, None, ALU.mult))
            link(V.tensor_scalar(r8[7][:, :], r8[3][:, :], CAPACITY, None, ALU.is_gt))
            link(V.tensor_scalar(r8[4][:, :], r8[4][:, :], 1.0, None, ALU.subtract))
            link(V.tensor_tensor(r8[4][:, :], r8[4][:, :], r8[7][:, :], ALU.mult))
            link(V.scalar_tensor_tensor(r8[2][:, :], r8[4][:, :], 1.0, r8[2][:, :], ALU.add, ALU.mult))
            link(V.reduce_max(r1[0][:, :], r8[2][:, :], AX))
            V.tensor_scalar(r8[5][:, :], r8[2][:, :], one(r1[0]), None, ALU.subtract).then_inc(f_e, 1)
            v.wait_ge(f_a, 2)
            link(V.reciprocal(r1[2][:, :], r1[3][:, :]))
            link(V.tensor_scalar(r8[3][:, :], r8[6][:, :], one(r1[2]), None, ALU.mult))
            link(V.max(top[:, :], r8[3][:, :]))
            link(V.max_index(topi[:, :], top[:, :], r8[3][:, :]))
            V.tensor_scalar(te[:, :], top[:, 0:2], one(top), None, ALU.subtract).then_inc(f_e, 1)
            v.wait_ge(f_a, 3)
            link(V.reciprocal(r1[5][:, :], r1[4][:, :]))
            V.tensor_scalar(tw[:, :], te[:, :], one(r1[5]), None, ALU.mult).then_inc(f_top, 1)
            v.wait_ge(f_twb, 1)
            link(V.tensor_copy(twb[:, :], bank[1][:, 16:18]))
            v.wait_ge(fw_in, 16 * 8)
            for k in range(2):
                go(V.tensor_scalar(fw2s[:, k, :, :], fw2[:, k, :, :], twb[:, k:k + 1], None, ALU.mult))
            link(V.tensor_scalar(fmix[:, :], fb2[:, 0, :], twb[:, 0:1], None, ALU.mult))
            link(V.scalar_tensor_tensor(fmix[:, :], fb2[:, 1, :], twb[:, 1:2], fmix[:, :], ALU.mult, ALU.add))
            v.sem_inc(fw_rdy, 1)
            v.sem_inc(fy_taken, 1)

            y_ps = [bank[0], bank[1], bank[6], bank[7]]

            def second(c, tiles):
                at = lambda x: x[:, bass.ds(c * CT, tiles), :]
                v.wait_ge(fy, c + 2)
                for j in range(tiles):
                    last = V.tensor_tensor(fo[:, j, :], y_ps[j][:, 0:D], fmix[:, :], ALU.add)
                last.then_inc(fy_taken, 1)
                v.wait_ge(fy_taken, c + 2)
                link(V.tensor_tensor(fo[:, 0:tiles, :], fo[:, 0:tiles, :], at(nat), ALU.add))
                for j in range(tiles):
                    last = V.bn_stats(stats[:, j, :], fo[:, j, :])
                link(last)
                moments(tiles).then_inc(fvar, 1)
                v.wait_ge(fstd, c + 1)
                link(V.reciprocal(rstd[:, 0:tiles], std[:, 0:tiles]))
                for j in range(tiles):
                    last = V.tensor_scalar(fn[:, j, :], fo[:, j, :], mean[:, j:j + 1], rstd[:, j:j + 1], ALU.subtract, ALU.mult)
                link(last)
                rows = lambda m: fgb[:, m:m + 1, :].to_broadcast([128, tiles, D])
                link(V.tensor_tensor(fn[:, 0:tiles, :], fn[:, 0:tiles, :], rows(0), ALU.mult))
                link(V.tensor_tensor(fn[:, 0:tiles, :], fn[:, 0:tiles, :], rows(1), ALU.add))
                V.tensor_tensor(at(res), at(res), fn[:, 0:tiles, :], ALU.add).then_inc(o_ready, 1)

            with ch.loop(0, NC, 12) as c:
                second(c, CT)
            second(NC, TW // 128)


_INS = ['x', 'src', 'dst', 'edge_weight', 'L0_gnn_W1', 'L0_gnn_b1', 'L0_gnn_ln_g1', 'L0_gnn_ln_b1', 'L0_gnn_W2', 'L0_gnn_b2', 'L0_gnn_ln_g2', 'L0_gnn_ln_b2',
        'L0_ffn_Wr', 'L0_ffn_br', 'L0_ffn_W1', 'L0_ffn_b1', 'L0_ffn_W2', 'L0_ffn_b2', 
        'L1_ffn_Wr', 'L1_ffn_br', 'L1_ffn_W1', 'L1_ffn_W2', 'L1_ffn_b2', 'L1_ffn_gamma', 'L1_ffn_beta']


def kernel(**inputs):
    import numpy as _np
    import concourse.bacc as _bacc
    from concourse import mybir as _mybir
    from concourse.bass_utils import run_bass_kernel_spmd as _run

    nc = _bacc.Bacc("TRN2", target_bir_lowering=False, num_devices=1)
    laid = {name: _np.ascontiguousarray(inputs[name]) for name in _INS}
    tall = lambda v, rows: _np.ascontiguousarray(_np.transpose(_np.reshape(v, (rows, -1, 128)), (0, 2, 1)))
    laid["L0_ffn_ln_gT"] = _np.ascontiguousarray(_np.transpose(inputs["L0_ffn_ln_g"]))
    laid["L0_ffn_ln_bT"] = _np.ascontiguousarray(_np.transpose(inputs["L0_ffn_ln_b"]))
    laid["L1_gnn_b_ihT"] = tall(inputs["L1_gnn_b_ih"], 1)[0]
    laid["L1_gnn_b_hhT"] = tall(inputs["L1_gnn_b_hh"], 1)[0]
    laid["L1_ffn_b1T"] = _np.reshape(tall(inputs["L1_ffn_b1"], X0), (X0 * 128, F1 // 128))
    laid["L1_gnn_weightT"] = _np.ascontiguousarray(_np.transpose(inputs["L1_gnn_weight"], (0, 2, 1)))
    laid["L1_gnn_w_ihT"] = _np.ascontiguousarray(_np.transpose(inputs["L1_gnn_w_ih"]))
    laid["L1_gnn_w_hhT"] = _np.ascontiguousarray(_np.transpose(inputs["L1_gnn_w_hh"]))
    aps = {name: nc.dram_tensor(f"in_{name}", v.shape, _mybir.dt.from_np(v.dtype), kind="ExternalInput").ap() for name, v in laid.items()}
    out = nc.dram_tensor("out_0", (N, D), _mybir.dt.from_np(_np.dtype("float32")), kind="ExternalOutput").ap()
    build(nc, aps, out)
    return _run(nc, [{f"in_{name}": v for name, v in laid.items()}], core_ids=[0]).results[0]["out_0"]
```

```python
import math

import concourse.bass as bass
from concourse import mybir
from contextlib import ExitStack, contextmanager

FP32 = mybir.dt.float32
FP32R = mybir.dt.float32r
BF16 = mybir.dt.bfloat16
I32 = mybir.dt.int32
U32 = mybir.dt.uint32
ALU = mybir.AluOpType
ACT = mybir.ActivationFunctionType
AX = mybir.AxisListType.X

N = 3125
D = 256
KD = D // 128
E = 50000
NT = -(-N // 128)
NP = NT * 128
EP = 125
ET = E // EP
G = 4
KB = 4
CW = 512
CT = CW // 128
NC = NP // CW
TW = NP - NC * CW
CH = NC + 1
RB = 5
HS = 8
RR = NT // RB
X0, H0 = 8, 1024
ST = 2 * NT + X0 - 1
F1 = 512
LAYERS = 5
EPS = 1e-5
FLT_MAX = 3.4028234663852886e38
CAPACITY = float(math.ceil(N * 1.25 / X0))


class Count:

    def __init__(self, eng, sem):
        self.eng, self.sem, self.base, self.k = eng, sem, 0, 0

    def go(self, ins):
        self.k += 1
        ins.then_inc(self.sem, 1)

    def link(self, ins):
        self.go(ins)
        self.eng.wait_ge(self.sem, self.base + self.k)

    @contextmanager
    def loop(self, start, end, steps):
        base, k = self.base, self.k
        with self.eng.Fori(start, end) as i:
            self.base, self.k = base + i * steps + k - start * steps, 0
            yield i
            assert self.k == steps, (self.k, steps)
        self.base, self.k = base, k + steps * (end - start)


def build(nc, a, out):
    adj = nc.dram_tensor("adj", [NP * NP + NP, 2], FP32).ap()
    adj_sd = adj[0:NP * NP, :].rearrange("(s d) k -> s d k", d=NP)
    adj_w = nc.dram_tensor("adj_w", [NP, NP], FP32).ap()
    slots_x = nc.dram_tensor("slots_x", [ST * 128, D], FP32).ap()
    slots_y = nc.dram_tensor("slots_y", [ST * 128, D], FP32).ap()
    gru_v = nc.dram_tensor("gru_v", [LAYERS * D, 3 * D], FP32).ap()
    res_d = nc.dram_tensor("res_d", [128, NT * D], FP32).ap()
    key_rows = nc.dram_tensor("key_rows", [ET, EP], FP32).ap()

    ctx = ExitStack()
    with ctx:
        scope = [ctx]

        def sb(n, s, d=FP32):
            return scope[-1].enter_context(nc.sbuf_tensor(n, s, d))

        def sem(n):
            return ctx.enter_context(nc.semaphore(n))

        bank = [ctx.enter_context(nc.psum_tensor(f"bank{n}", [128, 512], FP32)) for n in range(8)]
        agg_ps, gate_ps, tr_ps = bank[0:2], bank[2:6], bank[6:8]

        ident = sb("ident", [128, 128])
        row = sb("row", [128, 128])
        below = sb("below", [128, 128])
        ones = sb("ones", [128, 128])
        dis = sb("dis", [128, NT])
        stats = sb("stats", [128, NT, 6])
        st_sum = sb("st_sum", [128, NT]); st_dif = sb("st_dif", [128, NT]); st_m2 = sb("st_m2", [128, NT]); st_sq = sb("st_sq", [128, NT])
        mean = sb("mean", [128, NT]); var = sb("var", [128, NT]); std = sb("std", [128, NT]); rstd = sb("rstd", [128, NT])
        xT = sb("xT", [128, KD, NP])
        scope.append(ExitStack())
        res = sb("res", [128, NT, D])
        nat = sb("nat", [128, NT, D])
        nat2 = sb("nat2", [128, NT, D])
        scope.append(ExitStack())
        zeros = sb("zeros", [128, 2 * NP])
        srci = sb("srci", [EP, ET], I32); dsti = sb("dsti", [EP, ET], I32); w = sb("w", [EP, ET])
        wabs = sb("wabs", [EP, ET]); wbits = sb("wbits", [EP, ET]); finite = sb("finite", [EP, ET], U32)
        srcf = sb("srcf", [EP, ET]); dstf = sb("dstf", [EP, ET]); key = sb("key", [EP, ET])
        lo_i = sb("lo_i", [EP, ET], I32); hi_i = sb("hi_i", [EP, ET], I32)
        dlo = sb("dlo", [EP, ET]); dhi = sb("dhi", [EP, ET])
        spare_i = sb("spare_i", [EP, ET], I32); to_spare = sb("to_spare", [EP, ET]); rest = sb("rest", [EP, ET])
        parts0 = sb("parts0", [EP, ET, 8], BF16); parts1 = sb("parts1", [EP, ET, 8], BF16)
        before = sb("before", [EP, EP])
        keyT = sb("keyT", [100, 4, EP])
        keyrow = sb("keyrow", [EP, KB, G * EP])
        eq = sb("eq", [EP, 2, G, G * EP], BF16)
        hit_lo = sb("hit_lo", [EP, 2, G, 128]); hit_hi = sb("hit_hi", [EP, 2, G, NT])
        own = sb("own", [EP, 2, G, EP], BF16); own_n = sb("own_n", [EP, 2, G])
        sums = sb("sums", [EP, 2, G, 8]); half = sb("half", [EP, 2, G, 2]); pair = sb("pair", [EP, 2, G, 2])
        earlier = sb("earlier", [EP, 2, G]); shift = sb("shift", [EP, 2, G]); slot = sb("slot", [EP, 2, G], U32)
        spare = xT[:, :, :].rearrange("p k n -> p (k n)")
        wt_sb = spare[:, 0:LAYERS * KD * D].rearrange("p (i k f) -> p i k f", i=LAYERS, k=KD)
        wih = spare[:, LAYERS * KD * D:(LAYERS + 3) * KD * D].rearrange("p (k g) -> p k g", k=KD)
        v_st = nat2[:, :, :].rearrange("p t f -> p (t f)")[:, 0:12 * D].rearrange("p (b k g) -> p b k g", b=2, k=KD)
        scope.pop().close()
        scope.append(ExitStack())
        ring2 = sb("ring2", [128, RB, CW, 2])
        stage = sb("stage", [128, 2, RB, CW])
        aggT = sb("aggT", [128, KD, CW])
        gw = sb("gw", [128, 2, KD, D])
        grow = sb("grow", [128, 2, 3, D])
        conv = sb("conv", [128, CT, D]); conv_d = sb("conv_d", [128, CT, D]); fin_mask = sb("fin_mask", [128, CT, D], U32)
        safe = sb("safe", [128, CT, D]); normed = sb("normed", [128, CT, D])
        scope.pop().close()
        scope.append(ExitStack())
        w1 = sb("w1", [128, 2, KD, H0]); w2 = sb("w2", [128, 2, H0 // 128, D])
        erow = sb("erow", [128, 2, H0 + D])
        xtile = sb("xtile", [128, D]); xe = sb("xe", [128, KD, 128])
        hb = sb("hb", [128, H0]); hg = sb("hg", [128, H0]); hT = sb("hT", [128, H0 // 128, 128]); ytile = sb("ytile", [128, D])
        yg = sb("yg", [128, 4, 2, D]); acc = sb("acc", [128, 2, D])
        ewr = sb("ewr", [128, KD, X0]); ebr = sb("ebr", [128, X0])
        eg = sb("eg", [128, KD, X0]); eb = sb("eb", [128, KD, X0])
        lg = sb("lg", [128, NT, X0]); pr = sb("pr", [128, NT, X0]); t8 = sb("t8", [128, NT, X0]); u8 = sb("u8", [128, NT, X0])
        oh1 = sb("oh1", [128, NT, X0]); oh2 = sb("oh2", [128, NT, X0]); both = sb("both", [128, NT, X0])
        pre = [sb(f"pre{n}", [128, NT, X0]) for n in range(2)]; rank = sb("rank", [128, NT, X0]); tot = sb("tot", [128, NT, X0])
        nf = sb("nf", [128, X0]); ni = sb("ni", [128, X0], I32); ns = sb("ns", [128, X0]); first = [sb(f"first{n}", [128, X0 + 1]) for n in range(2)]
        first_i = sb("first_i", [1, X0 + 1], I32); of_t = sb("of_t", [1, ST, X0]); of_f = sb("of_f", [1, ST])
        of_i = sb("of_i", [1, ST], I32); par_i = sb("par_i", [1, ST], I32)
        slot_f = sb("slot_f", [128, 2, NT]); slot_u = sb("slot_u", [128, 2, NT], U32)
        wt = sb("wt", [128, NT]); m1 = sb("m1", [128, NT]); m2 = sb("m2", [128, NT]); ix = sb("ix", [128, NT]); q1 = sb("q1", [128, NT]); q2 = sb("q2", [128, NT])
        scope.pop().close()
        scope.pop().close()
        scope.append(ExitStack())
        ring_lo = sb("ring_lo", [128, NT, CW], FP32R)
        ring_hi = sb("ring_hi", [128, HS, CW], FP32R)
        h_hi = sb("h_hi", [128, NT, D], FP32R); h_lo = sb("h_lo", [128, NT, D], FP32R)
        gT = sb("gT", [128, KD, CW])
        gT_hi = sb("gT_hi", [128, KD, CW], FP32R); gT_lo = sb("gT_lo", [128, KD, CW], FP32R)
        gh_hi = sb("gh_hi", [128, KD, CW], FP32R); gh_lo = sb("gh_lo", [128, KD, CW], FP32R)
        v_hi = sb("v_hi", [128, KD, 3 * D], FP32R); v_lo = sb("v_lo", [128, KD, 3 * D], FP32R)
        whh_hi = sb("whh_hi", [128, KD, 3 * D], FP32R); whh_lo = sb("whh_lo", [128, KD, 3 * D], FP32R)
        bih = sb("bih", [128, 6]); bhh = sb("bhh", [128, 6]); brz = sb("brz", [128, 4])
        gates_sb = sb("gates_sb", [128, 3, KD, CW])
        gr, gz, gn = (gates_sb[:, n, :, :] for n in range(3))
        whh = gates_sb[:, :, :, :].rearrange("p n k c -> p (n k c)")[:, 0:KD * 3 * D].rearrange("p (k g) -> p k g", k=KD)
        scope.pop().close()
        scope.append(ExitStack())
        res_b = sb("res_b", [128, NT, D]); nat_b = sb("nat_b", [128, NT, D])
        fw1 = sb("fw1", [128, 2, KD, F1]); fw2 = sb("fw2", [128, 2, F1 // 128, D]); fw2s = sb("fw2s", [128, 2, F1 // 128, D])
        fb1 = sb("fb1", [128, 2, F1 // 128]); fb2 = sb("fb2", [128, 2, D]); fmix = sb("fmix", [128, D])
        fwr = sb("fwr", [128, KD, X0]); fbr = sb("fbr", [1, X0]); fgb = sb("fgb", [128, 2, D])
        fhid = sb("fhid", [128, 2, F1 // 128, CW])
        fmean = sb("fmean", [128, KD]); r8 = [sb(f"r8_{n}", [1, X0]) for n in range(8)]; r1 = [sb(f"r1_{n}", [1, 1]) for n in range(6)]
        top = sb("top", [1, 8]); topi = sb("topi", [1, 8], U32); tw = sb("tw", [1, 2]); te = sb("te", [1, 2]); twb = sb("twb", [128, 2])
        fo = sb("fo", [128, CT, D]); fn = sb("fn", [128, CT, D])
        scope.pop().close()

        consts = sem("consts"); edges_in = sem("edges_in"); x_in = sem("x_in")
        zeroed = sem("zeroed"); diag_in = sem("diag_in"); dve_n = sem("dve_n")
        key_done = sem("key_done"); keyT_ps = sem("keyT_ps"); keyT_sb = sem("keyT_sb"); keyT_out = sem("keyT_out")
        keyrow_in = [sem(f"keyrow_in{b}") for b in range(KB)]
        compared = sem("compared"); summed = sem("summed"); sums_out = sem("sums_out"); placed = sem("placed")
        turn = sem("turn"); scattered = sem("scattered"); deg_done = sem("deg_done")
        var_ready = sem("var_ready"); std_ready = sem("std_ready")
        gcn_in = sem("gcn_in")
        hs_ready = sem("hs_ready"); chunk_done = [sem(f"chunk_done{l}") for l in range(2)]
        ring_in = [[sem(f"ring_in{l}_{b}") for b in range(RB)] for l in range(2)]
        used = [sem(f"used{l}") for l in range(2)]
        planes = sem("planes"); staged = [sem(f"staged{b}") for b in range(2)]
        aggT_rdy = [sem(f"aggT_rdy{l}") for l in range(2)]
        projd = [sem(f"projd{l}") for l in range(2)]; conv_taken = [sem(f"conv_taken{l}") for l in range(2)]
        cvar = [sem(f"cvar{l}") for l in range(2)]; cstd = [sem(f"cstd{l}") for l in range(2)]
        nat_ready = sem("nat_ready"); tr_done = sem("tr_done"); tr_out = sem("tr_out"); logits_done = sem("logits_done")
        moe_in = sem("moe_in"); lmax = sem("lmax"); lexp = sem("lexp"); counted = sem("counted"); ranked = sem("ranked"); xs_zeroed = sem("xs_zeroed"); slots_ready = sem("slots_ready"); x_sorted = sem("x_sorted")
        w_in = [sem(f"w_in{b}") for b in range(2)]; w_ready = sem("w_ready")
        xt_in = sem("xt_in"); x_turned = sem("x_turned"); xe_rdy = sem("xe_rdy"); h_ps = sem("h_ps"); hb_rdy = sem("hb_rdy"); hg_rdy = sem("hg_rdy")
        hT_ps = sem("hT_ps"); hT_act = sem("hT_act"); hT_dve = sem("hT_dve"); y_ps_rdy = sem("y_ps_rdy"); y_rdy = sem("y_rdy"); y_out = sem("y_out")
        y_got = [sem(f"y_got{b}") for b in range(4)]; y_free = sem("y_free"); moe_done = sem("moe_done")
        gru_in = sem("gru_in"); v_ps = sem("v_ps"); v_out = sem("v_out"); v_set = sem("v_set")
        rw_in = [sem(f"rw_in{b}") for b in range(RB)]; rw_used = sem("rw_used")
        hi_rdy = sem("hi_rdy"); lo_rdy = sem("lo_rdy"); back_hi = sem("back_hi"); back_lo = sem("back_lo")
        gT_a = sem("gT_a"); gT_d = sem("gT_d"); gT_h = sem("gT_h"); gT_l = sem("gT_l"); gh_h = sem("gh_h"); gh_l = sem("gh_l"); v_in = sem("v_in"); v_h = sem("v_h"); whh_h = sem("whh_h"); whh_set = sem("whh_set")
        res_kept = sem("res_kept"); res_back = sem("res_back"); v_kept = [sem(f"v_kept{b}") for b in range(2)]; vw_in = sem("vw_in")
        gates = sem("gates"); g_act = sem("g_act"); g_dve = sem("g_dve"); g_tanh = sem("g_tanh"); g_new = sem("g_new"); back_ps = sem("back_ps")
        f_in = sem("f_in"); f_mean = sem("f_mean"); f_meanT = sem("f_meanT"); f_lg = sem("f_lg"); f_e = sem("f_e"); f_a = sem("f_a"); f_top = sem("f_top"); f_twb = sem("f_twb"); fw_in = sem("fw_in"); fw_rdy = sem("fw_rdy")
        fh_ps = sem("fh_ps"); fh_rdy = sem("fh_rdy"); fy = sem("fy"); fy_taken = sem("fy_taken"); fvar = sem("fvar"); fstd = sem("fstd"); o_ready = sem("o_ready"); stored = sem("stored")

        held = sem("held")

        def hold(eng):
            eng.sem_inc(held, 1)

        block = ctx.enter_context(nc.Block())
        def gate_of(j, n):
            return (gate_ps if j == 0 else (tr_ps[0], tr_ps[1], gate_ps[0], gate_ps[1]))[n]

        x_tiles = a["x"][0:(NT - 1) * 128, :].rearrange("(t p) f -> p t f", p=128)
        LAST = N - (NT - 1) * 128

        def bcast(v, rows=128):
            return v.rearrange("(a n) -> a n", a=1).to_broadcast([rows, v.shape[0]])

        @block.sync
        def _(sp):
            e = lambda v: v.rearrange("(p t) -> p t", p=EP)
            sp.dma_start(srci[:, :], e(a["src"])).then_inc(edges_in, 16)
            sp.dma_start(dsti[:, :], e(a["dst"])).then_inc(edges_in, 16)
            sp.dma_start(w[:, :], e(a["edge_weight"])).then_inc(edges_in, 16)
            sp.dma_start(wih[:, :, :], a["L1_gnn_w_ihT"].rearrange("(k p) g -> p k g", p=128)).then_inc(vw_in, 16)
            for i in range(LAYERS):
                sp.dma_start(wt_sb[:, i, :, :], a["L1_gnn_weightT"][i, :, :].rearrange("(k p) f -> p k f", p=128)).then_inc(vw_in, 16)
            sp.wait_ge(consts, 1)
            sp.dma_start(res[:, 0:NT - 1, :], x_tiles).then_inc(x_in, 16)
            sp.dma_start(res[0:LAST, NT - 1, :], a["x"][(NT - 1) * 128:N, :]).then_inc(x_in, 16)
            sp.wait_ge(consts, 2)
            for t in range(NT):
                sp.dma_start(adj[t * 128 * NP:(t + 1) * 128 * NP, :].rearrange("(p c) k -> p (c k)", p=128), zeros[:, :]).then_inc(zeroed, 16)
            sp.dma_start(adj[NP * NP:NP * NP + NP, :].rearrange("(p c) k -> p (c k)", p=128), zeros[:, 0:2 * NT]).then_inc(zeroed, 16)
            for t in range(3):
                sp.dma_start(slots_x[t * (ST // 3) * 128:(t + 1) * (ST // 3) * 128, :].rearrange("(p c) f -> p (c f)", p=128), zeros[:, 0:ST // 3 * D]).then_inc(xs_zeroed, 16)
            sp.wait_ge(zeroed, 16 * (NT + 1))
            sp.wait_ge(consts, 3)
            with nc.allow_non_contiguous_dma(reason="the diagonal"):
                sp.dma_start(bass.AP(tensor=adj.tensor, offset=1, ap=[[2 * (NP + 1) * NT, 128], [2 * (NP + 1), NT], [1, 1]]),
                             ones[:, 0:NT].rearrange("p (a b) -> p a b", b=1)).then_inc(diag_in, 16)
            sp.wait_ge(keyT_sb, 1)
            sp.dma_start(key_rows.rearrange("(c t) p -> t c p", c=4), keyT[:, :, :]).then_inc(keyT_out, 16)
            for i in range(LAYERS):
                sp.wait_ge(v_out, 4 * i + 4)
                sp.dma_start(gru_v[i * D:(i + 1) * D, :].rearrange("(k p) g -> p k g", p=128), v_st[:, i % 2, :, :]).then_inc(v_kept[i % 2], 16)
            sp.wait_ge(keyT_out, 16)
            flat = key_rows.rearrange("t p -> (t p)").rearrange("(a n) -> a n", a=1)
            with sp.Fori(0, ET // G // KB) as i:
                for b in range(KB):
                    sp.wait_ge(compared, KB * i + b + 1)
                    hold(sp)
                    sp.dma_start(keyrow[:, b, :], flat[:, bass.ds((KB * i + b) * G * EP, G * EP)].to_broadcast([EP, G * EP])).then_inc(keyrow_in[b], 16)
            sp.wait_ge(scattered, 16 * ET)
            sp.wait_ge(hs_ready, 1)
            for l in range(2):
                k = l + 1
                sp.dma_start(gw[:, l, :, :], a[f"L0_gnn_W{k}"].rearrange("(k p) f -> p k f", p=128)).then_inc(gcn_in, 16)
                for m, n in enumerate((f"L0_gnn_b{k}", f"L0_gnn_ln_g{k}", f"L0_gnn_ln_b{k}")):
                    sp.dma_start(grow[:, l, m, :], bcast(a[n])).then_inc(gcn_in, 16)

            def load2(l, c, width, r, b):
                n = NT * c + RB * r + b
                sp.wait_ge(used[l], n + 1)
                if l == 0:
                    sp.wait_ge(planes, n + 1)
                hold(sp)
                t = RB * r + b
                sp.dma_start(ring2[:, b, 0:width, :], adj_sd[t * 128:(t + 1) * 128, bass.ds(c * CW, width), :]).then_inc(ring_in[l][b], 16)

            def store_plane(c, width, r):
                sp.wait_ge(planes, NT * c + RB * r + 2 * RB)
                hold(sp)
                sp.dma_start(adj_w[RB * r * 128:RB * (r + 1) * 128, bass.ds(c * CW, width)].rearrange("(b p) d -> p b d", p=128),
                             stage[:, r % 2, :, 0:width]).then_inc(staged[r % 2], 16)

            def loads2(l, c, width):
                for r in range(RR):
                    for b in range(RB):
                        load2(l, c, width, r, b)
                    if l == 0 and r:
                        store_plane(c, width, r - 1)
                if l == 0:
                    store_plane(c, width, RR - 1)

            for b in range(2):
                sp.sem_inc(staged[b], 16)
            for l in range(2):
                with sp.Fori(0, NC) as c:
                    loads2(l, c, CW)
                loads2(l, NC, TW)
            sp.wait_ge(used[0], NT * CH + RB)
            sp.dma_start(nat[:, 0:NT - 1, :], x_tiles).then_inc(x_in, 16)
            sp.dma_start(nat[0:LAST, NT - 1, :], a["x"][(NT - 1) * 128:N, :]).then_inc(x_in, 16)
            sp.wait_ge(chunk_done[1], CH)
            sp.dma_start(ewr[:, :, :], a["L0_ffn_Wr"].rearrange("(k p) e -> p k e", p=128)).then_inc(moe_in, 16)
            sp.dma_start(ebr[:, :], bcast(a["L0_ffn_br"])).then_inc(moe_in, 16)
            sp.dma_start(eg[:, :, 0:X0], a["L0_ffn_ln_gT"].rearrange("(k p) e -> p k e", p=128)).then_inc(moe_in, 16)
            sp.dma_start(eb[:, :, 0:X0], a["L0_ffn_ln_bT"].rearrange("(k p) e -> p k e", p=128)).then_inc(moe_in, 16)
            sp.wait_ge(x_sorted, 16 * 2 * NT)
            sp.wait_ge(xs_zeroed, 48)
            def load_tokens(i):
                hold(sp)
                sp.dma_start(xtile[:, :], slots_x[bass.ds(i * 128, 128), :]).then_inc(xt_in, 16)

            def store_result(i):
                sp.wait_ge(y_rdy, i + 2)
                hold(sp)
                sp.dma_start(slots_y[bass.ds(i * 128, 128), :], ytile[:, :]).then_inc(y_out, 16)

            sp.sem_inc(y_out, 16)
            load_tokens(0)
            sp.wait_ge(x_turned, 1)
            load_tokens(1)
            with sp.Fori(1, ST - 1) as i:
                sp.wait_ge(x_turned, i + 1)
                load_tokens(i + 1)
                store_result(i - 1)
            store_result(ST - 2)
            store_result(ST - 1)
            sp.wait_ge(moe_done, 1)
            sp.dma_start(res_d, res[:, :, :].rearrange("p t f -> p (t f)")).then_inc(res_kept, 16)
            sp.wait_ge(tr_out, 2 * NT)
            sp.wait_ge(res_kept, 16)
            sp.dma_start(whh, a["L1_gnn_w_hhT"].rearrange("(k p) g -> p k g", p=128)).then_inc(gru_in, 16)
            sp.dma_start(bih[:, :], a["L1_gnn_b_ihT"]).then_inc(gru_in, 16)
            sp.dma_start(bhh[:, :], a["L1_gnn_b_hhT"]).then_inc(gru_in, 16)
            for b in range(2):
                sp.wait_ge(staged[b], 16 * ((RR + 1 - b) // 2 * CH + 1))
            for b in range(2):
                sp.wait_ge(v_kept[b], 16 * ((LAYERS + 1 - b) // 2))

            def loadw(i, c, width, r):
                sp.wait_ge(rw_used, NT * (CH * i + c) + RB * r + RB)
                hold(sp)
                sp.dma_start(ring_lo[:, RB * r:RB * (r + 1), 0:width].bitcast(FP32),
                             adj_w[RB * r * 128:RB * (r + 1) * 128, bass.ds(c * CW, width)].rearrange("(b p) d -> p b d", p=128)).then_inc(rw_in[r], 16)

            with sp.Fori(0, LAYERS) as i:
                for r in range(RR):
                    loadw(i, 0, CW, r)
                sp.wait_ge(gates, 2 * CH * i + 1)
                hold(sp)
                sp.dma_start(v_lo[:, :, :].bitcast(FP32), gru_v[bass.ds(i * D, D), :].rearrange("(k p) g -> p k g", p=128)).then_inc(v_in, 16)
                with sp.Fori(1, NC) as c:
                    for r in range(RR):
                        loadw(i, c, CW, r)
                for r in range(RR):
                    loadw(i, NC, TW, r)
            sp.wait_ge(rw_used, NT * CH * LAYERS + NT)
            sp.dma_start(res_b[:, :, :].rearrange("p t f -> p (t f)"), res_d).then_inc(res_back, 16)
            sp.wait_ge(back_lo, NT * (LAYERS + 1) + 2)
            sp.dma_start(fwr[:, :, :], a["L1_ffn_Wr"].rearrange("(k p) e -> p k e", p=128)).then_inc(f_in, 16)
            sp.dma_start(fbr[:, :], bcast(a["L1_ffn_br"], 1)).then_inc(f_in, 16)
            sp.dma_start(fgb[:, 0, :], bcast(a["L1_ffn_gamma"])).then_inc(f_in, 16)
            sp.dma_start(fgb[:, 1, :], bcast(a["L1_ffn_beta"])).then_inc(f_in, 16)
            sp.wait_ge(f_top, 1)
            fw1_all = a["L1_ffn_W1"].rearrange("e d f -> (e d) f")
            fw2_all = a["L1_ffn_W2"].rearrange("e f d -> (e f) d")
            for k in range(2):
                x = sp.value_load(topi[0:1, k:k + 1], min_val=0, max_val=X0 - 1)
                sp.dma_start(fw1[:, k, :, :], fw1_all[bass.ds(x * D, D), :].rearrange("(k p) h -> p k h", p=128)).then_inc(fw_in, 16)
                sp.dma_start(fw2[:, k, :, :], fw2_all[bass.ds(x * F1, F1), :].rearrange("(k p) d -> p k d", p=128)).then_inc(fw_in, 16)
                sp.dma_start(fb2[:, k, :], a["L1_ffn_b2"][bass.ds(x, 1), :].to_broadcast([128, D])).then_inc(fw_in, 16)
                sp.dma_start(fb1[:, k, :], a["L1_ffn_b1T"][bass.ds(x * 128, 128), :]).then_inc(fw_in, 16)
            with sp.Fori(0, NC) as c:
                sp.wait_ge(o_ready, c + 1)
                hold(sp)
                sp.dma_start(out[bass.ds(c * CW, CW), :].rearrange("(t p) f -> p t f", p=128), res_b[:, bass.ds(c * CT, CT), :]).then_inc(stored, 16)
            sp.wait_ge(o_ready, CH)
            sp.dma_start(out[NC * CW:N, :], res_b[0:LAST, NT - 1, :]).then_inc(stored, 16)
            sp.wait_ge(stored, 16 * CH)

        @block.gpsimd
        def _(pool):
            g_ = nc.gpsimd
            g_.memset(res[:, :, :], 0.0).then_inc(consts, 1)
            g_.memset(zeros[:, :], 0.0).then_inc(consts, 1)
            g_.memset(ones[:, :], 1.0).then_inc(consts, 1)
            g_.memset(ident[:, :], 0.0).then_inc(consts, 1)
            g_.memset(before[:, :], 1.0).then_inc(consts, 1)
            g_.memset(below[:, :], 1.0).then_inc(consts, 1)
            g_.iota(row[:, :], [[1, 128]], base=0, channel_multiplier=0, allow_small_or_imprecise_dtypes=True).then_inc(consts, 1)
            g_.iota(spare_i[:, :], [[0, ET // G], [EP, G]], base=NP * NP, channel_multiplier=1).then_inc(consts, 1)
            pool.wait_ge(consts, 8)
            g_.affine_select(out=ident[:, :], in_=ident[:, :], compare_op=ALU.not_equal, fill=1.0, base=0, pattern=[[-1, 128]], channel_multiplier=1).then_inc(consts, 1)
            g_.affine_select(out=before[:, :], in_=before[:, :], compare_op=ALU.is_gt, fill=0.0, base=0, pattern=[[-1, EP]], channel_multiplier=1).then_inc(consts, 1)
            g_.affine_select(out=below[:, :], in_=below[:, :], compare_op=ALU.is_gt, fill=0.0, base=0, pattern=[[1, 128]], channel_multiplier=-1).then_inc(consts, 1)
            pool.wait_ge(diag_in, 16)
            pool.sem_inc(turn, 1)
            with pool.Fori(0, ET // G // KB) as i:
                for b in range(KB):
                    pool.wait_ge(placed, KB * i + b + 3)
                    pool.sem_inc(turn, 1)
                    for g in range(G):
                        g_.indirect_dma_start(out=adj, out_offset=bass.IndirectOffsetOnAxis(slot[:, b % 2, g:g + 1], 0),
                                              in_=pair[:, b % 2, g, :], in_offset=None, compute_op=ALU.add).then_inc(scattered, 16)
                    pool.wait_ge(scattered, 16 * G * (KB * i + b + 1))

            w1_all = a["L0_ffn_W1"].rearrange("e d h -> (e d) h")
            w2_all = a["L0_ffn_W2"].rearrange("e h d -> (e h) d")

            def load_expert(e, b):
                pool.dma_start(w1[:, b, :, :], w1_all[bass.ds(e * D, D), :].rearrange("(k p) h -> p k h", p=128)).then_inc(w_in[b], 16)
                pool.dma_start(w2[:, b, :, :], w2_all[bass.ds(e * H0, H0), :].rearrange("(k p) d -> p k d", p=128)).then_inc(w_in[b], 16)
                pool.dma_start(erow[:, b, 0:H0], a["L0_ffn_b1"][bass.ds(e, 1), :].to_broadcast([128, H0])).then_inc(w_in[b], 16)
                pool.dma_start(erow[:, b, H0:H0 + D], a["L0_ffn_b2"][bass.ds(e, 1), :].to_broadcast([128, D])).then_inc(w_in[b], 16)

            pool.wait_ge(chunk_done[1], CH)
            for e in range(2):
                load_expert(e, e)
            pool.wait_ge(slots_ready, 1)
            pool.wait_ge(xs_zeroed, 48)
            for k in range(2):
                for t in range(NT):
                    g_.indirect_dma_start(out=slots_x, out_offset=bass.IndirectOffsetOnAxis(slot_u[:, k, t:t + 1], 0),
                                          in_=nat2[:, t, :], in_offset=None).then_inc(x_sorted, 16)
            for e in range(2):
                pool.wait_ge(w_in[e], 64)
                pool.sem_inc(w_ready, 1)
            with pool.Fori(1, X0 // 2) as i:
                for b in range(2):
                    done = pool.value_load(first_i[0:1, bass.ds(2 * i + b - 1, 1)], min_val=1, max_val=ST)
                    pool.wait_ge(y_rdy, done + 1)
                    hold(pool)
                    load_expert(2 * i + b, b)
                    pool.wait_ge(w_in[b], 64 * i + 64)
                    pool.sem_inc(w_ready, 1)
            pool.wait_ge(y_out, 16 * (ST + 1))
            for t in range(NT):
                if t >= 4:
                    pool.wait_ge(y_free, t - 3)
                for k in range(2):
                    g_.indirect_dma_start(out=yg[:, t % 4, k, :], out_offset=None, in_=slots_y,
                                          in_offset=bass.IndirectOffsetOnAxis(slot_u[:, k, t:t + 1], 0)).then_inc(y_got[t % 4], 16)

        @block.tensor
        def _(pe):
            mm, tr = nc.tensor.matmul, nc.tensor.transpose
            ps_sum = [bank[b][0:EP, 0:8 * G].rearrange("p (g k) -> p g k", k=8) for b in range(2)]
            ps_deg = bank[2][:, 0:NT]
            ps_key = bank[3][0:100, 0:4 * EP].rearrange("p (c k) -> p c k", c=4)
            pe.sem_inc(summed, 2)
            pe.wait_ge(consts, 11)
            mm(ps_deg, zeros[0:EP, 0:128], zeros[0:EP, 0:NT], start=True, stop=False)
            pe.wait_ge(key_done, 1)
            for c in range(4):
                last = tr(ps_key[:, c, :], key[:, c * 100:(c + 1) * 100], ident[0:EP, 0:EP])
            last.then_inc(keyT_ps, 1)
            pe.wait_ge(vw_in, 16 * (1 + LAYERS))
            n = 0
            for i in range(LAYERS):
                for m in range(KD):
                    for lo, hi in ((0, 512), (512, 768)):
                        if n >= 4:
                            pe.wait_ge(v_out, n - 3)
                        for k in range(KD):
                            last = mm(bank[4 + n % 4][:, 0:hi - lo], wt_sb[:, i, k, m * 128:(m + 1) * 128], wih[:, k, lo:hi], start=(k == 0), stop=(k == KD - 1))
                        last.then_inc(v_ps, 1)
                        n += 1
            with pe.Fori(0, ET // G // KB) as i:
                for b in range(KB):
                    pe.wait_ge(compared, KB * i + b + 1 + KB)
                    pe.wait_ge(sums_out, KB * i + b + 1)
                    for g in range(G):
                        for q in range(G):
                            parts = (parts1 if q < g else parts0)[:, bass.ds(KB * G * i + G * b + q, 1), :].rearrange("p a k -> p (a k)")
                            mm(ps_sum[b % 2][:, g, :], eq[:, b % 2, q, g * EP:(g + 1) * EP], parts, start=(q == 0), stop=(q == G - 1))
                    for g in range(G):
                        last = mm(ps_deg, hit_lo[:, b % 2, g, :], hit_hi[:, b % 2, g, :], start=False, stop=False)
                    last.then_inc(summed, 1)
            mm(ps_deg, zeros[0:EP, 0:128], zeros[0:EP, 0:NT], start=False, stop=True).then_inc(deg_done, 1)

            for l in range(2):
                hs = (nat, nat2)[l]
                pe.sem_inc(used[l], RB)

                def project(c, tiles):
                    pe.wait_ge(aggT_rdy[l], c + 2)
                    pe.wait_ge(conv_taken[l], c + 1)
                    for j in range(tiles):
                        for k in range(KD):
                            last = mm(gate_ps[j][:, 0:D], aggT[:, k, j * 128:(j + 1) * 128], gw[:, l, k, :], start=(k == 0), stop=(k == KD - 1))
                    last.then_inc(projd[l], 1)

                def aggregate(c, width, first=False, mid=None):
                    for t in range(NT):
                        if t == 0:
                            pe.wait_ge(aggT_rdy[l], c + 1)
                        if first and l == 0 and t == 0:
                            pe.wait_ge(hs_ready, 1)
                        if first and l == 1 and t % CT == 0:
                            pe.wait_ge(chunk_done[0], t // CT + 1)
                        pe.wait_ge(ring_in[l][t % RB], (RR * c + t // RB) * 16 + 16)
                        for f in range(KD):
                            last = mm(agg_ps[f][:, 0:width], hs[:, t, f * 128:(f + 1) * 128], ring2[:, t % RB, 0:width, 1], start=(t == 0), stop=(t == NT - 1))
                        last.then_inc(used[l], 1)
                        if mid and t == NT // 3:
                            mid()

                aggregate(0, CW, first=True)
                if l == 0:
                    pe.wait_ge(gcn_in, 16 * 8)
                with pe.Fori(0, NC - 1) as c:
                    aggregate(c + 1, CW, mid=lambda: project(c, CT))
                aggregate(NC, TW, mid=lambda: project(NC - 1, CT))
                project(NC, TW // 128)

            turned = [0]

            def transpose_in(src):
                for t in range(NT):
                    n = turned[0]
                    if n >= 2:
                        pe.wait_ge(tr_out, n - 1)
                    for k in range(KD):
                        last = tr(tr_ps[n % 2][:, k * 128:(k + 1) * 128], src[:, t, k * 128:(k + 1) * 128], ident[:, :])
                    last.then_inc(tr_done, 1)
                    turned[0] += 1

            pe.wait_ge(nat_ready, 1)
            transpose_in(nat)
            pe.wait_ge(tr_out, NT)
            pe.wait_ge(moe_in, 16 * 4)
            for t in range(NT):
                for k in range(KD):
                    last = mm(bank[0][:, t * X0:(t + 1) * X0], xT[:, k, t * 128:(t + 1) * 128], ewr[:, k, :], start=(k == 0), stop=(k == KD - 1))
            last.then_inc(logits_done, 1)
            pe.wait_ge(counted, 1)
            mm(bank[2][:, 0:NT * X0], below[:, :], both[:, :, :].rearrange("p t e -> p (t e)"), start=True, stop=True)
            mm(bank[3][:, 0:NT * X0], ones[:, :], both[:, :, :].rearrange("p t e -> p (t e)"), start=True, stop=True).then_inc(ranked, 1)

            pe.wait_ge(slots_ready, 1)

            def turn_tokens(i):
                pe.wait_ge(xt_in, 16 * i + 16)
                pe.wait_ge(xe_rdy, i + 1)
                for k in range(KD):
                    last = tr(bank[6][:, k * 128:(k + 1) * 128], xtile[:, k * 128:(k + 1) * 128], ident[:, :])
                last.then_inc(x_turned, 1)

            def turn_hidden(i):
                pe.wait_ge(hg_rdy, i + 2)
                pe.wait_ge(hT_act, i + 1)
                pe.wait_ge(hT_dve, i + 1)
                for h in range(H0 // 128):
                    last = tr(bank[2 + h // 4][:, h % 4 * 128:(h % 4 + 1) * 128], hg[:, h * 128:(h + 1) * 128], ident[:, :])
                last.then_inc(hT_ps, 1)

            def first_product(i):
                pe.wait_ge(w_ready, pe.value_load(of_i[0:1, bass.ds(i, 1)], min_val=0, max_val=X0 - 1) + 1)
                hold(pe)
                b = pe.value_load(par_i[0:1, bass.ds(i, 1)], min_val=0, max_val=1)
                pe.wait_ge(xe_rdy, i + 2)
                pe.wait_ge(hb_rdy, i + 1)
                for k in range(KD):
                    for h in range(2):
                        last = mm(bank[h][:, :], xe[:, k, :], w1[:, bass.ds(b, 1), k, h * 512:(h + 1) * 512].rearrange("p a h -> p (a h)"), start=(k == 0), stop=(k == KD - 1))
                last.then_inc(h_ps, 1)

            def second_product(i):
                b = pe.value_load(par_i[0:1, bass.ds(i, 1)], min_val=0, max_val=1)
                pe.wait_ge(hT_act, i + 2)
                pe.wait_ge(hT_dve, i + 2)
                pe.wait_ge(y_rdy, i + 1)
                for h in range(H0 // 128):
                    last = mm(bank[4][:, 0:D], hT[:, h, :], w2[:, bass.ds(b, 1), h, :].rearrange("p a d -> p (a d)"), start=(h == 0), stop=(h == H0 // 128 - 1))
                last.then_inc(y_ps_rdy, 1)

            pe.sem_inc(h_ps, 1)
            turn_tokens(0)
            first_product(0)
            with pe.Fori(1, ST) as i:
                turn_tokens(i)
                turn_hidden(i - 1)
                first_product(i)
                second_product(i - 1)
            turn_hidden(ST - 1)
            second_product(ST - 1)

            pe.wait_ge(nat_ready, 2)
            transpose_in(nat)
            pe.wait_ge(tr_out, 2 * NT)
            pe.wait_ge(whh_set, 1)
            pe.sem_inc(rw_used, NT)

            def product(ps, lhs, rhs, start, stop):
                for n, (x, y) in enumerate(((0, 0), (0, 1), (1, 0))):
                    last = mm(ps, lhs[x], rhs[y], start=start and n == 0, stop=stop and n == 2)
                return last

            def turn_back(i, t):
                pe.wait_ge(back_lo, NT * i + t + (2 if t == 0 else 1))
                for k in range(KD):
                    last = tr(tr_ps[t % 2][:, k * 128:(k + 1) * 128], xT[:, k, t * 128:(t + 1) * 128], ident[:, :])
                last.then_inc(back_ps, 1)

            def aggregate_w(i, c, width, back=False, mid=None):
                q = CH * i + c
                for t in range(NT):
                    if t == 0:
                        pe.wait_ge(gT_a, q + 1)
                        pe.wait_ge(gT_d, q + 1)
                    if back and t + 2 < NT:
                        turn_back(i, t + 2)
                    if back:
                        pe.wait_ge(back_lo, NT * i + t + 3)
                    pe.wait_ge(lo_rdy, NT * q + t + 1)
                    for f in range(KD):
                        cols = slice(f * 128, (f + 1) * 128)
                        last = product(agg_ps[f][:, 0:width], (h_hi[:, t, cols], h_lo[:, t, cols]),
                                       (ring_hi[:, t % HS, 0:width], ring_lo[:, t, 0:width]), t == 0, t == NT - 1)
                    last.then_inc(rw_used, 1)
                    if mid and t == NT // 3:
                        mid()

            def gate_products(i, c, width):
                q = CH * i + c
                pe.wait_ge(gT_l, q + 2)
                pe.wait_ge(gh_l, q + 1)
                for j in range(KD):
                    if j == 0:
                        pe.wait_ge(g_act, 2 * q + 1)
                        pe.wait_ge(g_dve, 2 * q + 1)
                    for n, (blk, parts) in enumerate(((j, "ih"), (KD + j, "ih"), (2 * KD + j, "i"), (2 * KD + j, "h"))):
                        if j and n == 2:
                            pe.wait_ge(g_act, 2 * q + 2)
                        cols = slice(blk * 128, (blk + 1) * 128)
                        ops = [((v_hi[:, k, cols], v_lo[:, k, cols]), (gT_hi[:, k, 0:width], gT_lo[:, k, 0:width])) for k in range(KD)] * ("i" in parts)
                        ops += [((whh_hi[:, k, cols], whh_lo[:, k, cols]), (gh_hi[:, k, 0:width], gh_lo[:, k, 0:width])) for k in range(KD)] * ("h" in parts)
                        for m, (lhs, rhs) in enumerate(ops):
                            last = product(gate_of(j, n)[:, 0:width], lhs, rhs, m == 0, m == len(ops) - 1)
                    last.then_inc(gates, 1)

            with pe.Fori(0, LAYERS) as i:
                pe.wait_ge(g_new, CH * i + 1)
                turn_back(i, 0)
                turn_back(i, 1)
                aggregate_w(i, 0, CW, back=True)
                pe.wait_ge(v_set, i + 1)
                hold(pe)
                with pe.Fori(0, NC - 1) as c:
                    aggregate_w(i, c + 1, CW, mid=lambda: gate_products(i, c, CW))
                aggregate_w(i, NC, TW, mid=lambda: gate_products(i, NC - 1, CW))
                gate_products(i, NC, TW)
            pe.wait_ge(g_new, CH * LAYERS + 1)
            for t in range(NT):
                turn_back(LAYERS, t)

            pe.wait_ge(nat_ready, 3)
            pe.wait_ge(back_lo, NT * (LAYERS + 1) + 2)
            for k in range(KD):
                for t in range(NT):
                    rows = 128 if t < NT - 1 else LAST
                    last = mm(bank[0][:, k:k + 1], nat_b[0:rows, t, k * 128:(k + 1) * 128], ones[0:rows, 0:1], start=(t == 0), stop=(t == NT - 1))
            last.then_inc(f_mean, 1)
            pe.wait_ge(f_meanT, 1)
            pe.wait_ge(f_in, 64)
            for k in range(KD):
                last = mm(bank[1][0:1, 0:X0], fmean[:, k:k + 1], fwr[:, k, :], start=(k == 0), stop=(k == KD - 1))
            last.then_inc(f_lg, 1)
            pe.wait_ge(f_top, 1)
            mm(bank[1][:, 16:18], ones[0:1, 0:128], tw[0:1, 0:2], start=True, stop=True).then_inc(f_twb, 1)
            transpose_in(nat_b)
            pe.wait_ge(tr_out, 3 * NT)
            pe.wait_ge(fw_rdy, 1)

            HB = F1 // 128
            y_ps = [bank[0], bank[1], bank[6], bank[7]]

            def second(c, width):
                at = bass.ds(c * CW, width)
                for x in range(2):
                    for h in range(HB):
                        m = x * HB + h
                        pe.wait_ge(fh_rdy, 2 * HB * c + m + 1)
                        for k in range(KD):
                            last = mm(gate_ps[m % 4][:, 0:width], fw1[:, x, k, h * 128:(h + 1) * 128], xT[:, k, at], start=(k == 0), stop=(k == KD - 1))
                        last.then_inc(fh_ps, 1)
                pe.wait_ge(fy_taken, c + 1)
                for m in range(2 * HB):
                    pe.wait_ge(fh_rdy, 2 * HB * c + m + 5)
                    for j in range(width // 128):
                        last = mm(y_ps[j][:, 0:D], fhid[:, m // HB, m % HB, j * 128:(j + 1) * 128], fw2s[:, m // HB, m % HB, :], start=(m == 0), stop=(m == 2 * HB - 1))
                last.then_inc(fy, 1)

            with pe.Fori(0, NC) as c:
                second(c, CW)
            second(NC, TW)

        @block.scalar
        def _(act):
            A = nc.scalar.activation
            roots = [0]

            def root(view, src):
                act.wait_ge(var_ready, roots[0] + 1)
                roots[0] += 1
                A(view, src, ACT.Sqrt).then_inc(std_ready, 1)

            root(std[:, :], var[:, :])
            act.sem_inc(sums_out, 2)
            act.wait_ge(keyT_ps, 1)
            A(keyT[:, :, :], bank[3][0:100, 0:4 * EP].rearrange("p (c k) -> p c k", c=4), ACT.Copy).then_inc(keyT_sb, 1)
            n = 0
            for i in range(LAYERS):
                if i >= 2:
                    act.wait_ge(v_kept[i % 2], 16 * (i // 2))
                for m in range(KD):
                    for lo, hi in ((0, 512), (512, 768)):
                        act.wait_ge(v_ps, n + 1)
                        A(v_st[:, i % 2, m, lo:hi], bank[4 + n % 4][:, 0:hi - lo], ACT.Copy).then_inc(v_out, 1)
                        n += 1
            with act.Fori(0, ET // G // KB) as i:
                for b in range(KB):
                    act.wait_ge(summed, KB * i + b + 3)
                    act.wait_ge(placed, KB * i + b + 1)
                    A(sums[:, b % 2, :, :], bank[b % 2][0:EP, 0:8 * G].rearrange("p (g k) -> p g k", k=8), ACT.Copy).then_inc(sums_out, 1)
            root(std[:, :], var[:, :])

            act.sem_inc(planes, RB)
            for l in range(2):
                act.sem_inc(aggT_rdy[l], 1)

                def chunk(c, width):
                    if l == 0:
                        for t in range(NT):
                            r = t // RB
                            if t % RB == 0:
                                act.wait_ge(staged[r % 2], 16 * ((RR + 1 - r % 2) // 2 * c + r // 2) + 16)
                            act.wait_ge(ring_in[0][t % RB], (RR * c + t // RB) * 16 + 16)
                            A(stage[:, r % 2, t % RB, 0:width], ring2[:, t % RB, 0:width, 0], ACT.Copy).then_inc(planes, 1)
                    act.wait_ge(used[l], NT * c + NT + RB)
                    act.wait_ge(projd[l], c + 1)
                    for f in range(KD):
                        last = A(aggT[:, f, 0:width], agg_ps[f][:, 0:width], ACT.Copy)
                    last.then_inc(aggT_rdy[l], 1)

                def chunk_root(c, tiles):
                    act.wait_ge(cvar[l], c + 1)
                    A(std[:, 0:tiles], var[:, 0:tiles], ACT.Sqrt).then_inc(cstd[l], 1)

                act.sem_inc(projd[l], 1)
                chunk(0, CW)
                with act.Fori(0, NC - 1) as c:
                    chunk(c + 1, CW)
                    chunk_root(c, CT)
                chunk(NC, TW)
                chunk_root(NC - 1, CT)
                chunk_root(NC, TW // 128)

            evicted = [0]

            def evict_turned():
                for t in range(NT):
                    n = evicted[0]
                    act.wait_ge(tr_done, n + 1)
                    A(xT[:, :, t * 128:(t + 1) * 128], tr_ps[n % 2][:, 0:D].rearrange("p (k n) -> p k n", k=KD), ACT.Copy).then_inc(tr_out, 1)
                    evicted[0] += 1

            root(std[:, :], var[:, :])
            root(std[:, :], var[:, :])
            evict_turned()
            act.wait_ge(lmax, 1)
            A(pr[:, :, :], t8[:, :, :], ACT.Exp).then_inc(lexp, 1)
            act.sem_inc(hT_act, 1)

            def turned_hidden(i):
                act.wait_ge(hT_ps, i + 1)
                act.wait_ge(y_ps_rdy, i + 1)
                A(hT[:, 0:4, :].rearrange("p h n -> p (h n)"), bank[2][:, :], ACT.Copy).then_inc(hT_act, 1)

            def gelu(i):
                act.wait_ge(hb_rdy, i + 2)
                act.wait_ge(hT_ps, i)
                A(hg[:, :], hb[:, :], ACT.Gelu).then_inc(hg_rdy, 1)

            act.sem_inc(y_ps_rdy, 1)
            act.sem_inc(hg_rdy, 1)
            act.wait_ge(hb_rdy, 2)
            A(hg[:, :], hb[:, :], ACT.Gelu).then_inc(hg_rdy, 1)
            with act.Fori(1, ST) as i:
                turned_hidden(i - 1)
                gelu(i)
            turned_hidden(ST - 1)

            root(std[:, :], var[:, :])
            evict_turned()
            act.wait_ge(gru_in, 48)
            A(whh_hi[:, :, :], whh, ACT.Copy).then_inc(whh_h, 1)
            act.sem_inc(g_act, 1)
            act.sem_inc(gates, 1)
            act.sem_inc(gT_a, 1)

            def high(i, c, t, width):
                m = NT * (CH * i + c) + t
                if t % RB == 0:
                    act.wait_ge(rw_in[t // RB], (CH * i + c) * 16 + 16)
                if t >= HS:
                    act.wait_ge(rw_used, m + NT - HS + 1)
                else:
                    act.wait_ge(rw_used, NT * (CH * i + c) + (NT - 1 - t) // HS * HS + t + 1)
                A(ring_hi[:, t % HS, 0:width], ring_lo[:, t, 0:width].bitcast(FP32), ACT.Copy).then_inc(hi_rdy, 1)

            def back(i, t):
                act.wait_ge(back_ps, NT * i + t + 1)
                A(h_hi[:, t, :], tr_ps[t % 2][:, 0:D], ACT.Copy).then_inc(back_hi, 1)

            def gru_evict(i, c, width):
                q = CH * i + c
                act.wait_ge(rw_used, NT * (q + 2))
                act.wait_ge(gT_l, q + 1)
                A(gT[:, 0, 0:width], agg_ps[0][:, 0:width], ACT.Copy).then_inc(gT_a, 1)
                act.wait_ge(gates, 2 * q + 1)
                act.wait_ge(gT_a, q + 2)
                act.wait_ge(gT_d, q + 2)
                A(gT_hi[:, :, 0:width], gT[:, :, 0:width], ACT.Copy).then_inc(gT_h, 1)
                A(gh_hi[:, :, 0:width], xT[:, :, bass.ds(c * CW, width)], ACT.Copy).then_inc(gh_h, 1)

            def gru_act(i, c, width):
                q = CH * i + c
                act.wait_ge(g_new, q + 1)
                for j in range(KD):
                    act.wait_ge(gates, 2 * q + j + 2)
                    A(gr[:, j, 0:width], gate_of(j, 0)[:, 0:width], ACT.Sigmoid, bias=brz[:, j:j + 1])
                    A(gz[:, j, 0:width], gate_of(j, 1)[:, 0:width], ACT.Sigmoid, bias=brz[:, KD + j:KD + j + 1]).then_inc(g_act, 1)
                for j in range(KD):
                    act.wait_ge(g_dve, 2 * q + j + 2)
                    A(gn[:, j, 0:width], gr[:, j, 0:width], ACT.Tanh, bias=bih[:, 2 * KD + j:2 * KD + j + 1]).then_inc(g_tanh, 1)

            MID = NT // 3 + 1 + HS
            with act.Fori(0, LAYERS) as i:
                for t in range(3):
                    high(i, 0, t, CW)
                back(i, 0)
                back(i, 1)
                for t in range(NT):
                    if t + 2 < NT:
                        back(i, t + 2)
                    if t + 3 < NT:
                        high(i, 0, t + 3, CW)
                act.wait_ge(v_in, 16 * i + 16)
                A(v_hi[:, :, :], v_lo[:, :, :].bitcast(FP32), ACT.Copy).then_inc(v_h, 1)
                gru_evict(i, 0, CW)

                def chunk_w(c, width):
                    for t in range(MID):
                        high(i, c + 1, t, width)
                    gru_act(i, c, CW)
                    for t in range(MID, NT):
                        high(i, c + 1, t, width)
                    gru_evict(i, c + 1, width)

                with act.Fori(0, NC - 1) as c:
                    chunk_w(c, CW)
                chunk_w(NC - 1, TW)
                gru_act(i, NC, TW)

            root(std[:, :], var[:, :])
            act.wait_ge(f_e, 1)
            A(r8[1][:, :], r8[0][:, :], ACT.Exp, accum_out=r1[1][:, :]).then_inc(f_a, 1)
            act.wait_ge(f_e, 2)
            A(r8[6][:, :], r8[5][:, :], ACT.Exp, accum_out=r1[3][:, :]).then_inc(f_a, 1)
            act.wait_ge(f_e, 3)
            A(te[:, :], te[:, :], ACT.Exp, accum_out=r1[4][:, :]).then_inc(f_a, 1)
            evict_turned()

            act.sem_inc(fh_rdy, 4)
            act.sem_inc(fy, 1)
            act.wait_ge(fw_in, 16 * 8)
            HB = F1 // 128

            def second(c, width):
                for m in range(2 * HB):
                    act.wait_ge(fh_ps, 2 * HB * c + m + 1)
                    if m == 0:
                        act.wait_ge(fy, c + 1)
                    A(fhid[:, m // HB, m % HB, 0:width], gate_ps[m % 4][:, 0:width], ACT.Gelu, bias=fb1[:, m // HB, m % HB:m % HB + 1]).then_inc(fh_rdy, 1)

            def second_root(c, tiles):
                act.wait_ge(fvar, c + 1)
                A(std[:, 0:tiles], var[:, 0:tiles], ACT.Sqrt).then_inc(fstd, 1)

            with act.Fori(0, NC) as c:
                second(c, CW)
                second_root(c, CT)
            second(NC, TW)
            second_root(NC, TW // 128)

        @block.vector
        def _(v):
            V = nc.vector
            ch = Count(v, dve_n)
            link, go = ch.link, ch.go

            def moments(tiles):
                s = lambda k: stats[:, 0:tiles, k]
                go(V.tensor_tensor(st_sum[:, 0:tiles], s(1), s(4), ALU.add))
                go(V.tensor_tensor(st_dif[:, 0:tiles], s(1), s(4), ALU.subtract))
                link(V.tensor_tensor(st_m2[:, 0:tiles], s(2), s(5), ALU.add))
                go(V.tensor_scalar(mean[:, 0:tiles], st_sum[:, 0:tiles], 0.5, None, ALU.mult))
                go(V.tensor_tensor(st_sq[:, 0:tiles], st_dif[:, 0:tiles], st_dif[:, 0:tiles], ALU.mult))
                link(V.tensor_scalar(st_m2[:, 0:tiles], st_m2[:, 0:tiles], 1.0 / D, EPS, ALU.mult, ALU.add))
                return V.scalar_tensor_tensor(var[:, 0:tiles], st_sq[:, 0:tiles], 0.25, st_m2[:, 0:tiles], ALU.mult, ALU.add)

            roots = [0]

            def inverse_root():
                v.wait_ge(std_ready, roots[0] + 1)
                roots[0] += 1
                link(V.reciprocal(rstd[:, :], std[:, :]))

            def layernorm(dst, src):
                with ch.loop(0, NT, 1) as t:
                    go(V.bn_stats(stats[:, bass.ds(t, 1), :].rearrange("p a k -> p (a k)"), src[:, bass.ds(t, 1), :].rearrange("p a f -> p (a f)")))
                v.wait_ge(ch.sem, ch.base + ch.k)
                moments(NT).then_inc(var_ready, 1)
                inverse_root()
                with ch.loop(0, NT, 1) as t:
                    go(V.tensor_scalar(dst[:, bass.ds(t, 1), :].rearrange("p a f -> p (a f)"), src[:, bass.ds(t, 1), :].rearrange("p a f -> p (a f)"),
                                       mean[:, bass.ds(t, 1)], rstd[:, bass.ds(t, 1)], ALU.subtract, ALU.mult))
                v.wait_ge(ch.sem, ch.base + ch.k)

            v.sem_inc(placed, 2)
            v.wait_ge(edges_in, 48)
            go(V.tensor_copy(srcf[:, :], srci[:, :]))
            link(V.tensor_copy(dstf[:, :], dsti[:, :]))
            V.scalar_tensor_tensor(key[:, :], srcf[:, :], float(NP), dstf[:, :], ALU.mult, ALU.add).then_inc(key_done, 1)
            go(V.tensor_scalar(lo_i[:, :], dsti[:, :], 127, None, ALU.bitwise_and))
            go(V.tensor_scalar(hi_i[:, :], dsti[:, :], 7, None, ALU.logical_shift_right))
            go(V.tensor_scalar(wbits[:, :].bitcast(I32), w[:, :].bitcast(I32), 0x7fffffff, None, ALU.bitwise_and))
            go(V.memset(wabs[:, :], 1e-6))
            go(V.memset(parts0[:, :, :], 0.0))
            link(V.memset(parts1[:, :, :], 1.0))
            go(V.tensor_copy(dlo[:, :], lo_i[:, :]))
            go(V.tensor_copy(dhi[:, :], hi_i[:, :]))
            go(V.tensor_scalar(finite[:, :], wbits[:, :], FLT_MAX, None, ALU.is_le))
            v.wait_ge(consts, 11)
            link(V.tensor_copy(to_spare[:, :], spare_i[:, :]))
            go(V.tensor_tensor(to_spare[:, :], to_spare[:, :], key[:, :], ALU.subtract))
            link(V.copy_predicated(wabs[:, :], finite[:, :], wbits[:, :]))
            link(V.tensor_scalar(wabs[:, :], wabs[:, :], 1e-6, None, ALU.max))
            for k, x in enumerate((w, wabs)):
                link(V.tensor_copy(parts0[:, :, 3 * k], x[:, :]))
                link(V.tensor_tensor(rest[:, :], x[:, :], parts0[:, :, 3 * k], ALU.subtract))
                link(V.tensor_copy(parts0[:, :, 3 * k + 1], rest[:, :]))
                link(V.tensor_tensor(rest[:, :], rest[:, :], parts0[:, :, 3 * k + 1], ALU.subtract))
                link(V.tensor_copy(parts0[:, :, 3 * k + 2], rest[:, :]))
            link(V.tensor_copy(parts1[:, :, 0:6], parts0[:, :, 0:6]))
            v.sem_inc(compared, KB)
            v.wait_ge(x_in, 32)
            layernorm(res, res)

            def compare(i, b):
                c = b % 2
                v.wait_ge(keyrow_in[b], 16 * i + 16)
                v.wait_ge(summed, KB * i + b + 1)
                at = lambda x, g: x[:, bass.ds(KB * G * i + G * b + g, 1)]
                for g in range(G):
                    V.tensor_scalar(eq[:, c, g, :], keyrow[:, b, :], at(key, g), None, ALU.is_equal)
                for g in range(G):
                    V.scalar_tensor_tensor(own[:, c, g, :], keyrow[:, b, g * EP:(g + 1) * EP], at(key, g), before[:, :], ALU.is_equal, ALU.mult, accum_out=own_n[:, c, g:g + 1])
                for g in range(G):
                    V.tensor_scalar(hit_lo[:, c, g, :], row[0:EP, :], at(dlo, g), None, ALU.is_equal)
                    last = V.tensor_scalar(hit_hi[:, c, g, :], row[0:EP, 0:NT], at(dhi, g), at(wabs, g), ALU.is_equal, ALU.mult)
                last.then_inc(compared, 1)

            def place(i, b):
                c = b % 2
                v.wait_ge(sums_out, KB * i + b + 3)
                v.wait_ge(turn, KB * i + b + 1)
                at = lambda x: x[:, bass.ds(KB * G * i + G * b, G)]
                V.tensor_tensor(half[:, c, :, :], sums[:, c, :, 1:5:3], sums[:, c, :, 2:6:3], ALU.add)
                link(V.tensor_tensor(earlier[:, c, :], sums[:, c, :, 6], own_n[:, c, :], ALU.add))
                V.tensor_tensor(pair[:, c, :, :], sums[:, c, :, 0:4:3], half[:, c, :, :], ALU.add)
                link(V.scalar_tensor_tensor(shift[:, c, :], earlier[:, c, :], 1.0, at(to_spare), ALU.min, ALU.mult))
                V.tensor_tensor(slot[:, c, :], shift[:, c, :], at(key), ALU.add).then_inc(placed, 1)

            with ch.loop(0, ET // G // KB, 2 * KB) as i:
                for b in range(0, KB, 2):
                    compare(i, b)
                    compare(i, b + 1)
                    place(i, b)
                    place(i, b + 1)
            v.wait_ge(deg_done, 1)
            V.tensor_scalar(var[:, :], bank[2][:, 0:NT], 1.0, None, ALU.add).then_inc(var_ready, 1)
            v.wait_ge(std_ready, roots[0] + 1)
            roots[0] += 1
            link(V.reciprocal(dis[:, :], std[:, :]))
            v.wait_ge(scattered, 16 * ET)
            with ch.loop(0, NT, 1) as t:
                go(V.tensor_scalar(nat[:, bass.ds(t, 1), :].rearrange("p a f -> p (a f)"), res[:, bass.ds(t, 1), :].rearrange("p a f -> p (a f)"), dis[:, bass.ds(t, 1)], None, ALU.mult))
            v.wait_ge(ch.sem, ch.base + ch.k)
            v.sem_inc(hs_ready, 1)

            v.wait_ge(gcn_in, 16 * 8)
            for l in range(2):
                v.sem_inc(conv_taken[l], 1)

                def finish(c, tiles):
                    at = lambda x: x[:, bass.ds(c * CT, tiles), :]
                    rows = lambda m: grow[:, l, m:m + 1, :].to_broadcast([128, tiles, D])
                    v.wait_ge(projd[l], c + 2)
                    for j in range(tiles):
                        last = V.scalar_tensor_tensor(conv[:, j, :], gate_ps[j][:, 0:D], dis[:, bass.ds(c * CT + j, 1)], grow[:, l, 0, :], ALU.mult, ALU.add)
                    last.then_inc(conv_taken[l], 1)
                    v.wait_ge(conv_taken[l], c + 2)
                    go(V.memset(safe[:, 0:tiles, :], 0.0))
                    link(V.tensor_tensor(conv_d[:, 0:tiles, :], conv[:, 0:tiles, :], conv[:, 0:tiles, :], ALU.subtract))
                    link(V.tensor_scalar(fin_mask[:, 0:tiles, :], conv_d[:, 0:tiles, :], 0.0, None, ALU.is_equal))
                    hold(v)
                    link(V.copy_predicated(safe[:, 0:tiles, :], fin_mask[:, 0:tiles, :], conv[:, 0:tiles, :]))
                    for j in range(tiles):
                        last = V.bn_stats(stats[:, j, :], safe[:, j, :])
                    link(last)
                    moments(tiles).then_inc(cvar[l], 1)
                    v.wait_ge(cstd[l], c + 1)
                    link(V.reciprocal(rstd[:, 0:tiles], std[:, 0:tiles]))
                    for j in range(tiles):
                        last = V.tensor_scalar(normed[:, j, :], safe[:, j, :], mean[:, j:j + 1], rstd[:, j:j + 1], ALU.subtract, ALU.mult)
                    link(last)
                    link(V.tensor_tensor(normed[:, 0:tiles, :], normed[:, 0:tiles, :], rows(1), ALU.mult))
                    link(V.tensor_tensor(normed[:, 0:tiles, :], normed[:, 0:tiles, :], rows(2), ALU.add))
                    last = V.scalar_tensor_tensor(at(res), normed[:, 0:tiles, :], 0.0, at(res), ALU.max, ALU.add)
                    if l == 0:
                        link(last)
                        for j in range(tiles):
                            last = V.tensor_scalar(nat2[:, bass.ds(c * CT + j, 1), :].rearrange("p a f -> p (a f)"), res[:, bass.ds(c * CT + j, 1), :].rearrange("p a f -> p (a f)"), dis[:, bass.ds(c * CT + j, 1)], None, ALU.mult)
                    last.then_inc(chunk_done[l], 1)

                with ch.loop(0, NC, 16 if l == 0 else 15) as c:
                    finish(c, CT)
                finish(NC, TW // 128)

            v.wait_ge(chunk_done[1], CH)
            v.wait_ge(x_in, 64)
            link(V.tensor_tensor(res[:, :, :], res[:, :, :], nat[:, :, :], ALU.add))
            layernorm(nat, res)
            v.sem_inc(nat_ready, 1)
            layernorm(nat2, nat)

            v.wait_ge(logits_done, 1)
            v.wait_ge(moe_in, 16 * 4)
            wide = lambda x: x[:, :].rearrange("p (t a) -> p t a", a=1).to_broadcast([128, NT, X0])
            pos = row[:, 0:X0].rearrange("p (a e) -> p a e", a=1).to_broadcast([128, NT, X0])
            link(V.tensor_tensor(lg[:, :, :], bank[0][:, 0:NT * X0].rearrange("p (t e) -> p t e", e=X0), ebr[:, :].rearrange("p (a e) -> p a e", a=1).to_broadcast([128, NT, X0]), ALU.add))
            link(V.reduce_max(m1[:, :], lg[:, :, :], AX))
            V.tensor_tensor(t8[:, :, :], lg[:, :, :], wide(m1), ALU.subtract).then_inc(lmax, 1)
            v.wait_ge(lexp, 1)

            def first_of_max(hit, probs, best):
                link(V.reduce_max(best[:, :], probs[:, :, :], AX))
                link(V.tensor_tensor(u8[:, :, :], probs[:, :, :], wide(best), ALU.is_lt))
                link(V.scalar_tensor_tensor(u8[:, :, :], u8[:, :, :], 16.0, pos, ALU.mult, ALU.add))
                link(V.tensor_reduce(ix[:, :], u8[:, :, :], AX, ALU.min))
                link(V.tensor_tensor(hit[:, :, :], u8[:, :, :], wide(ix), ALU.is_equal))

            first_of_max(oh1, pr, m1)
            link(V.scalar_tensor_tensor(t8[:, :, :], oh1[:, :, :], -4.0, pr[:, :, :], ALU.mult, ALU.add))
            first_of_max(oh2, t8, m2)
            V.tensor_tensor(both[:, :, :], oh1[:, :, :], oh2[:, :, :], ALU.add).then_inc(counted, 1)
            link(V.tensor_tensor(q1[:, :], m1[:, :], m2[:, :], ALU.add))
            link(V.reciprocal(q1[:, :], q1[:, :]))
            go(V.tensor_tensor(q2[:, :], m2[:, :], q1[:, :], ALU.mult))
            link(V.tensor_tensor(wt[:, :], m1[:, :], q1[:, :], ALU.mult))
            v.wait_ge(ranked, 1)
            link(V.tensor_copy(tot[:, :, :], bank[3][:, 0:NT * X0].rearrange("p (t e) -> p t e", e=X0)))

            def prefix(bufs, n):
                old, new, s = bufs[0], bufs[1], 1
                while s < n:
                    go(V.tensor_copy(new(0, s), old(0, s)))
                    link(V.tensor_tensor(new(s, n), old(s, n), old(0, n - s), ALU.add))
                    old, new, s = new, old, 2 * s
                return old

            go(V.memset(pre[0][:, 0:1, :], 0.0))
            link(V.tensor_copy(pre[0][:, 1:NT, :], tot[:, 0:NT - 1, :]))
            ahead = prefix([lambda lo, hi, x=x: x[:, lo:hi, :] for x in pre], NT)
            go(V.tensor_tensor(rank[:, :, :], bank[2][:, 0:NT * X0].rearrange("p (t e) -> p t e", e=X0), ahead(0, NT), ALU.add))
            link(V.tensor_tensor(nf[:, :], ahead(NT - 1, NT).rearrange("p a e -> p (a e)"), tot[:, NT - 1, :], ALU.add))
            link(V.tensor_scalar(nf[:, :], nf[:, :], 127.0, None, ALU.add))
            link(V.tensor_copy(ni[:, :], nf[:, :]))
            link(V.tensor_scalar(ni[:, :], ni[:, :], 7, None, ALU.logical_shift_right))
            link(V.tensor_copy(ns[:, :], ni[:, :]))
            go(V.memset(first[0][:, 0:1], 0.0))
            link(V.tensor_scalar(first[0][:, 1:X0 + 1], ns[:, :], 1.0, None, ALU.max))
            start = prefix([lambda lo, hi, x=x: x[:, lo:hi] for x in first], X0 + 1)
            link(V.scalar_tensor_tensor(rank[:, :, :], start(0, X0).rearrange("p (a e) -> p a e", a=1).to_broadcast([128, NT, X0]), 128.0, rank[:, :, :], ALU.mult, ALU.add))
            for k, hit in enumerate((oh1, oh2)):
                link(V.tensor_tensor(u8[:, :, :], rank[:, :, :], hit[:, :, :], ALU.mult))
                link(V.reduce_sum(slot_f[:, k, :], u8[:, :, :], AX))
            link(V.tensor_copy(slot_u[:, :, :], slot_f[:, :, :]))
            go(V.tensor_copy(first_i[:, :], start(0, X0 + 1)[0:1, :]))
            link(V.tensor_tensor(of_t[:, :, :], row[0:1, 0:ST].rearrange("p (t a) -> p t a", a=1).to_broadcast([1, ST, X0]),
                                 start(0, X0)[0:1, :].rearrange("p (a e) -> p a e", a=1).to_broadcast([1, ST, X0]), ALU.is_ge))
            link(V.reduce_sum(of_f[:, :], of_t[:, :, :], AX))
            link(V.tensor_scalar(of_f[:, :], of_f[:, :], 1.0, None, ALU.subtract))
            link(V.tensor_copy(of_i[:, :], of_f[:, :]))
            link(V.tensor_scalar(par_i[:, :], of_i[:, :], 1, None, ALU.bitwise_and))
            v.sem_inc(slots_ready, 1)
            v.sem_inc(xe_rdy, 1)
            v.sem_inc(y_rdy, 1)
            v.sem_inc(hb_rdy, 1)
            v.sem_inc(hT_dve, 1)

            def scale_tokens(i):
                e = v.value_load(of_i[0:1, bass.ds(i, 1)], min_val=0, max_val=X0 - 1)
                v.wait_ge(x_turned, i + 1)
                v.wait_ge(h_ps, i + 1)
                for k in range(KD):
                    last = V.tensor_scalar(xe[:, k, :], bank[6][:, k * 128:(k + 1) * 128], eg[:, k, bass.ds(e, 1)], eb[:, k, bass.ds(e, 1)], ALU.mult, ALU.add)
                last.then_inc(xe_rdy, 1)

            def turned_hidden(i):
                v.wait_ge(hT_ps, i + 1)
                v.wait_ge(y_ps_rdy, i + 1)
                V.tensor_copy(hT[:, 4:8, :].rearrange("p h n -> p (h n)"), bank[3][:, :]).then_inc(hT_dve, 1)

            def add_bias1(i):
                b = v.value_load(par_i[0:1, bass.ds(i, 1)], min_val=0, max_val=1)
                v.wait_ge(h_ps, i + 2)
                v.wait_ge(hg_rdy, i + 1)
                for h in range(2):
                    last = V.tensor_tensor(hb[:, h * 512:(h + 1) * 512], bank[h][:, :], erow[:, bass.ds(b, 1), h * 512:(h + 1) * 512].rearrange("p a h -> p (a h)"), ALU.add)
                last.then_inc(hb_rdy, 1)

            def add_bias2(i):
                b = v.value_load(par_i[0:1, bass.ds(i, 1)], min_val=0, max_val=1)
                v.wait_ge(y_ps_rdy, i + 2)
                v.wait_ge(y_out, 16 * i + 16)
                V.tensor_tensor(ytile[:, :], bank[4][:, 0:D], erow[:, bass.ds(b, 1), H0:H0 + D].rearrange("p a d -> p (a d)"), ALU.add).then_inc(y_rdy, 1)

            scale_tokens(0)
            add_bias1(0)
            with v.Fori(1, ST) as i:
                scale_tokens(i)
                turned_hidden(i - 1)
                add_bias1(i)
                add_bias2(i - 1)
            turned_hidden(ST - 1)
            add_bias2(ST - 1)
            for t in range(NT):
                v.wait_ge(y_got[t % 4], 32 * (t // 4) + 32)
                link(V.scalar_tensor_tensor(acc[:, t % 2, :], yg[:, t % 4, 0, :], wt[:, t:t + 1], res[:, t, :], ALU.mult, ALU.add))
                V.scalar_tensor_tensor(res[:, t, :], yg[:, t % 4, 1, :], q2[:, t:t + 1], acc[:, t % 2, :], ALU.mult, ALU.add).then_inc(y_free, 1)
            v.wait_ge(y_free, NT)
            layernorm(nat, res)
            v.sem_inc(moe_done, 1)
            v.sem_inc(nat_ready, 1)

            v.wait_ge(gru_in, 48)
            v.wait_ge(whh_h, 1)
            V.tensor_tensor(whh_lo[:, :, :], whh, whh_hi[:, :, :].bitcast(FP32), ALU.subtract).then_inc(whh_set, 1)
            V.tensor_tensor(brz[:, :], bih[:, 0:4], bhh[:, 0:4], ALU.add).then_inc(g_dve, 1)
            v.wait_ge(g_dve, 1)
            v.wait_ge(whh_set, 1)
            v.sem_inc(g_new, 1)
            v.sem_inc(back_lo, 2)
            v.sem_inc(gT_d, 1)
            v.sem_inc(gT_l, 1)

            def low(i, c, t, width):
                v.wait_ge(hi_rdy, NT * (CH * i + c) + t + 1)
                V.tensor_tensor(ring_lo[:, t, 0:width], ring_lo[:, t, 0:width].bitcast(FP32), ring_hi[:, t % HS, 0:width].bitcast(FP32), ALU.subtract).then_inc(lo_rdy, 1)

            def back(i, t):
                v.wait_ge(back_hi, NT * i + t + 1)
                V.tensor_tensor(h_lo[:, t, :], tr_ps[t % 2][:, 0:D], h_hi[:, t, :].bitcast(FP32), ALU.subtract).then_inc(back_lo, 1)

            def gru_low(i, c, width):
                q = CH * i + c
                v.wait_ge(rw_used, NT * (q + 2))
                V.tensor_copy(gT[:, 1, 0:width], agg_ps[1][:, 0:width]).then_inc(gT_d, 1)
                v.wait_ge(gT_h, q + 1)
                V.tensor_tensor(gT_lo[:, :, 0:width], gT[:, :, 0:width], gT_hi[:, :, 0:width].bitcast(FP32), ALU.subtract).then_inc(gT_l, 1)
                v.wait_ge(gh_h, q + 1)
                V.tensor_tensor(gh_lo[:, :, 0:width], xT[:, :, bass.ds(c * CW, width)], gh_hi[:, :, 0:width].bitcast(FP32), ALU.subtract).then_inc(gh_l, 1)

            def gru(i, c, width):
                q = CH * i + c
                for j in range(KD):
                    v.wait_ge(g_act, 2 * q + j + 2)
                    link(V.scalar_tensor_tensor(gr[:, j, 0:width], gate_of(j, 3)[:, 0:width], bhh[:, 2 * KD + j:2 * KD + j + 1], gr[:, j, 0:width], ALU.add, ALU.mult))
                    V.tensor_tensor(gr[:, j, 0:width], gate_of(j, 2)[:, 0:width], gr[:, j, 0:width], ALU.add).then_inc(g_dve, 1)
                at = xT[:, :, bass.ds(c * CW, width)]
                v.wait_ge(g_tanh, 2 * q + 2)
                link(V.tensor_tensor(gr[:, :, 0:width], at, gn[:, :, 0:width], ALU.subtract))
                link(V.tensor_tensor(gr[:, :, 0:width], gr[:, :, 0:width], gz[:, :, 0:width], ALU.mult))
                V.tensor_tensor(at, gr[:, :, 0:width], gn[:, :, 0:width], ALU.add).then_inc(g_new, 1)

            MID = NT // 3 + 1 + HS
            with ch.loop(0, LAYERS, 4 * CH) as i:
                for t in range(3):
                    low(i, 0, t, CW)
                back(i, 0)
                back(i, 1)
                for t in range(NT):
                    if t + 2 < NT:
                        back(i, t + 2)
                    if t + 3 < NT:
                        low(i, 0, t + 3, CW)
                v.wait_ge(v_h, i + 1)
                V.tensor_tensor(v_lo[:, :, :], v_lo[:, :, :].bitcast(FP32), v_hi[:, :, :].bitcast(FP32), ALU.subtract).then_inc(v_set, 1)
                gru_low(i, 0, CW)

                def chunk_w(c, width):
                    for t in range(MID):
                        low(i, c + 1, t, width)
                    gru(i, c, CW)
                    for t in range(MID, NT):
                        low(i, c + 1, t, width)
                    gru_low(i, c + 1, width)

                with ch.loop(0, NC - 1, 4) as c:
                    chunk_w(c, CW)
                chunk_w(NC - 1, TW)
                gru(i, NC, TW)
            v.wait_ge(res_back, 16)
            for t in range(NT):
                v.wait_ge(back_ps, NT * LAYERS + t + 1)
                V.tensor_tensor(res_b[:, t, :], res_b[:, t, :], tr_ps[t % 2][:, 0:D], ALU.add).then_inc(back_lo, 1)
            v.wait_ge(back_lo, NT * (LAYERS + 1) + 2)
            layernorm(nat_b, res_b)
            v.sem_inc(nat_ready, 1)

            v.wait_ge(f_mean, 1)
            V.tensor_scalar(fmean[:, :], bank[0][:, 0:KD], 1.0 / N, None, ALU.mult).then_inc(f_meanT, 1)
            v.wait_ge(f_lg, 1)
            v.wait_ge(f_in, 64)
            one = lambda x: x[0:1, 0:1]
            link(V.tensor_tensor(r8[2][:, :], bank[1][0:1, 0:X0], fbr[:, :], ALU.add))
            link(V.reduce_max(r1[0][:, :], r8[2][:, :], AX))
            V.tensor_scalar(r8[0][:, :], r8[2][:, :], one(r1[0]), None, ALU.subtract).then_inc(f_e, 1)
            v.wait_ge(f_a, 1)
            link(V.reciprocal(r1[2][:, :], r1[1][:, :]))
            link(V.tensor_scalar(r8[2][:, :], r8[1][:, :], one(r1[2]), None, ALU.mult))
            link(V.tensor_scalar(r8[3][:, :], r8[2][:, :], float(N), None, ALU.mult))
            link(V.tensor_scalar(r8[4][:, :], r8[3][:, :], CAPACITY, None, ALU.max))
            link(V.reciprocal(r8[4][:, :], r8[4][:, :]))
            link(V.tensor_scalar(r8[4][:, :], r8[4][:, :], CAPACITY, None, ALU.mult))
            link(V.tensor_scalar(r8[7][:, :], r8[3][:, :], CAPACITY, None, ALU.is_gt))
            link(V.tensor_scalar(r8[4][:, :], r8[4][:, :], 1.0, None, ALU.subtract))
            link(V.tensor_tensor(r8[4][:, :], r8[4][:, :], r8[7][:, :], ALU.mult))
            link(V.scalar_tensor_tensor(r8[2][:, :], r8[4][:, :], 1.0, r8[2][:, :], ALU.add, ALU.mult))
            link(V.reduce_max(r1[0][:, :], r8[2][:, :], AX))
            V.tensor_scalar(r8[5][:, :], r8[2][:, :], one(r1[0]), None, ALU.subtract).then_inc(f_e, 1)
            v.wait_ge(f_a, 2)
            link(V.reciprocal(r1[2][:, :], r1[3][:, :]))
            link(V.tensor_scalar(r8[3][:, :], r8[6][:, :], one(r1[2]), None, ALU.mult))
            link(V.max(top[:, :], r8[3][:, :]))
            link(V.max_index(topi[:, :], top[:, :], r8[3][:, :]))
            V.tensor_scalar(te[:, :], top[:, 0:2], one(top), None, ALU.subtract).then_inc(f_e, 1)
            v.wait_ge(f_a, 3)
            link(V.reciprocal(r1[5][:, :], r1[4][:, :]))
            V.tensor_scalar(tw[:, :], te[:, :], one(r1[5]), None, ALU.mult).then_inc(f_top, 1)
            v.wait_ge(f_twb, 1)
            link(V.tensor_copy(twb[:, :], bank[1][:, 16:18]))
            v.wait_ge(fw_in, 16 * 8)
            for k in range(2):
                go(V.tensor_scalar(fw2s[:, k, :, :], fw2[:, k, :, :], twb[:, k:k + 1], None, ALU.mult))
            link(V.tensor_scalar(fmix[:, :], fb2[:, 0, :], twb[:, 0:1], None, ALU.mult))
            link(V.scalar_tensor_tensor(fmix[:, :], fb2[:, 1, :], twb[:, 1:2], fmix[:, :], ALU.mult, ALU.add))
            v.sem_inc(fw_rdy, 1)
            v.sem_inc(fy_taken, 1)

            y_ps = [bank[0], bank[1], bank[6], bank[7]]

            def second(c, tiles):
                at = lambda x: x[:, bass.ds(c * CT, tiles), :]
                v.wait_ge(fy, c + 2)
                for j in range(tiles):
                    last = V.tensor_tensor(fo[:, j, :], y_ps[j][:, 0:D], fmix[:, :], ALU.add)
                last.then_inc(fy_taken, 1)
                v.wait_ge(fy_taken, c + 2)
                link(V.tensor_tensor(fo[:, 0:tiles, :], fo[:, 0:tiles, :], at(nat_b), ALU.add))
                for j in range(tiles):
                    last = V.bn_stats(stats[:, j, :], fo[:, j, :])
                link(last)
                moments(tiles).then_inc(fvar, 1)
                v.wait_ge(fstd, c + 1)
                link(V.reciprocal(rstd[:, 0:tiles], std[:, 0:tiles]))
                for j in range(tiles):
                    last = V.tensor_scalar(fn[:, j, :], fo[:, j, :], mean[:, j:j + 1], rstd[:, j:j + 1], ALU.subtract, ALU.mult)
                link(last)
                rows = lambda m: fgb[:, m:m + 1, :].to_broadcast([128, tiles, D])
                link(V.tensor_tensor(fn[:, 0:tiles, :], fn[:, 0:tiles, :], rows(0), ALU.mult))
                link(V.tensor_tensor(fn[:, 0:tiles, :], fn[:, 0:tiles, :], rows(1), ALU.add))
                V.tensor_tensor(at(res_b), at(res_b), fn[:, 0:tiles, :], ALU.add).then_inc(o_ready, 1)

            with ch.loop(0, NC, 12) as c:
                second(c, CT)
            second(NC, TW // 128)


_INS = ['x', 'src', 'dst', 'edge_weight', 'L0_gnn_W1', 'L0_gnn_b1', 'L0_gnn_ln_g1', 'L0_gnn_ln_b1', 'L0_gnn_W2', 'L0_gnn_b2', 'L0_gnn_ln_g2', 'L0_gnn_ln_b2',
        'L0_ffn_Wr', 'L0_ffn_br', 'L0_ffn_W1', 'L0_ffn_b1', 'L0_ffn_W2', 'L0_ffn_b2', 
        'L1_ffn_Wr', 'L1_ffn_br', 'L1_ffn_W1', 'L1_ffn_W2', 'L1_ffn_b2', 'L1_ffn_gamma', 'L1_ffn_beta']


def kernel(**inputs):
    import numpy as _np
    import concourse.bacc as _bacc
    from concourse import mybir as _mybir
    from concourse.bass_utils import run_bass_kernel_spmd as _run

    nc = _bacc.Bacc("TRN2", target_bir_lowering=False, num_devices=1)
    laid = {name: _np.ascontiguousarray(inputs[name]) for name in _INS}
    tall = lambda v, rows: _np.ascontiguousarray(_np.transpose(_np.reshape(v, (rows, -1, 128)), (0, 2, 1)))
    laid["L0_ffn_ln_gT"] = _np.ascontiguousarray(_np.transpose(inputs["L0_ffn_ln_g"]))
    laid["L0_ffn_ln_bT"] = _np.ascontiguousarray(_np.transpose(inputs["L0_ffn_ln_b"]))
    laid["L1_gnn_b_ihT"] = tall(inputs["L1_gnn_b_ih"], 1)[0]
    laid["L1_gnn_b_hhT"] = tall(inputs["L1_gnn_b_hh"], 1)[0]
    laid["L1_ffn_b1T"] = _np.reshape(tall(inputs["L1_ffn_b1"], X0), (X0 * 128, F1 // 128))
    laid["L1_gnn_weightT"] = _np.ascontiguousarray(_np.transpose(inputs["L1_gnn_weight"], (0, 2, 1)))
    laid["L1_gnn_w_ihT"] = _np.ascontiguousarray(_np.transpose(inputs["L1_gnn_w_ih"]))
    laid["L1_gnn_w_hhT"] = _np.ascontiguousarray(_np.transpose(inputs["L1_gnn_w_hh"]))
    aps = {name: nc.dram_tensor(f"in_{name}", v.shape, _mybir.dt.from_np(v.dtype), kind="ExternalInput").ap() for name, v in laid.items()}
    out = nc.dram_tensor("out_0", (N, D), _mybir.dt.from_np(_np.dtype("float32")), kind="ExternalOutput").ap()
    build(nc, aps, out)
    return _run(nc, [{f"in_{name}": v for name, v in laid.items()}], core_ids=[0]).results[0]["out_0"]
```
